# Optimizing a Trainium2 kernel written in Bass

```python
import numpy as np
import jax
import jax.numpy as jnp

def _softmax(x, axis=-1):
    return jax.nn.softmax(x, axis=axis)

def _gelu(x):
    return jax.nn.gelu(x, approximate=True)

def _silu(x):
    return jax.nn.silu(x)

def _sigmoid(x):
    return jax.nn.sigmoid(x)

def _layernorm(x, axis=-1, eps=1e-05):
    m = jnp.mean(x, axis=axis, keepdims=True)
    v = jnp.var(x, axis=axis, keepdims=True)
    return (x - m) / jnp.sqrt(v + eps)

def _scatter_add(tgt, idx, src, axis=0):
    return tgt.at[idx].add(src)

def _segment_sum(src, seg, n):
    return jax.ops.segment_sum(src, seg, n)
kernel_name = 'mk_cond_resid_d4_seqx_r4_a14864'

def setup_inputs(seed: int=0):
    np.random.seed(seed)
    _w = jnp.asarray

    def _rec_inputs():
        import jax
        import jax.numpy as jnp
        _rk = jax.random.key(seed)
        x = -0.0003929 + 0.9999 * jax.random.normal(jax.random.fold_in(_rk, 1), (64, 64, 1024), jnp.float32)
        _lenS = 64 - jax.random.randint(jax.random.fold_in(_rk, 7), (64,), 0, max(1, 64 // 4) + 1, jnp.int32)
        _lenS2 = 64 - jax.random.randint(jax.random.fold_in(_rk, 8), (64,), 0, max(1, 64 // 4) + 1, jnp.int32)
        itok_B_8_3872 = jax.random.randint(jax.random.fold_in(_rk, 11), (64,), 8, 3873, jnp.int32)
        itok_B_0_7 = jax.random.randint(jax.random.fold_in(_rk, 12), (64,), 0, 8, jnp.int32)
        itok_B_0_2 = jax.random.randint(jax.random.fold_in(_rk, 13), (64,), 0, 3, jnp.int32)
        condB_codebook = -0.0625 + 0.715345 * jax.random.normal(jax.random.fold_in(_rk, 14), (64,), jnp.float32)
        return (x, itok_B_8_3872, itok_B_0_7, itok_B_0_2, condB_codebook)
    x, itok_B_8_3872, itok_B_0_7, itok_B_0_2, condB_codebook = _rec_inputs()

    def _L0_cond_setup():
        import math
        import jax, jax.numpy as jnp
        import numpy as np
        H, N, B, L = (64, 64, 16, 1024)
        DT_MIN, DT_MAX = (0.001, 0.1)

        def _get_kernel(log_dt, C, log_A_real, A_imag, length):
            Cc = C[..., 0] + 1j * C[..., 1]
            dt = jnp.exp(log_dt)
            A = -jnp.exp(log_A_real) + 1j * A_imag
            dtA = A * dt[:, None]
            P = dtA[:, :, None] * jnp.arange(length, dtype=jnp.float32)
            Cs = Cc * (jnp.exp(dtA) - 1.0) / A
            K = 2.0 * jnp.einsum('hn,hnl->hl', Cs, jnp.exp(P)).real
            return K
        key = jax.random.key(seed)
        ks = jax.random.split(key, 6)
        u = jax.random.normal(ks[0], (B, H, L), dtype=jnp.float32)
        length = jax.random.randint(ks[1], (B,), 0, L)
        log_dt = jax.random.uniform(ks[2], (H,), dtype=jnp.float32) * (math.log(DT_MAX) - math.log(DT_MIN)) + math.log(DT_MIN)
        C = jax.random.normal(ks[3], (H, N, 2), dtype=jnp.float32)
        log_A_real = jnp.log(0.5 * jnp.ones((H, N), dtype=jnp.float32))
        A_imag = math.pi * jnp.broadcast_to(jnp.arange(N, dtype=jnp.float32), (H, N))
        D = jax.random.normal(ks[4], (H,), dtype=jnp.float32)
        return {'u': u, 'length': length, 'log_dt': log_dt, 'C': C, 'log_A_real': log_A_real, 'A_imag': A_imag, 'D': D}
    _L0_cond_all = _L0_cond_setup()
    _L0_cond_in = {k: v for k, v in _L0_cond_all.items() if k in ('log_dt', 'C', 'log_A_real', 'A_imag', 'D')}
    del _L0_cond_all

    def _L1_cond_setup():
        import jax, jax.numpy as jnp
        import numpy as np
        TOP_K = 2
        LANG_BIAS = 5.0
        SCALING = 32.0 / 16.0
        LANGUAGE_PAD_ID = -1
        key = jax.random.key(seed)
        ks = jax.random.split(key, 6)
        B, T, D, O, E, R = (4, 512, 1024, 1024, 8, 16)
        x = jax.random.normal(ks[0], (B, T, D), dtype=jnp.float32)
        language_ids = jax.random.randint(ks[1], (B,), 0, E).astype(jnp.int64)
        W = jax.random.normal(ks[2], (O, D), dtype=jnp.float32) * (1.0 / np.sqrt(D))
        Wr = jax.random.normal(ks[3], (E, D), dtype=jnp.float32) * (1.0 / np.sqrt(D))
        A = jax.random.normal(ks[4], (E, R, D), dtype=jnp.float32) * (1.0 / np.sqrt(D))
        Bm = jax.random.normal(ks[5], (O, R), dtype=jnp.float32) * 0.0
        Bm = jnp.broadcast_to(Bm, (E, O, R)) + jax.random.normal(ks[5], (E, O, R), dtype=jnp.float32) * 0.02
        return {'x': x, 'language_ids': language_ids, 'W': W, 'Wr': Wr, 'A': A, 'B': Bm}
    _L1_cond_all = _L1_cond_setup()
    _L1_cond_in = {k: v for k, v in _L1_cond_all.items() if k in ('W', 'Wr', 'A', 'B')}
    del _L1_cond_all

    def _L2_cond_setup():
        import jax, jax.numpy as jnp
        import numpy as np
        B, S, D_IN, D_OUT = (4, 512, 1024, 1024)
        R, NUM_LABELERS = (32, 5)
        LORA_SCALING = 16 / 32
        key = jax.random.key(seed)
        k1, k2, k3, k4, k5 = jax.random.split(key, 5)
        x = jax.random.normal(k1, (B, S, D_IN), dtype=jnp.float32)
        labeler_index = jax.random.randint(k2, (B,), 0, NUM_LABELERS, dtype=jnp.int64)
        W = jax.random.normal(k3, (D_OUT, D_IN), dtype=jnp.float32) * 0.02
        lora_A = jax.random.normal(k4, (NUM_LABELERS, D_IN, R), dtype=jnp.float32) * 0.02
        lora_B_w = jax.random.normal(k5, (D_OUT, R), dtype=jnp.float32) * 0.02
        return {'x': x, 'labeler_index': labeler_index, 'W': W, 'lora_A': lora_A, 'lora_B_w': lora_B_w}
    _L2_cond_all = _L2_cond_setup()
    _L2_cond_in = {k: v for k, v in _L2_cond_all.items() if k in ('W', 'lora_A', 'lora_B_w')}
    del _L2_cond_all

    def _L3_cond_setup():
        import jax, jax.numpy as jnp
        import numpy as np
        GROUP = 128
        LORA_ALPHA = 32.0
        LORA_RANK = 64
        key = jax.random.key(seed)
        k1, k2, k3, k4 = jax.random.split(key, 4)
        O, I = (1024, 1024)
        x = jax.random.normal(k1, (4, 512, I), dtype=jnp.float32)
        weight = jax.random.normal(k2, (O, I), dtype=jnp.float32) * 0.02
        wg = weight.reshape(O, I // GROUP, GROUP)
        scale_log = jnp.log(jnp.clip(jnp.max(jnp.abs(wg), axis=2, keepdims=True), 1e-05))
        codebook = jnp.array([-1.0, -0.25, 0.0, 1.0], dtype=jnp.float32)
        lora_A = jax.random.normal(k3, (LORA_RANK, I), dtype=jnp.float32) * 0.02
        lora_B = jax.random.normal(k4, (O, LORA_RANK), dtype=jnp.float32) * 0.02
        return {'x': x, 'weight': weight, 'scale_log': scale_log, 'codebook': codebook, 'lora_A': lora_A, 'lora_B': lora_B}
    _L3_cond_all = _L3_cond_setup()
    _L3_cond_in = {k: v for k, v in _L3_cond_all.items() if k in ('weight', 'scale_log', 'lora_A', 'lora_B')}
    del _L3_cond_all
    return {'x': x, 'itok_B_8_3872': itok_B_8_3872, 'itok_B_0_7': itok_B_0_7, 'itok_B_0_2': itok_B_0_2, 'condB_codebook': condB_codebook, 'L0_cond_log_dt': _L0_cond_in['log_dt'], 'L0_cond_C': _L0_cond_in['C'], 'L0_cond_log_A_real': _L0_cond_in['log_A_real'], 'L0_cond_A_imag': _L0_cond_in['A_imag'], 'L0_cond_D': _L0_cond_in['D'], 'L1_cond_W': _L1_cond_in['W'], 'L1_cond_Wr': _L1_cond_in['Wr'], 'L1_cond_A': _L1_cond_in['A'], 'L1_cond_B': _L1_cond_in['B'], 'L2_cond_W': _L2_cond_in['W'], 'L2_cond_lora_A': _L2_cond_in['lora_A'], 'L2_cond_lora_B_w': _L2_cond_in['lora_B_w'], 'L3_cond_weight': _L3_cond_in['weight'], 'L3_cond_scale_log': _L3_cond_in['scale_log'], 'L3_cond_lora_A': _L3_cond_in['lora_A'], 'L3_cond_lora_B': _L3_cond_in['lora_B']}

def reference(x, itok_B_8_3872, itok_B_0_7, itok_B_0_2, condB_codebook, L0_cond_log_dt, L0_cond_C, L0_cond_log_A_real, L0_cond_A_imag, L0_cond_D, L1_cond_W, L1_cond_Wr, L1_cond_A, L1_cond_B, L2_cond_W, L2_cond_lora_A, L2_cond_lora_B_w, L3_cond_weight, L3_cond_scale_log, L3_cond_lora_A, L3_cond_lora_B):
    import jax
    import jax.numpy as jnp

    def _L0_cond_ref(u, length, log_dt, C, log_A_real, A_imag, D):
        import math
        import jax, jax.numpy as jnp
        import numpy as np
        H, N, B, L = (64, 64, 16, 1024)
        DT_MIN, DT_MAX = (0.001, 0.1)

        def _get_kernel(log_dt, C, log_A_real, A_imag, length):
            Cc = C[..., 0] + 1j * C[..., 1]
            dt = jnp.exp(log_dt)
            A = -jnp.exp(log_A_real) + 1j * A_imag
            dtA = A * dt[:, None]
            P = dtA[:, :, None] * jnp.arange(length, dtype=jnp.float32)
            Cs = Cc * (jnp.exp(dtA) - 1.0) / A
            K = 2.0 * jnp.einsum('hn,hnl->hl', Cs, jnp.exp(P)).real
            return K
        Bq, Hq, Lq = u.shape
        mask = (jnp.arange(Lq) < length[:, None]).astype(u.dtype)
        u_m = u * mask[:, None, :]
        kernel = _get_kernel(log_dt, C, log_A_real, A_imag, Lq)
        n = 2 * Lq
        k_f = jnp.fft.rfft(kernel, n=n)
        u_f = jnp.fft.rfft(u_m, n=n)
        y = jnp.fft.irfft(u_f * k_f, n=n)[..., :Lq]
        y = y + u_m * D[:, None]
        return y * mask[:, None, :]

    def _L1_cond_ref(x, language_ids, W, Wr, A, B):
        import jax, jax.numpy as jnp
        import numpy as np
        TOP_K = 2
        LANG_BIAS = 5.0
        SCALING = 32.0 / 16.0
        LANGUAGE_PAD_ID = -1
        base = jnp.einsum('btd,od->bto', x, W)
        E = Wr.shape[0]
        logits = jnp.einsum('btd,ed->bte', x.astype(jnp.float32), Wr.astype(jnp.float32))
        expert_targets = language_ids
        valid = expert_targets >= 0
        tgt = jnp.where(valid, expert_targets, 0)
        bias = jax.nn.one_hot(tgt, E, dtype=logits.dtype) * LANG_BIAS
        bias = jnp.where(valid[:, None], bias, 0.0)
        logits = logits + bias[:, None, :]
        topw, topi = jax.lax.top_k(logits, TOP_K)
        weights = jax.nn.softmax(topw, axis=-1)
        gates = jnp.sum(jax.nn.one_hot(topi, E, dtype=weights.dtype) * weights[..., None], axis=-2)
        gates = gates.astype(x.dtype)
        h = jnp.einsum('btd,erd->bter', x, A)
        lora_out = jnp.einsum('bter,bte,eor->bto', h, gates, B)
        return base + SCALING * lora_out

    def _L2_cond_ref(x, labeler_index, W, lora_A, lora_B_w):
        import jax, jax.numpy as jnp
        import numpy as np
        B, S, D_IN, D_OUT = (4, 512, 1024, 1024)
        R, NUM_LABELERS = (32, 5)
        LORA_SCALING = 16 / 32
        base = jnp.einsum('bsi,oi->bso', x, W)
        labelers_A = lora_A[labeler_index]
        low = jnp.einsum('bsi,bir->bsr', x, labelers_A)
        delta = jnp.einsum('bsr,or->bso', low, lora_B_w) * LORA_SCALING
        return base + delta

    def _L3_cond_ref(x, weight, scale_log, codebook, lora_A, lora_B):
        import jax, jax.numpy as jnp
        import numpy as np
        GROUP = 128
        LORA_ALPHA = 32.0
        LORA_RANK = 64
        O, I = weight.shape
        lora_delta = lora_B @ lora_A * (LORA_ALPHA / LORA_RANK)
        cb = codebook / jnp.clip(jnp.max(jnp.abs(codebook)), 1e-08)
        scale = jnp.exp(scale_log)
        wg = (weight + lora_delta).reshape(O, I // GROUP, GROUP)
        normalized = wg / scale
        thresholds = (cb[:-1] + cb[1:]) * 0.5
        idx = jnp.searchsorted(thresholds, normalized, side='left')
        quantized = cb[idx]
        w = jax.lax.stop_gradient(quantized - normalized) + normalized
        w_q = (w * scale).reshape(O, I)
        w_eff = w_q + lora_delta
        return x @ w_eff.T
    x = x + _L0_cond_ref(x, itok_B_8_3872, L0_cond_log_dt, L0_cond_C, L0_cond_log_A_real, L0_cond_A_imag, L0_cond_D)
    x = x + _L1_cond_ref(x, itok_B_0_7, L1_cond_W, L1_cond_Wr, L1_cond_A, L1_cond_B)
    x = x + _L2_cond_ref(x, itok_B_0_2, L2_cond_W, L2_cond_lora_A, L2_cond_lora_B_w)
    x = x + _L3_cond_ref(x, L3_cond_weight, L3_cond_scale_log, condB_codebook, L3_cond_lora_A, L3_cond_lora_B)
    return x

_drawn_inputs = setup_inputs


def setup_inputs(seed=0):
    import zlib

    import numpy as np

    out = dict(_drawn_inputs(seed))
    spreads = {'L0_cond_log_A_real': (-0.6931471824645996, 0.2)}
    factors = {}
    for name, (base, spread) in spreads.items():
        noise = np.random.default_rng([zlib.crc32(name.encode()), seed]).standard_normal(out[name].shape)
        drawn = base * np.exp(spread * noise) if base else spread * noise
        out[name] = jnp.asarray(drawn.astype(out[name].dtype))
    for name, factor in factors.items():
        out[name] = (out[name] * factor).astype(out[name].dtype)
    return out
```

```python
from contextlib import ExitStack
import math

import concourse.bass as bass
from concourse import mybir

F32 = mybir.dt.float32
F32R = mybir.dt.float32r
I32 = mybir.dt.int32
U32 = mybir.dt.uint32
ALU = mybir.AluOpType
ACT = mybir.ActivationFunctionType
AX_X = mybir.AxisListType.X

P = 128
BANK = 512
MAGIC = 12582912.0
LN2_HI, LN2_LO = 0.693145751953125, 1.42860682030941723e-6
TWO_PI = (6.28125, 0.0019350051879882812, 3.0199157663446e-07)
BIG = 3.0e38


def resid_stack_kernel(nc, x, lengths, languages, labels, codebook, log_dt, C_ri, log_A_real, A_imag, D_skip,
                       W1, Wr, A_lang, B_lang, W2, A_lab, B_lab, W3, scale_log, A3_lora, B3_lora, out):
    B, H, L = x.shape
    N = A_imag.shape[1]
    NC = L // P
    E, R, _ = A_lang.shape
    ER = E * R
    NL, _, RL = A_lab.shape
    LR = NL * RL
    R3 = A3_lora.shape[0]
    K_CODES = codebook.shape[0]
    HB = 2
    TILES = H // HB
    SPAN = 32
    LOWC = ER + E + LR
    C_H, C_LOG, C_LOW = L, L + ER, L + ER + E
    MW = L + LOWC
    EW = L + ER
    KP = P + L
    assert (B, N, ER, LR, HB * B, L // SPAN) == (64, 64, 128, 160, P, SPAN)
    MT = EW // P

    kpad = nc.dram_tensor("kpad", [H, 2, KP], F32, kind="Internal").ap()

    cursor = [(nc.sbuf_base + 31) // 32 * 32]

    def place(name, shape, dt, at=None):
        off = cursor[0] if at is None else at
        size = 4 * math.prod(shape[1:])
        t = nc.alloc_sbuf_tensor_at(name, shape, dt, offset=off)
        cursor[0] = off + (size + 31) // 32 * 32
        return t

    ident = place("ident", [P, P], F32)
    iota8 = place("iota8", [P, E], F32)
    mask = place("mask", [P, NC, B], I32)
    langbias = place("langbias", [P, E], F32)
    labsel = place("labsel", [P, NL], F32)
    region_m = cursor[0]
    Mh = place("Mh", [P, NC, MW], F32R)
    Ml = place("Ml", [P, NC, MW], F32R)
    R1h = place("R1h", [P, L], F32R)
    R1l = place("R1l", [P, L], F32R)
    R2s = place("R2s", [3 * RL, L], F32R)
    BLh = place("BLh", [P, LR], F32R)
    BLl = place("BLl", [P, LR], F32R)
    region_carry = cursor[0]
    QT = place("QT", [P, NC, EW], F32)
    LAp = place("LAp", [P, MT, LR], F32)
    Bw3 = place("Bw3", [P, NC, 3 * RL], F32)
    AT = place("AT", [P, NC, ER + E], F32)
    quant = place("quant", [P, NC, L], F32)
    vnorm = place("vnorm", [P, NC, L], F32)
    A3 = place("A3", [P, NC, L], F32, at=cursor[0] - 4 * NC * L)
    tau = place("tau", [P, K_CODES + 1], F32)
    cb = place("cb", [P, K_CODES], F32)
    cbmid = place("cbmid", [P, K_CODES], F32)
    cbs = place("cbs", [P, 8], F32)
    keep = place("keep", [P, K_CODES], I32)
    tabs = place("tabs", [P, 4, H], F32)
    mrow = place("mrow", [P, SPAN], F32)
    Drow = place("Drow", [1, H], F32)
    half_pi = place("half_pi", [P, 1], F32)
    scale3 = place("scale3", [P, NC, NC], F32)
    inv_scale3 = place("inv_scale3", [P, NC, NC], F32)
    assert cursor[0] <= nc.sbuf_usable_end, cursor[0]
    E1 = place("E1", [P, NC, EW], F32, at=region_m)
    A2 = place("A2", [P, NC, L], F32)
    LA = place("LA", [P, NC, NL, RL], F32)
    w2s_at = cursor[0]
    W2s = place("W2s", [P, 2, L], F32)
    B3T = place("B3T", [R3, L], F32, at=w2s_at)
    A3l = place("A3l", [R3, L], F32)
    step_t = place("step_t", [P, 2, 1024], F32)
    Vt = place("Vt", [P, H, SPAN], F32, at=cursor[0] - 4 * 2048)
    assert cursor[0] <= region_carry, (cursor[0], region_carry)
    HH = H // 2
    quant_at = region_carry + 4 * (NC * EW + MT * LR + NC * 3 * RL + NC * (ER + E))
    theta = place("theta", [P, HH, SPAN], F32, at=quant_at)
    expo = place("expo", [P, HH, SPAN], F32)
    turns = place("turns", [P, HH, SPAN], F32)
    rem = place("rem", [P, HH, SPAN], F32)
    sin_half = place("sin_half", [P, HH, SPAN], F32)
    cos_half = place("cos_half", [P, HH, SPAN], F32)
    Ut = place("Ut", [P, H, SPAN], F32)
    Kf = place("Kf", [SPAN, H, SPAN], F32, at=quant_at)
    Kh = place("Kh", [SPAN, H, SPAN], F32R)
    Kl = place("Kl", [SPAN, H, SPAN], F32R)
    nat = place("nat", [H, 16, N], F32, at=region_carry)
    logs = place("logs", [H, 1 + N], F32)
    exps = place("exps", [H, 1 + N], F32)
    c_in = place("c_in", [H, N, 2], F32)
    nat4 = place("nat4", [H, 4, 2 * N], F32)
    ex = place("ex", [P, 6, H + 1], F32)
    ex_bits = place("ex_bits", [P, H + 1], I32)
    B3n = place("B3n", [P, NC, R3], F32)
    A_nat = place("A_nat", [P, L], F32)
    Wr_nat = place("Wr_nat", [E, L], F32)
    BwIn = place("BwIn", [P, NC, RL], F32)
    len_i = place("len_i", [P, B], I32)
    len_f = place("len_f", [P, B], F32)
    ids_i = place("ids_i", [P, 2], I32)
    ids_f = place("ids_f", [P, 2], F32)
    lidx = place("lidx", [P, NC, B], F32)
    zpad = place("zpad", [H, 2, P], F32)
    assert cursor[0] <= region_carry + 4 * NC * EW

    X = place("X", [P, L], F32, at=region_carry)
    Xr = place("Xr", [P, NC, P], F32)
    xT = place("xT", [P, HB, NC, B], F32)
    xrh = place("xrh", [P, HB, NC, B], F32R)
    xrl = place("xrl", [P, HB, NC, B], F32R)
    toep = [place(f"toep{hh}", [P, 2, L], F32R) for hh in range(HB)]
    x0h = place("x0h", [P, NC, P], F32R)
    x0l = place("x0l", [P, NC, P], F32R)
    O = place("O", [P, L], F32)
    gsm = place("gsm", [P, 8, E], F32)
    gidx = place("gidx", [P, E], U32)
    hg = place("hg", [P, E, R], F32)
    hgTh = place("hgTh", [P, P], F32R)
    hgTl = place("hgTl", [P, P], F32R)
    lowm = place("lowm", [P, NL, RL], F32)
    low3 = place("low3", [P, 3, RL], F32)
    lowTs = place("lowTs", [3 * RL, P], F32R)
    assert cursor[0] <= nc.sbuf_usable_end

    with ExitStack() as ctx:
        bank = [ctx.enter_context(nc.psum_tensor(f"bank{n}", [P, BANK], F32)) for n in range(8)]

        def sem(name):
            return ctx.enter_context(nc.semaphore(name))

        ld_kgen, ld_codes, ld_ids = sem("ld_kgen"), sem("ld_codes"), sem("ld_ids")
        ld_w2 = [sem("ld_w2a"), sem("ld_w2b")]
        ld_w1, ld_blang, ld_rank = sem("ld_w1"), sem("ld_blang"), sem("ld_rank")
        ld_a3l, ld_la, ld_w3, kpad_stored = sem("ld_a3l"), sem("ld_la"), sem("ld_w3"), sem("kpad_stored")
        consts_ready, pool_step = sem("consts_ready"), sem("pool_step")
        e1_ready, bw_ready, a2_ready = sem("e1_ready"), sem("bw_ready"), sem("a2_ready")
        dve_step, act_step = sem("dve_step"), sem("act_step")
        stage_full = sem("stage_full")
        stage_free = {"act": sem("stage_free_act"), "dve": sem("stage_free_dve")}
        nat_rem, nat_sin, nat4_ready = sem("nat_rem"), sem("nat_sin"), sem("nat4_ready")
        tab_rem, tab_sin, tab_ready = sem("tab_rem"), sem("tab_sin"), sem("tab_ready")
        kf_ready, kh_ready, kl_ready, cb_ready = sem("kf_ready"), sem("kh_ready"), sem("kl_ready"), sem("cb_ready")
        quant_init = sem("quant_init")
        qt_full, qt_free = sem("qt_full"), sem("qt_free")

        passed = {e: sem(f"waits_passed_{e}") for e in ("pe", "dve", "pool")}

        def hold(eng, name):
            eng.sem_inc(passed[name], 1)

        jobs = []
        for ot in range(NC):
            jobs += [("w2t", ot, 0), ("w2t", ot, 1)]
            if ot == 3:
                jobs.append(("nat4", 0, 0))
        jobs += [("at", 0, 0), ("at", 1, 0), ("wrt", 0, 0), ("b3t", 0, 0), ("b3t", 1, 0)]
        jobs += [("kern", g, 0) for g in range(4)]
        jobs += [("delta", ot, half) for ot in range(NC) for half in range(2)]
        jobs += [("lap", mt, 0) for mt in range(MT)]
        jobs += [("delta2", ot, half) for ot in range(NC) for half in range(2)]
        taker = ["dve" if j[0].startswith("delta") else "act" for j in jobs]
        jobno = {j: n for n, j in enumerate(jobs)}

        def stage(j):
            return bank[jobno[j] % 2]

        def wait_stage_free(pe, j):
            n = jobno[j] - 2
            if n >= 0:
                pe.wait_ge(stage_free[taker[n]], taker[:n + 1].count(taker[n]))

        with nc.Block() as block:

            @block.sync
            def _(sp):
                sp.dma_start(logs[:, 0:1], log_dt.rearrange("(h a) -> h a", a=1)).then_inc(ld_kgen, 16)
                sp.dma_start(logs[:, 1:1 + N], log_A_real).then_inc(ld_kgen, 16)
                sp.dma_start(nat[:, 0, :], A_imag).then_inc(ld_kgen, 16)
                sp.dma_start(c_in[:, :, :], C_ri).then_inc(ld_kgen, 16)
                sp.dma_start(scale3[:, :, :], scale_log.rearrange("(t p) g a -> p t (g a)", p=P)).then_inc(ld_codes, 16)
                sp.dma_start(cb[:, :], bass.AP(codebook.tensor, 0, [[0, P], [1, K_CODES]])).then_inc(ld_codes, 16)
                for ot in range(2):
                    sp.dma_start(W2s[:, ot, :], W2[ot * P:(ot + 1) * P, :]).then_inc(ld_w2[ot], 16)
                sp.dma_start(Drow[:, :], D_skip.rearrange("(a h) -> a h", a=1)).then_inc(ld_rank, 16)
                sp.dma_start(A_nat[:, :], A_lang.rearrange("e r d -> (e r) d")).then_inc(ld_rank, 16)
                sp.dma_start(Wr_nat[:, :], Wr).then_inc(ld_rank, 16)
                sp.dma_start(B3n[:, :, :], B3_lora.rearrange("(t p) r -> p t r", p=P)).then_inc(ld_rank, 16)
                sp.dma_start(BwIn[:, :, :], B_lab.rearrange("(t p) r -> p t r", p=P)).then_inc(ld_rank, 16)
                for ot in range(2, NC):
                    sp.wait_ge(stage_full, jobno[("w2t", ot - 2, 1)] + 1)
                    sp.dma_start(W2s[:, ot % 2, :], W2[ot * P:(ot + 1) * P, :]).then_inc(ld_w2[ot % 2], 16)
                    sp.dma_start(E1[:, ot - 2, 0:L], W1[(ot - 2) * P:(ot - 1) * P, :]).then_inc(ld_w1, 16)
                for ot in range(NC - 2, NC):
                    sp.dma_start(E1[:, ot, 0:L], W1[ot * P:(ot + 1) * P, :]).then_inc(ld_w1, 16)
                for it in range(NC):
                    sp.dma_start(E1[:, it, L:EW].rearrange("p (e r) -> p e r", e=E),
                                 B_lang[:, it * P:(it + 1) * P, :].rearrange("e o r -> o e r")).then_inc(ld_blang, 16)
                for ot in range(NC):
                    sp.dma_start(vnorm[:, ot, :], W3[ot * P:(ot + 1) * P, :]).then_inc(ld_w3, 16)
                for it in range(NC):
                    sp.dma_start(LA[:, it, :, :], A_lab[:, it * P:(it + 1) * P, :].rearrange("l i r -> i l r")).then_inc(ld_la, 16)
                sp.wait_ge(stage_full, jobno[("w2t", NC - 1, 1)] + 1)
                sp.dma_start(A3l[:, :], A3_lora).then_inc(ld_a3l, 16)
                sp.dma_start(len_i[:, :], bass.AP(lengths.tensor, 0, [[0, P], [1, B]])).then_inc(ld_ids, 16)
                for hh in range(HB):
                    rows = slice(hh * B, (hh + 1) * B)
                    sp.dma_start(ids_i[rows, 0:1], languages.rearrange("(b a) -> b a", a=1)).then_inc(ld_ids, 16)
                    sp.dma_start(ids_i[rows, 1:2], labels.rearrange("(b a) -> b a", a=1)).then_inc(ld_ids, 16)
                sp.wait_ge(consts_ready, 1)
                sp.dma_start(kpad[:, :, 0:P], zpad[:, :, :]).then_inc(kpad_stored, 16)
                for part, t, ready in ((0, Kh, kh_ready), (1, Kl, kl_ready)):
                    sp.wait_ge(ready, 1)
                    sp.dma_start(bass.AP(kpad.tensor, part * KP + P, [[SPAN, SPAN], [2 * KP, H], [1, SPAN]]),
                                 t[:, :, :].bitcast(F32)).then_inc(kpad_stored, 16)

            @block.gpsimd
            def _(pool):
                n_step = [0]

                def step(ins):
                    n_step[0] += 1
                    ins.then_inc(pool_step, 1)
                    pool.wait_ge(pool_step, n_step[0])

                step(pool.memset(ident[:, :], 0.0))
                pool.memset(half_pi[:, :], math.pi / 2)
                pool.memset(zpad[:, :, :], 0.0)
                pool.iota(mrow[:, :], pattern=[[1, SPAN]], base=0, channel_multiplier=0,
                          allow_small_or_imprecise_dtypes=True)
                pool.iota(iota8[:, :], pattern=[[1, E]], base=0, channel_multiplier=0,
                          allow_small_or_imprecise_dtypes=True)
                pool.iota(lidx[:, :, :], pattern=[[P, NC], [0, B]], base=0, channel_multiplier=1,
                          allow_small_or_imprecise_dtypes=True)
                pool.affine_select(out=ident[:, :], in_=ident[:, :], compare_op=ALU.not_equal, fill=1.0, base=0,
                                   pattern=[[-1, P]], channel_multiplier=1).then_inc(consts_ready, 1)
                pool.wait_ge(ld_rank, 80)
                for n in range(3):
                    pool.tensor_scalar(Bw3[:, :, n * RL:(n + 1) * RL], BwIn[:, :, :], 0.5, None, ALU.mult).then_inc(bw_ready, 1)
                pool.wait_ge(consts_ready, 1)
                pool.wait_ge(ld_w1, 16 * NC)
                for it in range(NC):
                    d = E1[:, it, it * P:(it + 1) * P]
                    pool.tensor_tensor(d, d, ident[:, :], ALU.add).then_inc(e1_ready, 1)
                pool.wait_ge(ld_blang, 16 * NC)
                pool.tensor_scalar(E1[:, :, L:EW], E1[:, :, L:EW], 2.0, None, ALU.mult).then_inc(e1_ready, 1)
                for it in range(NC):
                    j = jobno[("w2t", it, it // 4)]
                    pool.wait_ge(stage_free["act"], taker[:j + 1].count("act"))
                    d = A2[:, it, it * P:(it + 1) * P]
                    pool.tensor_tensor(d, d, ident[:, :], ALU.add).then_inc(a2_ready, 1)

            @block.tensor
            def _(pe):
                pe.wait_ge(consts_ready, 1)

                def w2t(ot):
                    pe.wait_ge(ld_w2[ot % 2], 16 * (ot // 2 + 1))
                    for half in range(2):
                        j = ("w2t", ot, half)
                        wait_stage_free(pe, j)
                        for n in range(4):
                            it = 4 * half + n
                            last = pe.transpose(stage(j)[:, n * P:(n + 1) * P], W2s[:, ot % 2, it * P:(it + 1) * P], ident[:, :])
                        last.then_inc(stage_full, 1)

                for ot in range(NC):
                    w2t(ot)
                    if ot == 3:
                        j = ("nat4", 0, 0)
                        wait_stage_free(pe, j)
                        pe.wait_ge(nat4_ready, 1)
                        for q in range(4):
                            last = pe.transpose(stage(j)[:, q * H:(q + 1) * H], nat4[:, q, :], ident[0:H, 0:H])
                        last.then_inc(stage_full, 1)
                pe.wait_ge(ld_rank, 80)
                for g in range(2):
                    j = ("at", g, 0)
                    wait_stage_free(pe, j)
                    for n in range(4):
                        c = 4 * g + n
                        last = pe.transpose(stage(j)[:, n * P:(n + 1) * P], A_nat[:, c * P:(c + 1) * P], ident[:, :])
                    last.then_inc(stage_full, 1)
                j = ("wrt", 0, 0)
                wait_stage_free(pe, j)
                for c in range(NC):
                    last = pe.transpose(stage(j)[:, c * E:(c + 1) * E], Wr_nat[:, c * P:(c + 1) * P], ident[0:E, 0:E])
                last.then_inc(stage_full, 1)
                for g in range(2):
                    j = ("b3t", g, 0)
                    wait_stage_free(pe, j)
                    for n in range(4):
                        last = pe.transpose(stage(j)[0:R3, n * P:(n + 1) * P], B3n[:, 4 * g + n, :], ident[:, :])
                    last.then_inc(stage_full, 1)

                def qt(kt):
                    s = 2 + 3 * (kt % 2)
                    if kt >= 2:
                        pe.wait_ge(qt_free, kt - 1)
                    for n, (a, b) in enumerate(((0, BANK), (BANK, L), (L, EW))):
                        for it in range(NC):
                            last = pe.matmul(bank[s + n][:, 0:b - a], A2[:, it, kt * P:(kt + 1) * P], E1[:, it, a:b],
                                             start=(it == 0), stop=(it == NC - 1))
                    last.then_inc(qt_full, 1)

                def delta(kind):
                    for ot in range(NC):
                        for half in range(2):
                            j = (kind, ot, half)
                            wait_stage_free(pe, j)
                            pe.matmul(stage(j)[:, :], B3T[:, ot * P:(ot + 1) * P], A3l[:, half * BANK:(half + 1) * BANK],
                                      start=True, stop=True).then_inc(stage_full, 1)

                pe.wait_ge(e1_ready, NC + 1)
                pe.wait_ge(a2_ready, NC)
                qt(0)
                qt(1)
                pe.wait_ge(tab_ready, 2)
                for g in range(4):
                    j = ("kern", g, 0)
                    wait_stage_free(pe, j)
                    for n in range(16):
                        h = 16 * g + n
                        last = pe.matmul(stage(j)[0:SPAN, n * SPAN:(n + 1) * SPAN], Ut[:, h, :], Vt[:, h, :], start=True, stop=True)
                    last.then_inc(stage_full, 1)
                pe.wait_ge(stage_free["act"], taker[:jobno[("b3t", 1, 0)] + 1].count("act"))
                pe.wait_ge(ld_a3l, 16)
                delta("delta")
                for kt in range(2, NC):
                    qt(kt)
                pe.wait_ge(ld_la, 16 * NC)
                for mt in range(MT):
                    j = ("lap", mt, 0)
                    wait_stage_free(pe, j)
                    for it in range(NC):
                        last = pe.matmul(stage(j)[:, 0:LR], E1[:, it, mt * P:(mt + 1) * P],
                                         LA[:, it, :, :].rearrange("p l r -> p (l r)"), start=(it == 0), stop=(it == NC - 1))
                    last.then_inc(stage_full, 1)
                delta("delta2")

            @block.scalar
            def _(act):
                n_step = [0]

                def step(ins):
                    n_step[0] += 1
                    ins.then_inc(act_step, 1)
                    act.wait_ge(act_step, n_step[0])

                def take(j, out, in_, scale=None):
                    act.wait_ge(stage_full, jobno[j] + 1)
                    ins = act.activation(out, in_, ACT.Copy) if scale is None else act.activation(out, in_, ACT.Copy, scale=scale)
                    ins.then_inc(stage_free["act"], 1)

                def w2t(ot):
                    for half in range(2):
                        j = ("w2t", ot, half)
                        take(j, A2[:, 4 * half:4 * half + 4, ot * P:(ot + 1) * P], stage(j)[:, :].rearrange("p (t k) -> p t k", t=4))

                def table(k):
                    act.wait_ge(tab_rem, k + 1)
                    step(act.activation(sin_half[:, :, :], rem[:, :, :], ACT.Sin, scale=0.5))
                    step(act.activation(turns[:, :, :], rem[:, :, :], ACT.Abs))
                    step(act.activation(cos_half[:, :, :], turns[:, :, :], ACT.Sin, bias=half_pi[:, 0:1], scale=-0.5))
                    act.activation(rem[:, :, :], expo[:, :, :], ACT.Exp, scale=(1.0, float(SPAN))[k % 2]).then_inc(tab_sin, 1)

                w2t(0)
                w2t(1)
                act.wait_ge(nat_rem, 1)
                step(act.activation(nat[:, 4, :], nat[:, 3, :], ACT.Sin, scale=0.5))
                step(act.activation(nat[:, 5, :], nat[:, 3, :], ACT.Abs))
                act.activation(nat[:, 6, :], nat[:, 5, :], ACT.Sin, bias=half_pi[0:H, 0:1], scale=-0.5).then_inc(nat_sin, 1)
                w2t(2)
                w2t(3)
                j = ("nat4", 0, 0)
                take(j, tabs[:, :, :], stage(j)[:, 0:4 * H].rearrange("p (q h) -> p q h", q=4))
                w2t(4)
                w2t(5)
                table(0)
                w2t(6)
                w2t(7)
                for g in range(2):
                    j = ("at", g, 0)
                    take(j, AT[:, 4 * g:4 * g + 4, 0:ER], stage(j)[:, :].rearrange("p (c e) -> p c e", c=4))
                j = ("wrt", 0, 0)
                take(j, AT[:, :, ER:ER + E], stage(j)[:, 0:NC * E].rearrange("p (c e) -> p c e", c=NC))
                for g in range(2):
                    j = ("b3t", g, 0)
                    take(j, B3T[:, g * BANK:(g + 1) * BANK], stage(j)[0:R3, :], scale=0.5)
                for k in range(1, 4):
                    table(k)

                def qt(kt):
                    s = 2 + 3 * (kt % 2)
                    act.wait_ge(qt_full, kt + 1)
                    act.activation(QT[:, kt, 0:BANK], bank[s][:, :], ACT.Copy)
                    act.activation(QT[:, kt, BANK:L], bank[s + 1][:, :], ACT.Copy)
                    act.activation(QT[:, kt, L:EW], bank[s + 2][:, 0:ER], ACT.Copy).then_inc(qt_free, 1)

                qt(0)
                qt(1)
                for g in range(4):
                    j = ("kern", g, 0)
                    take(j, Kf[:, 16 * g:16 * g + 16, :], stage(j)[0:SPAN, :].rearrange("a (h b) -> a h b", h=16))
                act.wait_ge(kf_ready, 1)
                act.activation(Kh[:, :, :], Kf[:, :, :], ACT.Copy).then_inc(kh_ready, 1)
                act.wait_ge(kpad_stored, 48)
                act.wait_ge(cb_ready, 1)
                act.activation(quant[:, :, :].rearrange("p t k -> p (t k)"), cb[:, 0:1].to_broadcast([P, NC * L]), ACT.Copy).then_inc(quant_init, 1)
                for kt in range(2, NC):
                    qt(kt)
                for mt in range(MT):
                    j = ("lap", mt, 0)
                    take(j, LAp[:, mt, :], stage(j)[:, 0:LR])

            @block.vector
            def _(dve):
                n_step = [0]

                def step(ins):
                    n_step[0] += 1
                    ins.then_inc(dve_step, 1)
                    dve.wait_ge(dve_step, n_step[0])

                def exp_to(dst, src, rows, w):
                    t = [ex[0:rows, n, 0:w] for n in range(6)]
                    bits = ex_bits[0:rows, 0:w]
                    step(dve.tensor_scalar(t[0], src, -87.0, 88.0, ALU.max, ALU.min))
                    step(dve.tensor_scalar(t[1], t[0], 1.0 / math.log(2.0), MAGIC, ALU.mult, ALU.add))
                    step(dve.tensor_scalar(t[2], t[1], MAGIC, None, ALU.subtract))
                    step(dve.scalar_tensor_tensor(t[3], t[2], -LN2_HI, t[0], ALU.mult, ALU.add))
                    step(dve.scalar_tensor_tensor(t[4], t[2], -LN2_LO, t[3], ALU.mult, ALU.add))
                    step(dve.tensor_scalar(t[5], t[4], 1.0 / math.factorial(7), None, ALU.mult))
                    for n in range(6, 0, -1):
                        step(dve.scalar_tensor_tensor(t[5], t[5], 1.0 / math.factorial(n), t[4], ALU.add, ALU.mult))
                    step(dve.tensor_scalar(t[5], t[5], 1.0, None, ALU.add))
                    step(dve.tensor_scalar(bits, t[2], 127.0, float(1 << 23), ALU.add, ALU.mult))
                    step(dve.tensor_tensor(dst, t[5], bits.bitcast(F32), ALU.mult))

                def reduce_angle(dst, ang, tmp):
                    step(dve.tensor_scalar(tmp, ang, 1.0 / (2 * math.pi), MAGIC, ALU.mult, ALU.add))
                    step(dve.tensor_scalar(tmp, tmp, MAGIC, None, ALU.subtract))
                    step(dve.scalar_tensor_tensor(dst, tmp, -TWO_PI[0], ang, ALU.mult, ALU.add))
                    step(dve.scalar_tensor_tensor(dst, tmp, -TWO_PI[1], dst, ALU.mult, ALU.add))
                    return dve.scalar_tensor_tensor(dst, tmp, -TWO_PI[2], dst, ALU.mult, ALU.add)

                dve.wait_ge(ld_kgen, 64)
                exp_to(exps[:, :], logs[:, :], H, 1 + N)
                dt, eA, Aim = exps[:, 0:1], exps[:, 1:1 + N], nat[:, 0, :]
                step(dve.tensor_scalar(nat[:, 1, :], eA, dt, -1.0, ALU.mult, ALU.mult))
                step(dve.tensor_scalar(nat[:, 2, :], Aim, dt, None, ALU.mult))
                dtA_re, dtA_im = nat[:, 1, :], nat[:, 2, :]
                reduce_angle(nat[:, 3, :], dtA_im, nat[:, 7, :]).then_inc(nat_rem, 1)
                exp_to(nat[:, 8, :], dtA_re, H, N)
                dve.wait_ge(nat_sin, 1)
                sh, ch, mag = nat[:, 4, :], nat[:, 6, :], nat[:, 8, :]
                step(dve.scalar_tensor_tensor(nat[:, 9, :], sh, -2.0, sh, ALU.mult, ALU.mult))
                step(dve.scalar_tensor_tensor(nat[:, 9, :], nat[:, 9, :], 1.0, mag, ALU.add, ALU.mult))
                step(dve.tensor_scalar(nat[:, 9, :], nat[:, 9, :], 1.0, None, ALU.subtract))
                step(dve.scalar_tensor_tensor(nat[:, 10, :], sh, 2.0, ch, ALU.mult, ALU.mult))
                step(dve.tensor_tensor(nat[:, 10, :], nat[:, 10, :], mag, ALU.mult))
                Er, Ei, Cr, Ci = nat[:, 9, :], nat[:, 10, :], c_in[:, :, 0], c_in[:, :, 1]
                num_r, num_i, t0, t1, t2 = (nat[:, k, :] for k in (11, 12, 13, 14, 15))
                step(dve.tensor_tensor(t0, Cr, Er, ALU.mult))
                step(dve.tensor_tensor(t1, Ci, Ei, ALU.mult))
                step(dve.tensor_tensor(num_r, t0, t1, ALU.subtract))
                step(dve.tensor_tensor(t0, Cr, Ei, ALU.mult))
                step(dve.tensor_tensor(t1, Ci, Er, ALU.mult))
                step(dve.tensor_tensor(num_i, t0, t1, ALU.add))
                step(dve.tensor_tensor(t0, eA, eA, ALU.mult))
                step(dve.tensor_tensor(t1, Aim, Aim, ALU.mult))
                step(dve.tensor_tensor(t0, t0, t1, ALU.add))
                step(dve.reciprocal(t2, t0))
                step(dve.tensor_tensor(t0, num_i, Aim, ALU.mult))
                step(dve.tensor_tensor(t1, num_r, eA, ALU.mult))
                step(dve.tensor_tensor(t0, t0, t1, ALU.subtract))
                step(dve.scalar_tensor_tensor(nat4[:, 2, 0:N], t0, 2.0, t2, ALU.mult, ALU.mult))
                step(dve.scalar_tensor_tensor(nat4[:, 2, N:2 * N], t0, -2.0, t2, ALU.mult, ALU.mult))
                step(dve.tensor_tensor(t0, num_r, Aim, ALU.mult))
                step(dve.tensor_tensor(t1, num_i, eA, ALU.mult))
                step(dve.tensor_tensor(t0, t0, t1, ALU.add))
                for s in range(2):
                    cols = slice(s * N, (s + 1) * N)
                    step(dve.scalar_tensor_tensor(nat4[:, 3, cols], t0, 2.0, t2, ALU.mult, ALU.mult))
                    step(dve.tensor_copy(nat4[:, 0, cols], dtA_re))
                    last = dve.tensor_copy(nat4[:, 1, cols], dtA_im)
                    if s == 0:
                        step(last)
                last.then_inc(nat4_ready, 1)

                dve.wait_ge(ld_codes, 32)
                flat = scale3[:, :, :].rearrange("p t g -> p (t g)")
                exp_to(flat, flat, P, NC * NC)
                step(dve.reciprocal(inv_scale3[:, :, :], scale3[:, :, :]))
                step(dve.scalar_tensor_tensor(cbmid[:, :], cb[:, :], -1.0, cb[:, :], ALU.mult, ALU.max))
                step(dve.reduce_max(cbs[:, 1:2], cbmid[:, :], AX_X))
                step(dve.tensor_scalar(cbs[:, 0:1], cbs[:, 1:2], 1e-8, None, ALU.max))
                step(dve.reciprocal(cbs[:, 1:2], cbs[:, 0:1]))
                dve.tensor_scalar(cb[:, :], cb[:, :], cbs[:, 1:2], None, ALU.mult).then_inc(cb_ready, 1)

                dve.wait_ge(stage_free["act"], taker[:jobno[("nat4", 0, 0)] + 1].count("act"))
                tb = [P, HH, SPAN]
                lo, hi = slice(0, N), slice(N, 2 * N)
                for half in range(2):
                    rows = slice(half * HH, (half + 1) * HH)
                    q = [tabs[:, k, rows].unsqueeze(2).broadcast_to(tb) for k in range(4)]
                    m = mrow[:, :].unsqueeze(1).broadcast_to(tb)
                    step(dve.tensor_tensor(theta[:, :, :], q[1], m, ALU.mult))
                    step(dve.tensor_tensor(expo[:, :, :], q[0], m, ALU.mult))
                    reduce_angle(rem[:, :, :], theta[:, :, :], turns[:, :, :]).then_inc(tab_rem, 1)
                    dve.wait_ge(tab_sin, 2 * half + 1)
                    step(dve.scalar_tensor_tensor(turns[lo, :, :], sin_half[lo, :, :], -2.0, sin_half[lo, :, :], ALU.mult, ALU.mult))
                    step(dve.tensor_scalar(turns[lo, :, :], turns[lo, :, :], 1.0, None, ALU.add))
                    step(dve.scalar_tensor_tensor(turns[hi, :, :], sin_half[hi, :, :], 2.0, cos_half[hi, :, :], ALU.mult, ALU.mult))
                    step(dve.tensor_tensor(Vt[:, rows, :], turns[:, :, :], rem[:, :, :], ALU.mult))
                    step(dve.tensor_scalar(theta[:, :, :], theta[:, :, :], float(SPAN), None, ALU.mult))
                    reduce_angle(rem[:, :, :], theta[:, :, :], turns[:, :, :]).then_inc(tab_rem, 1)
                    dve.wait_ge(tab_sin, 2 * half + 2)
                    sine, cosine = cos_half, sin_half
                    step(dve.scalar_tensor_tensor(sine[:, :, :], sin_half[:, :, :], 2.0, cos_half[:, :, :], ALU.mult, ALU.mult))
                    step(dve.scalar_tensor_tensor(cosine[:, :, :], sin_half[:, :, :], -2.0, sin_half[:, :, :], ALU.mult, ALU.mult))
                    step(dve.tensor_scalar(cosine[:, :, :], cosine[:, :, :], 1.0, None, ALU.add))
                    for part, first, second in ((lo, cosine, sine), (hi, sine, cosine)):
                        step(dve.tensor_tensor(turns[part, :, :], first[part, :, :], q[2][part, :, :], ALU.mult))
                        step(dve.tensor_tensor(theta[part, :, :], second[part, :, :], q[3][part, :, :], ALU.mult))
                    step(dve.tensor_tensor(turns[:, :, :], turns[:, :, :], theta[:, :, :], ALU.add))
                    dve.tensor_tensor(Ut[:, rows, :], turns[:, :, :], rem[:, :, :], ALU.mult).then_inc(tab_ready, 1)
                    dve.wait_ge(tab_ready, half + 1)

                dve.wait_ge(cb_ready, 1)
                step(dve.tensor_tensor(tau[:, 1:K_CODES], cb[:, 0:K_CODES - 1], cb[:, 1:K_CODES], ALU.add))
                step(dve.tensor_scalar(tau[:, 1:K_CODES], tau[:, 1:K_CODES], 0.5, None, ALU.mult))
                step(dve.memset(tau[:, 0:1], -BIG))
                step(dve.memset(tau[:, K_CODES:K_CODES + 1], BIG))
                s = K_CODES // 2
                while s >= 1:
                    mid, below, above = (tau[:, a:a + K_CODES - 2 * s + 1:2 * s] for a in (s, 0, 2 * s))
                    step(dve.tensor_tensor(mid, mid, below, ALU.max))
                    step(dve.tensor_tensor(mid, mid, above, ALU.min))
                    s //= 2
                step(dve.tensor_tensor(keep[:, :], tau[:, 1:K_CODES + 1], tau[:, 0:K_CODES], ALU.is_gt))

                dve.wait_ge(ld_ids, 80)
                step(dve.tensor_copy(len_f[:, :], len_i[:, :]))
                step(dve.tensor_tensor(mask[:, :, :], lidx[:, :, :], len_f[:, :].unsqueeze(1).broadcast_to([P, NC, B]), ALU.is_lt))
                step(dve.tensor_copy(ids_f[:, :], ids_i[:, :]))
                step(dve.tensor_scalar(langbias[:, :], iota8[:, :], ids_f[:, 0:1], 5.0, ALU.is_equal, ALU.mult))
                step(dve.tensor_scalar(labsel[:, :], iota8[:, 0:NL], ids_f[:, 1:2], None, ALU.is_equal))

                dve.wait_ge(stage_free["act"], taker[:jobno[("kern", 3, 0)] + 1].count("act"))
                dve.wait_ge(ld_rank, 80)
                dve.scalar_tensor_tensor(Kf[0:1, :, 0], Kf[0:1, :, 0], 1.0, Drow[:, :], ALU.add, ALU.add).then_inc(kf_ready, 1)
                dve.wait_ge(kh_ready, 1)
                dve.tensor_tensor(Kl[:, :, :], Kf[:, :, :], Kh[:, :, :].bitcast(F32), ALU.subtract).then_inc(kl_ready, 1)

                def take_delta(kind, t):
                    for ot in range(NC):
                        for half in range(2):
                            j = (kind, ot, half)
                            dve.wait_ge(stage_full, jobno[j] + 1)
                            part = t[:, ot, half * BANK:(half + 1) * BANK]
                            last = dve.tensor_tensor(part, stage(j)[:, :], part, ALU.add)
                            last.then_inc(stage_free["dve"], 1)

                dve.wait_ge(ld_w3, 16 * NC)
                take_delta("delta", vnorm)
                dve.wait_ge(stage_free["dve"], 2 * NC)
                by_group = "p t (g k) -> p (t g) k"
                gshape = [P, NC * NC, P]
                vg = vnorm[:, :, :].rearrange(by_group, g=NC)
                qg = quant[:, :, :].rearrange(by_group, g=NC)
                step(dve.tensor_tensor(vg, vg, inv_scale3[:, :, :].rearrange("p t g -> p (t g)").unsqueeze(2).broadcast_to(gshape), ALU.mult))

                tau_k, rise, held = cbs[:, 2:3], cbs[:, 3:4], cbs[:, 1:2]
                step(dve.tensor_copy(held, cb[:, 0:1]))
                dve.wait_ge(quant_init, 1)
                CH = 1024
                vf, qf = (t[:, :, :].rearrange("p t k -> p (t k)") for t in (vnorm, quant))
                n_ch = NC * L // CH
                per = 3 + 2 * n_ch
                base = n_step[0]
                with dve.Fori(1, K_CODES) as k:
                    here = dve.value_load(keep[0:1, bass.ds(k, 1)], min_val=0, max_val=1)
                    at = base - per + k * per

                    def stepk(ins, n):
                        ins.then_inc(dve_step, 1)
                        dve.wait_ge(dve_step, at + n)

                    with dve.If(here != 0):
                        stepk(dve.tensor_copy(tau_k, tau[:, bass.ds(k, 1)]), 1)
                        stepk(dve.tensor_tensor(rise, cb[:, bass.ds(k, 1)], held, ALU.subtract), 2)
                        hold(dve, "dve")
                        stepk(dve.tensor_copy(held, cb[:, bass.ds(k, 1)]), 3)
                        for c in range(n_ch):
                            cols = slice(c * CH, (c + 1) * CH)
                            stepk(dve.tensor_scalar(step_t[:, c % 2, :], vf[:, cols], tau_k, rise, ALU.is_gt, ALU.mult), 4 + 2 * c)
                            stepk(dve.tensor_tensor(qf[:, cols], qf[:, cols], step_t[:, c % 2, :], ALU.add), 5 + 2 * c)
                        hold(dve, "dve")
                    with dve.Else():
                        dve.sem_inc(dve_step, per)
                n_step[0] = base + per * (K_CODES - 1)

                step(dve.tensor_tensor(qf, qf, vf, ALU.subtract))
                step(dve.tensor_tensor(qf, qf, vf, ALU.add))
                step(dve.tensor_tensor(qg, qg, scale3[:, :, :].rearrange("p t g -> p (t g)").unsqueeze(2).broadcast_to(gshape), ALU.mult))
                take_delta("delta2", quant)

        a3_full, a3_free, a3_ready = sem("a3_full"), sem("a3_free"), sem("a3_ready")
        m_full, m_hi, m_lo, lowrank_hi, lowrank_lo = sem("m_full"), sem("m_hi"), sem("m_lo"), sem("lowrank_hi"), sem("lowrank_lo")
        mjobs = [(mt, nh) for mt in range(MT) for nh in range(2)] + [("r2", 0), ("r2", 1)]

        with nc.Block() as block:

            @block.tensor
            def _(pe):
                for kt in range(NC):
                    for half in range(2):
                        n = 2 * kt + half
                        if n >= 2:
                            pe.wait_ge(a3_free, n - 1)
                        for q in range(4):
                            last = pe.transpose(bank[n % 2][:, q * P:(q + 1) * P], quant[:, 4 * half + q, kt * P:(kt + 1) * P], ident[:, :])
                        last.then_inc(a3_full, 1)
                pe.wait_ge(a3_free, 2 * NC)
                pe.wait_ge(a3_ready, NC)
                for n, (mt, nh) in enumerate(mjobs):
                    if n >= 6:
                        pe.wait_ge(m_lo, n - 5)
                    out_rows = 3 * RL if mt == "r2" else P
                    for kt in range(NC):
                        lhs = Bw3[:, kt, :] if mt == "r2" else QT[:, kt, mt * P:(mt + 1) * P]
                        last = pe.matmul(bank[2 + n % 6][0:out_rows, :], lhs, A3[:, kt, nh * BANK:(nh + 1) * BANK],
                                         start=(kt == 0), stop=(kt == NC - 1))
                    last.then_inc(m_full, 1)

            @block.gpsimd
            def _(pool):
                for kt in range(NC):
                    pool.wait_ge(a3_free, 2 * kt + kt // 4 + 1)
                    d = A3[:, kt, kt * P:(kt + 1) * P]
                    pool.tensor_tensor(d, d, ident[:, :], ALU.add).then_inc(a3_ready, 1)

            def m_parts(mt, nh):
                cols = slice(nh * BANK, (nh + 1) * BANK)
                if mt == "r2":
                    return R2s[:, cols], None
                return (R1h[:, cols], R1l[:, cols]) if mt == NC else (Mh[:, mt, cols], Ml[:, mt, cols])

            @block.scalar
            def _(act):
                for n in range(2 * NC):
                    kt, half = n // 2, n % 2
                    act.wait_ge(a3_full, n + 1)
                    act.activation(A3[:, kt, half * BANK:(half + 1) * BANK], bank[n % 2][:, :], ACT.Copy).then_inc(a3_free, 1)
                act.activation(Mh[:, :, C_H:C_LOW], AT[:, :, :], ACT.Copy).then_inc(lowrank_hi, 1)
                act.activation(Mh[:, :, C_LOW:MW], LAp[:, 0:NC, :], ACT.Copy).then_inc(lowrank_hi, 1)
                act.activation(BLh[:, :], LAp[:, NC, :], ACT.Copy).then_inc(lowrank_hi, 1)
                for n, (mt, nh) in enumerate(mjobs):
                    act.wait_ge(m_full, n + 1)
                    rows = 3 * RL if mt == "r2" else P
                    act.activation(m_parts(mt, nh)[0], bank[2 + n % 6][0:rows, :], ACT.Copy).then_inc(m_hi, 1)

            @block.vector
            def _(dve):
                dve.wait_ge(lowrank_hi, 3)
                dve.tensor_tensor(Ml[:, :, C_H:C_LOW], AT[:, :, :], Mh[:, :, C_H:C_LOW].bitcast(F32), ALU.subtract).then_inc(lowrank_lo, 1)
                dve.tensor_tensor(Ml[:, :, C_LOW:MW], LAp[:, 0:NC, :], Mh[:, :, C_LOW:MW].bitcast(F32), ALU.subtract).then_inc(lowrank_lo, 1)
                dve.tensor_tensor(BLl[:, :], LAp[:, NC, :], BLh[:, :].bitcast(F32), ALU.subtract).then_inc(lowrank_lo, 1)
                for n, (mt, nh) in enumerate(mjobs):
                    dve.wait_ge(m_hi, n + 1)
                    src = bank[2 + n % 6]
                    hi, lo = m_parts(mt, nh)
                    if mt == "r2":
                        part = R2s[2 * RL:3 * RL, nh * BANK:(nh + 1) * BANK]
                        dve.tensor_tensor(part, src[2 * RL:3 * RL, :], part.bitcast(F32), ALU.subtract).then_inc(m_lo, 1)
                    else:
                        dve.tensor_tensor(lo, src[:, :], hi.bitcast(F32), ALU.subtract).then_inc(m_lo, 1)

        x_loaded, xr_copied, out_stored = sem("x_loaded"), sem("xr_copied"), sem("out_stored")
        toep_loaded = [sem("toep0_loaded"), sem("toep1_loaded")]
        xrev_ready, xrh_done, xrl_done = sem("xrev_ready"), sem("xrh_done"), sem("xrl_done")
        xnat_ready, xT_done = sem("xnat_ready"), sem("xT_done")
        conv_done, x0_done, x0h_done, x0l_done = sem("conv_done"), sem("x0_done"), sem("x0h_done"), sem("x0l_done")
        lr_done, gap_done, gexp_done, hg_done = sem("lr_done"), sem("gap_done"), sem("gexp_done"), sem("hg_done")
        hgT_ready, hgTh_done, hgTl_done = sem("hgT_ready"), sem("hgTh_done"), sem("hgTl_done")
        low_done, low3_done, lowT_ready, lowTh_done, lowTl_done = (
            sem("low_done"), sem("low3_done"), sem("lowT_ready"), sem("lowTh_done"), sem("lowTl_done"))
        out_full, out_taken, gate_step, gate_low = sem("out_full"), sem("out_taken"), sem("gate_step"), sem("gate_low")
        psX, psY, psO, psL, psT = bank[0:2], bank[2:4], bank[4:6], bank[6], bank[7]
        LAST = TILES - 1

        with nc.Block() as block:

            @block.sync
            def _(sp):
                def load_x(i):
                    for hh in range(HB):
                        sp.dma_start(X[hh * B:(hh + 1) * B, :],
                                     bass.AP(x.tensor, (HB * i + hh) * L, [[H * L, B], [1, L]])).then_inc(x_loaded, 16)

                def load_toep(i, hh):
                    src = bass.AP(kpad.tensor, (HB * i + hh) * 2 * KP + 1, [[1, P], [KP, 2], [1, L]])
                    sp.dma_start(toep[hh][:, :, :].bitcast(F32), src).then_inc(toep_loaded[hh], 16)

                def store(i):
                    for hh in range(HB):
                        sp.dma_start(bass.AP(out.tensor, (HB * i + hh) * L, [[H * L, B], [1, L]]),
                                     O[hh * B:(hh + 1) * B, :]).then_inc(out_stored, 16)

                def tile(i, more):
                    if more:
                        sp.wait_ge(xnat_ready, HB * i + 2 * HB)
                        load_x(i + 2)
                        for hh in range(HB):
                            sp.wait_ge(conv_done, HB * i + HB + hh + 1)
                            load_toep(i + 2, hh)
                    sp.wait_ge(out_taken, 2 * i + 3)
                    store(i)

                load_x(0)
                for hh in range(HB):
                    load_toep(0, hh)
                sp.wait_ge(xnat_ready, HB)
                load_x(1)
                for hh in range(HB):
                    sp.wait_ge(conv_done, hh + 1)
                    load_toep(1, hh)
                with sp.Fori(0, TILES - 2) as i:
                    tile(i, True)
                for i in range(TILES - 2, TILES):
                    tile(i, False)
                sp.wait_ge(out_stored, 32 * TILES)

            @block.gpsimd
            def _(pool):
                def reverse(i, first=False):
                    if not first:
                        pool.wait_ge(xrev_ready, HB * i)
                        hold(pool, "pool")
                    pool.wait_ge(x_loaded, 32 * i + 32)
                    hold(pool, "pool")
                    pool.tensor_copy(Xr[:, :, :], X[:, :].rearrange("p (c l) -> p c l", c=NC)[:, :, ::-1]).then_inc(xr_copied, 1)

                reverse(0, first=True)
                with pool.Fori(1, TILES) as i:
                    reverse(i)

            @block.tensor
            def _(pe):
                def reversed_in(i, first=False):
                    pe.wait_ge(xr_copied, i + 1)
                    if not first:
                        pe.wait_ge(xT_done, HB * i)
                    hold(pe, "pe")
                    for hh in range(HB):
                        rows = slice(hh * B, (hh + 1) * B)
                        for c in range(NC):
                            last = pe.transpose(psX[hh][:, c * B:(c + 1) * B], Xr[rows, c, :], ident[rows, rows])
                        last.then_inc(xrev_ready, 1)

                def natural_in(i):
                    for hh in range(HB):
                        rows = slice(hh * B, (hh + 1) * B)
                        pe.wait_ge(xrl_done, HB * i + hh + 1)
                        hold(pe, "pe")
                        for c in range(NC):
                            last = pe.transpose(psX[hh][:, c * B:(c + 1) * B], X[rows, c * P:(c + 1) * P], ident[rows, rows])
                        last.then_inc(xnat_ready, 1)

                def conv(i, hh):
                    pe.wait_ge(toep_loaded[hh], 16 * i + 16)
                    for d in range(NC):
                        cols = slice(d * P, (d + 1) * P)
                        for n, (part, xr) in enumerate(((0, xrh), (0, xrl), (1, xrh))):
                            last = pe.matmul(psY[hh][:, d * B:NC * B], toep[hh][:, part, cols],
                                             xr[:, hh, 0:NC - d, :].rearrange("p c b -> p (c b)"),
                                             start=(d == 0 and n == 0), stop=(d == NC - 1 and n == 2))
                    last.then_inc(conv_done, 1)

                def low_in(i):
                    pe.wait_ge(x0l_done, HB * i + HB)
                    for c in range(NC):
                        for n, (xs, ms) in enumerate(((x0h, Mh), (x0h, Ml), (x0l, Mh))):
                            last = pe.matmul(psL[:, 0:LOWC], xs[:, c, :], ms[:, c, L:MW], start=(c == 0 and n == 0), stop=False,
                                             skip_group_check=True)
                    last.then_inc(lr_done, 1)

                def main(i):
                    pe.wait_ge(out_taken, 2 * i + 1)
                    for c in range(NC):
                        for n, (xs, ms) in enumerate(((x0h, Mh), (x0h, Ml), (x0l, Mh))):
                            for nh in range(2):
                                pe.matmul(psO[nh][:, :], xs[:, c, :], ms[:, c, nh * BANK:(nh + 1) * BANK],
                                          start=(c == 0 and n == 0), stop=False)

                def gated_transpose(i):
                    pe.wait_ge(hg_done, i + 1)
                    pe.transpose(psT[:, 0:P], hg[:, :, :].rearrange("p e r -> p (e r)"), ident[:, :]).then_inc(hgT_ready, 1)

                def low_gated(i):
                    pe.wait_ge(hgTl_done, i + 1)
                    for n, (a, b) in enumerate(((hgTh, BLh), (hgTh, BLl), (hgTl, BLh))):
                        last = pe.matmul(psL[:, ER + E:LOWC], a[:, :], b[:, :], start=False, stop=(n == 2), skip_group_check=True)
                    last.then_inc(low_done, 1)

                def low_transpose(i):
                    pe.wait_ge(low3_done, i + 1)
                    pe.transpose(psT[0:3 * RL, P:2 * P], low3[:, :, :].rearrange("p n r -> p (n r)"), ident[:, :]).then_inc(lowT_ready, 1)

                def gated_out(i):
                    for a, b in ((hgTh, R1h), (hgTh, R1l), (hgTl, R1h)):
                        for nh in range(2):
                            pe.matmul(psO[nh][:, :], a[:, :], b[:, nh * BANK:(nh + 1) * BANK], start=False, stop=False)

                def low_out(i):
                    pe.wait_ge(lowTl_done, i + 1)
                    for nh in range(2):
                        last = pe.matmul(psO[nh][:, :], lowTs[:, :], R2s[:, nh * BANK:(nh + 1) * BANK], start=False, stop=True)
                    last.then_inc(out_full, 1)

                def tile(i, more):
                    if more:
                        reversed_in(i + 1)
                    low_in(i)
                    if more:
                        natural_in(i + 1)
                    main(i)
                    gated_transpose(i)
                    if more:
                        conv(i + 1, 0)
                    low_gated(i)
                    if more:
                        conv(i + 1, 1)
                    low_transpose(i)
                    gated_out(i)
                    low_out(i)

                reversed_in(0, first=True)
                natural_in(0)
                conv(0, 0)
                conv(0, 1)
                with pe.Fori(0, LAST) as i:
                    tile(i, True)
                tile(LAST, False)

            @block.scalar
            def _(act):
                def reversed_hi(i):
                    for hh in range(HB):
                        act.wait_ge(xrev_ready, HB * i + hh + 1)
                        act.activation(xrh[:, hh, :, :].rearrange("p c b -> p (c b)"), psX[hh][:, :], ACT.Copy).then_inc(xrh_done, 1)

                def natural(i):
                    for hh in range(HB):
                        act.wait_ge(xnat_ready, HB * i + hh + 1)
                        act.activation(xT[:, hh, :, :].rearrange("p c b -> p (c b)"), psX[hh][:, :], ACT.Copy).then_inc(xT_done, 1)

                def x0_hi(i, hh):
                    act.wait_ge(x0_done, HB * i + hh + 1)
                    act.activation(x0h[:, :, hh * B:(hh + 1) * B], xT[:, hh, :, :], ACT.Copy).then_inc(x0h_done, 1)

                def gate_exp(i):
                    act.wait_ge(gap_done, i + 1)
                    act.activation(gsm[:, 3, 0:1], gsm[:, 2, 0:1], ACT.Exp).then_inc(gexp_done, 1)

                def gated_hi(i):
                    act.wait_ge(hgT_ready, i + 1)
                    act.activation(hgTh[:, :], psT[:, 0:P], ACT.Copy).then_inc(hgTh_done, 1)

                def low_hi(i):
                    act.wait_ge(lowT_ready, i + 1)
                    act.activation(lowTs[:, :], psT[0:3 * RL, P:2 * P], ACT.Copy).then_inc(lowTh_done, 1)

                def take_out(i, first=False):
                    act.wait_ge(out_full, i + 1)
                    if not first:
                        act.wait_ge(out_stored, 32 * i)
                    for nh in range(2):
                        act.activation(O[:, nh * BANK:(nh + 1) * BANK], psO[nh][:, :], ACT.Copy).then_inc(out_taken, 1)

                def tile(i, more, first=False):
                    if more:
                        reversed_hi(i + 1)
                    gate_exp(i)
                    if more:
                        natural(i + 1)
                    gated_hi(i)
                    if more:
                        x0_hi(i + 1, 0)
                    low_hi(i)
                    if more:
                        x0_hi(i + 1, 1)
                    take_out(i, first)

                act.sem_inc(out_taken, 1)
                reversed_hi(0)
                natural(0)
                x0_hi(0, 0)
                x0_hi(0, 1)
                tile(0, True, first=True)
                with act.Fori(1, LAST) as i:
                    tile(i, True)
                tile(LAST, False)

            @block.vector
            def _(dve):
                def reversed_lo(i):
                    for hh in range(HB):
                        dve.wait_ge(xrh_done, HB * i + hh + 1)
                        t = [v[:, hh, :, :].rearrange("p c b -> p (c b)") for v in (xrl, xrh)]
                        dve.tensor_tensor(t[0], psX[hh][:, :], t[1].bitcast(F32), ALU.subtract).then_inc(xrl_done, 1)

                def select(i, hh):
                    dve.wait_ge(xT_done, HB * i + hh + 1)
                    dve.wait_ge(conv_done, HB * i + hh + 1)
                    hold(dve, "dve")
                    dve.copy_predicated(xT[:, hh, :, :].rearrange("p c b -> p (c b)"), mask[:, :, :].rearrange("p c b -> p (c b)"),
                                        psY[hh][:, :]).then_inc(x0_done, 1)

                def x0_lo(i, hh):
                    dve.wait_ge(x0h_done, HB * i + hh + 1)
                    cols = slice(hh * B, (hh + 1) * B)
                    dve.tensor_tensor(x0l[:, :, cols], xT[:, hh, :, :], x0h[:, :, cols].bitcast(F32), ALU.subtract).then_inc(x0l_done, 1)

                GATE_STEPS = 10

                def gate(i):
                    done = [0]

                    def step(ins):
                        done[0] += 1
                        ins.then_inc(gate_step, 1)
                        dve.wait_ge(gate_step, GATE_STEPS * i + done[0])

                    logit, top, gap, e, g0, g1, g = (gsm[:, k, :] for k in range(7))
                    w = gsm[:, 7, :]
                    dve.wait_ge(lr_done, i + 1)
                    step(dve.tensor_tensor(logit, psL[:, ER:ER + E], langbias[:, :], ALU.add))
                    hold(dve, "dve")
                    step(dve.max(top, logit))
                    dve.tensor_tensor(gap[:, 0:1], top[:, 1:2], top[:, 0:1], ALU.subtract).then_inc(gap_done, 1)
                    step(dve.max_index(gidx[:, :], top, logit))
                    step(dve.tensor_copy(top[:, 0:2], gidx[:, 0:2]))
                    dve.wait_ge(gexp_done, i + 1)
                    step(dve.tensor_scalar(w[:, 2:3], e[:, 0:1], 1.0, None, ALU.add))
                    step(dve.reciprocal(w[:, 0:1], w[:, 2:3]))
                    step(dve.tensor_tensor(w[:, 1:2], e[:, 0:1], w[:, 0:1], ALU.mult))
                    step(dve.tensor_scalar(g0, iota8[:, :], top[:, 0:1], w[:, 0:1], ALU.is_equal, ALU.mult))
                    step(dve.tensor_scalar(g1, iota8[:, :], top[:, 1:2], w[:, 1:2], ALU.is_equal, ALU.mult))
                    step(dve.tensor_tensor(g, g0, g1, ALU.add))
                    assert done[0] == GATE_STEPS
                    dve.tensor_tensor(hg[:, :, :], psL[:, 0:ER].rearrange("p (e r) -> p e r", e=E),
                                      g.unsqueeze(2).broadcast_to([P, E, R]), ALU.mult).then_inc(hg_done, 1)

                def gated_lo(i):
                    dve.wait_ge(hgTh_done, i + 1)
                    dve.tensor_tensor(hgTl[:, :], psT[:, 0:P], hgTh[:, :].bitcast(F32), ALU.subtract).then_inc(hgTl_done, 1)

                def low_select(i):
                    dve.wait_ge(low_done, i + 1)
                    dve.tensor_tensor(lowm[:, :, :], psL[:, ER + E:LOWC].rearrange("p (l r) -> p l r", l=NL),
                                      labsel[:, :].unsqueeze(2).broadcast_to([P, NL, RL]), ALU.mult).then_inc(gate_low, 1)
                    dve.wait_ge(gate_low, 2 * i + 1)
                    dve.tensor_reduce(low3[:, 0, :], lowm[:, :, :].rearrange("p l r -> p r l"), AX_X, ALU.add).then_inc(gate_low, 1)
                    dve.wait_ge(gate_low, 2 * i + 2)
                    dve.tensor_copy(low3[:, 1:3, :], low3[:, 0:1, :].broadcast_to([P, 2, RL])).then_inc(low3_done, 1)

                def low_lo(i):
                    dve.wait_ge(lowTh_done, i + 1)
                    part = lowTs[RL:2 * RL, :]
                    dve.tensor_tensor(part, psT[RL:2 * RL, P:2 * P], part.bitcast(F32), ALU.subtract).then_inc(lowTl_done, 1)

                def tile(i, more):
                    if more:
                        reversed_lo(i + 1)
                    gate(i)
                    gated_lo(i)
                    if more:
                        select(i + 1, 0)
                        x0_lo(i + 1, 0)
                    low_select(i)
                    if more:
                        select(i + 1, 1)
                    low_lo(i)
                    if more:
                        x0_lo(i + 1, 1)

                reversed_lo(0)
                for hh in range(HB):
                    select(0, hh)
                    x0_lo(0, hh)
                with dve.Fori(0, LAST) as i:
                    tile(i, True)
                tile(LAST, False)


_INS = ["x", "itok_B_8_3872", "itok_B_0_7", "itok_B_0_2", "condB_codebook", "L0_cond_log_dt", "L0_cond_C",
        "L0_cond_log_A_real", "L0_cond_A_imag", "L0_cond_D", "L1_cond_W", "L1_cond_Wr", "L1_cond_A", "L1_cond_B",
        "L2_cond_W", "L2_cond_lora_A", "L2_cond_lora_B_w", "L3_cond_weight", "L3_cond_scale_log", "L3_cond_lora_A",
        "L3_cond_lora_B"]


def kernel(**inputs):
    import numpy as np
    import concourse.bacc as bacc
    from concourse.bass_utils import run_bass_kernel_spmd

    nc = bacc.Bacc("TRN2", target_bir_lowering=False, num_devices=1, dynamic_dma_scratch_size=1024)
    arrays, args = {}, []
    for name in _INS:
        a = np.ascontiguousarray(inputs[name])
        arrays[f"in_{name}"] = a
        args.append(nc.dram_tensor(f"in_{name}", a.shape, mybir.dt.from_np(a.dtype), kind="ExternalInput").ap())
    shape = inputs["x"].shape
    args.append(nc.dram_tensor("out_x", shape, F32, kind="ExternalOutput").ap())
    resid_stack_kernel(nc, *args)
    r = run_bass_kernel_spmd(nc, [arrays], core_ids=[0])
    return r.results[0]["out_x"]
```

```python
from contextlib import ExitStack
import math

import concourse.bass as bass
from concourse import mybir

F32 = mybir.dt.float32
F32R = mybir.dt.float32r
I32 = mybir.dt.int32
U32 = mybir.dt.uint32
ALU = mybir.AluOpType
ACT = mybir.ActivationFunctionType
AX_X = mybir.AxisListType.X

P = 128
BANK = 512
MAGIC = 12582912.0
LN2_HI, LN2_LO = 0.693145751953125, 1.42860682030941723e-6
TWO_PI = (6.28125, 0.0019350051879882812, 3.0199157663446e-07)
BIG = 3.0e38


def resid_stack_kernel(nc, x, lengths, languages, labels, codebook, log_dt, C_ri, log_A_real, A_imag, D_skip,
                       W1, Wr, A_lang, B_lang, W2, A_lab, B_lab, W3, scale_log, A3_lora, B3_lora, out):
    B, H, L = x.shape
    N = A_imag.shape[1]
    NC = L // P
    E, R, _ = A_lang.shape
    ER = E * R
    NL, _, RL = A_lab.shape
    LR = NL * RL
    R3 = A3_lora.shape[0]
    K_CODES = codebook.shape[0]
    HB = 2
    TILES = H // HB
    SPAN = 32
    LOWC = ER + E + LR
    C_H, C_LOG, C_LOW = L, L + ER, L + ER + E
    MW = L + LOWC
    EW = L + ER
    KP = P + L
    assert (B, N, ER, LR, HB * B, L // SPAN) == (64, 64, 128, 160, P, SPAN)
    MT = EW // P

    kpad = nc.dram_tensor("kpad", [H, 2, KP], F32, kind="Internal").ap()

    cursor = [(nc.sbuf_base + 31) // 32 * 32]

    def place(name, shape, dt, at=None):
        off = cursor[0] if at is None else at
        size = 4 * math.prod(shape[1:])
        t = nc.alloc_sbuf_tensor_at(name, shape, dt, offset=off)
        cursor[0] = off + (size + 31) // 32 * 32
        return t

    QUARTERS = 4
    QO = L // QUARTERS
    QT_TILES = QO // P
    QCOLS = QT_TILES * L
    ident = place("ident", [P, P], F32)
    iota = place("iota", [P, K_CODES], F32)
    mask = place("mask", [P, NC, B], I32)
    langbias = place("langbias", [P, E], F32)
    labsel = place("labsel", [P, NL], F32)
    region_m = cursor[0]
    Mh = place("Mh", [P, NC, MW], F32R)
    Ml = place("Ml", [P, NC, MW], F32R)
    R1h = place("R1h", [P, L], F32R)
    R1l = place("R1l", [P, L], F32R)
    R2s = place("R2s", [3 * RL, L], F32R)
    BLh = place("BLh", [P, LR], F32R)
    BLl = place("BLl", [P, LR], F32R)
    region_carry = cursor[0]
    QT = place("QT", [P, NC, EW], F32)
    LAp = place("LAp", [P, MT, LR], F32)
    Bw3 = place("Bw3", [P, NC, 3 * RL], F32)
    AT = place("AT", [P, NC, ER + E], F32)
    A3 = place("A3", [P, NC, QO], F32)
    m32 = place("m32", [P, 2, QO], F32)
    region_q = cursor[0]
    vq = place("vq", [P, QT_TILES, L], F32)
    dq = place("dq", [P, QT_TILES, L], F32)
    step_t = place("step_t", [P, 1024], F32)
    B3T = place("B3T", [R3, L], F32)
    A3l = place("A3l", [R3, L], F32)
    qq = [place(f"quant{q}", [P, QT_TILES, L], F32) for q in range(QUARTERS)]
    tau = place("tau", [P, K_CODES + 1], F32)
    cb = place("cb", [P, K_CODES], F32)
    steps = place("steps", [P, 2, K_CODES], F32)
    n_steps = place("n_steps", [1, 1], I32)
    tabs = place("tabs", [P, 4, H], F32)
    mrow = place("mrow", [P, SPAN], F32)
    Drow = place("Drow", [1, H], F32)
    half_pi = place("half_pi", [P, 1], F32)
    scale3 = place("scale3", [P, NC, NC], F32)
    inv_scale3 = place("inv_scale3", [P, NC, NC], F32)
    assert cursor[0] <= nc.sbuf_usable_end, cursor[0]
    E1 = place("E1", [P, NC, EW], F32, at=region_m)
    A2 = place("A2", [P, NC, L], F32)
    LA = place("LA", [P, NC, NL, RL], F32)
    W2s = place("W2s", [P, 2, L], F32)
    assert cursor[0] <= region_carry, (cursor[0], region_carry)
    HH = H // 2
    theta = place("theta", [P, HH, SPAN], F32, at=region_q)
    expo = place("expo", [P, HH, SPAN], F32)
    turns = place("turns", [P, HH, SPAN], F32)
    rem = place("rem", [P, HH, SPAN], F32)
    sin_half = place("sin_half", [P, HH, SPAN], F32)
    cos_half = place("cos_half", [P, HH, SPAN], F32)
    Ut = place("Ut", [P, H, SPAN], F32)
    Vt = place("Vt", [P, H, SPAN], F32)
    assert cursor[0] <= region_q + 4 * (4 * QCOLS + 1024 + 2 * L)
    Kf = place("Kf", [SPAN, H, SPAN], F32, at=region_q)
    Kh = place("Kh", [SPAN, H, SPAN], F32R)
    Kl = place("Kl", [SPAN, H, SPAN], F32R)
    nat = place("nat", [H, 16, N], F32, at=region_carry)
    logs = place("logs", [H, 1 + N], F32)
    exps = place("exps", [H, 1 + N], F32)
    c_in = place("c_in", [H, N, 2], F32)
    nat4 = place("nat4", [H, 4, 2 * N], F32)
    ex = place("ex", [P, 6, H + 1], F32)
    ex_bits = place("ex_bits", [P, H + 1], I32)
    B3n = place("B3n", [P, NC, R3], F32)
    A_nat = place("A_nat", [P, L], F32)
    Wr_nat = place("Wr_nat", [E, L], F32)
    BwIn = place("BwIn", [P, NC, RL], F32)
    len_i = place("len_i", [P, B], I32)
    len_f = place("len_f", [P, B], F32)
    ids_i = place("ids_i", [P, 2], I32)
    ids_f = place("ids_f", [P, 2], F32)
    lidx = place("lidx", [P, NC, B], F32)
    zpad = place("zpad", [H, 2, P], F32)
    cbw = place("cbw", [P, 4, K_CODES], F32)
    cbs = place("cbs", [P, 4], F32)
    codesT = place("codesT", [K_CODES, 3, P], F32)
    sel = place("sel", [K_CODES, K_CODES], F32)
    assert cursor[0] <= region_carry + 4 * NC * EW

    X = place("X", [P, L], F32, at=region_carry)
    Xr = place("Xr", [P, NC, P], F32)
    xT = place("xT", [P, NC, P], F32)
    xrh = place("xrh", [P, NC, P], F32R)
    xrl = place("xrl", [P, NC, P], F32R)
    toep = [place(f"toep{hh}", [P, 2, L], F32R) for hh in range(HB)]
    x0h = place("x0h", [P, NC, P], F32R)
    x0l = place("x0l", [P, NC, P], F32R)
    O = place("O", [P, L], F32)
    gsm = place("gsm", [P, 8, E], F32)
    gidx = place("gidx", [P, E], U32)
    hg = place("hg", [P, E, R], F32)
    hgTh = place("hgTh", [P, P], F32R)
    hgTl = place("hgTl", [P, P], F32R)
    lowm = place("lowm", [P, NL, RL], F32)
    low3 = place("low3", [P, 3, RL], F32)
    lowTs = place("lowTs", [3 * RL, P], F32R)
    assert cursor[0] <= nc.sbuf_usable_end

    with ExitStack() as ctx:
        bank = [ctx.enter_context(nc.psum_tensor(f"bank{n}", [P, BANK], F32)) for n in range(8)]

        def sem(name):
            return ctx.enter_context(nc.semaphore(name))

        ld_kgen, ld_codes, ld_ids, ld_d = sem("ld_kgen"), sem("ld_codes"), sem("ld_ids"), sem("ld_d")
        ld_b3, ld_rank, ld_w3, ld_w1, ld_blang, ld_la = (
            sem("ld_b3"), sem("ld_rank"), sem("ld_w3"), sem("ld_w1"), sem("ld_blang"), sem("ld_la"))
        ld_w2 = [sem("ld_w2a"), sem("ld_w2b")]
        kpad_stored = sem("kpad_stored")
        consts_ready, pool_step, bw_ready, e1_ready, a2_ready = (
            sem("consts_ready"), sem("pool_step"), sem("bw_ready"), sem("e1_ready"), sem("a2_ready"))
        dve_step, act_step, stage_full, stage_free = sem("dve_step"), sem("act_step"), sem("stage_full"), sem("stage_free")
        places_ready, sel_ready, early_done = sem("places_ready"), sem("sel_ready"), sem("early_done")
        nat_rem, nat_sin, nat4_ready = sem("nat_rem"), sem("nat_sin"), sem("nat4_ready")
        tab_rem, tab_sin, tab_ready = sem("tab_rem"), sem("tab_sin"), sem("tab_ready")
        kf_ready, kh_ready, kl_ready = sem("kf_ready"), sem("kh_ready"), sem("kl_ready")
        quant_init, quant_done = sem("quant_init"), sem("quant_done")
        qt_full, qt_free, a3_ready = sem("qt_full"), sem("qt_free"), sem("a3_ready")
        m_full, m_taken, m_lo, lowrank_hi, lowrank_lo = sem("m_full"), sem("m_taken"), sem("m_lo"), sem("lowrank_hi"), sem("lowrank_lo")
        passed = {e: sem(f"waits_passed_{e}") for e in ("dve", "pool")}

        def hold(eng, name):
            eng.sem_inc(passed[name], 1)

        def deltas(q):
            return [("delta", q, n) for n in range(2 * QT_TILES)]

        order = [("b3t", 0), ("b3t", 1)] + deltas(0)
        for ot in range(NC):
            order += [("w2t", ot, 0), ("w2t", ot, 1)]
            order += {1: [("codesT",)], 3: [("nat4",)], 5: [("codes",)]}.get(ot, [])
        order += [("at", 0), ("at", 1), ("wrt",)]
        for kt in range(NC):
            order += [("qt", kt)]
            order += {2: deltas(1), 5: deltas(2)}.get(kt, [])
        order += [("lap", mt) for mt in range(MT)] + deltas(3)
        for q in range(QUARTERS):
            order += [("a3", q, n) for n in range(4)]
            if q == QUARTERS - 1:
                order += [("kern", g) for g in range(4)]
            order += [("m", q, mt) for mt in range(MT + 1)]
        jobs = [j for j in order if j[0] not in ("qt", "m")]
        jobno = {j: n for n, j in enumerate(jobs)}
        mno = {j: n for n, j in enumerate(j for j in order if j[0] == "m")}

        def stage(j):
            return bank[jobno[j] % 2]

        def quarter_of(ot):
            return ot // QT_TILES, ot % QT_TILES

        def m_parts(q, mt):
            cols = slice(q * QO, (q + 1) * QO)
            if mt == MT:
                return slice(0, 3 * RL), R2s[:, cols], None
            if mt == NC:
                return slice(0, P), R1h[:, cols], R1l[:, cols]
            return slice(0, P), Mh[:, mt, cols], Ml[:, mt, cols]

        TABLES_AT = [(1, 8), (2, 1), (2, 4), (2, 7)]

        with nc.Block() as block:

            @block.sync
            def _(sp):
                sp.dma_start(cb[:, :], bass.AP(codebook.tensor, 0, [[0, P], [1, K_CODES]])).then_inc(ld_codes, 16)
                sp.dma_start(scale3[:, :, :], scale_log.rearrange("(t p) g a -> p t (g a)", p=P)).then_inc(ld_codes, 16)
                sp.dma_start(logs[:, 0:1], log_dt.rearrange("(h a) -> h a", a=1)).then_inc(ld_kgen, 16)
                sp.dma_start(logs[:, 1:1 + N], log_A_real).then_inc(ld_kgen, 16)
                sp.dma_start(nat[:, 0, :], A_imag).then_inc(ld_kgen, 16)
                sp.dma_start(c_in[:, :, :], C_ri).then_inc(ld_kgen, 16)
                sp.dma_start(B3n[:, :, :], B3_lora.rearrange("(t p) r -> p t r", p=P)).then_inc(ld_b3, 16)
                sp.dma_start(A3l[:, :], A3_lora).then_inc(ld_b3, 16)

                def load_quarter(q):
                    sp.dma_start(vq[:, :, :], W3[q * QO:(q + 1) * QO, :].rearrange("(t p) k -> p t k", p=P)).then_inc(ld_w3, 16)

                for ot in range(2):
                    sp.dma_start(W2s[:, ot, :], W2[ot * P:(ot + 1) * P, :]).then_inc(ld_w2[ot], 16)
                load_quarter(0)
                sp.dma_start(len_i[:, :], bass.AP(lengths.tensor, 0, [[0, P], [1, B]])).then_inc(ld_ids, 16)
                for hh in range(HB):
                    rows = slice(hh * B, (hh + 1) * B)
                    sp.dma_start(ids_i[rows, 0:1], languages.rearrange("(b a) -> b a", a=1)).then_inc(ld_ids, 16)
                    sp.dma_start(ids_i[rows, 1:2], labels.rearrange("(b a) -> b a", a=1)).then_inc(ld_ids, 16)
                sp.dma_start(Drow[:, :], D_skip.rearrange("(a h) -> a h", a=1)).then_inc(ld_d, 16)
                for ot in range(2, NC):
                    sp.wait_ge(stage_full, jobno[("w2t", ot - 2, 1)] + 1)
                    sp.dma_start(W2s[:, ot % 2, :], W2[ot * P:(ot + 1) * P, :]).then_inc(ld_w2[ot % 2], 16)
                    sp.dma_start(E1[:, ot - 2, 0:L], W1[(ot - 2) * P:(ot - 1) * P, :]).then_inc(ld_w1, 16)
                sp.dma_start(A_nat[:, :], A_lang.rearrange("e r d -> (e r) d")).then_inc(ld_rank, 16)
                sp.dma_start(Wr_nat[:, :], Wr).then_inc(ld_rank, 16)
                sp.dma_start(BwIn[:, :, :], B_lab.rearrange("(t p) r -> p t r", p=P)).then_inc(ld_rank, 16)
                for ot in range(NC - 2, NC):
                    sp.dma_start(E1[:, ot, 0:L], W1[ot * P:(ot + 1) * P, :]).then_inc(ld_w1, 16)
                for it in range(NC):
                    sp.dma_start(E1[:, it, L:EW].rearrange("p (e r) -> p e r", e=E),
                                 B_lang[:, it * P:(it + 1) * P, :].rearrange("e o r -> o e r")).then_inc(ld_blang, 16)
                sp.wait_ge(consts_ready, 1)
                sp.dma_start(kpad[:, :, 0:P], zpad[:, :, :]).then_inc(kpad_stored, 16)
                for it in range(NC):
                    sp.dma_start(LA[:, it, :, :], A_lab[:, it * P:(it + 1) * P, :].rearrange("l i r -> i l r")).then_inc(ld_la, 16)
                for q in range(1, QUARTERS):
                    sp.wait_ge(quant_done, q)
                    load_quarter(q)
                for part, t, ready in ((0, Kh, kh_ready), (1, Kl, kl_ready)):
                    sp.wait_ge(ready, 1)
                    sp.dma_start(bass.AP(kpad.tensor, part * KP + P, [[SPAN, SPAN], [2 * KP, H], [1, SPAN]]),
                                 t[:, :, :].bitcast(F32)).then_inc(kpad_stored, 16)
                sp.wait_ge(kpad_stored, 48)

            @block.gpsimd
            def _(pool):
                n_step = [0]

                def step(ins):
                    n_step[0] += 1
                    ins.then_inc(pool_step, 1)
                    pool.wait_ge(pool_step, n_step[0])

                step(pool.memset(ident[:, :], 0.0))
                pool.memset(half_pi[:, :], math.pi / 2)
                pool.memset(zpad[:, :, :], 0.0)
                for t, pattern, multiplier in ((mrow[:, :], [[1, SPAN]], 0), (iota[:, :], [[1, K_CODES]], 0),
                                               (lidx[:, :, :], [[P, NC], [0, B]], 1)):
                    pool.iota(t, pattern=pattern, base=0, channel_multiplier=multiplier, allow_small_or_imprecise_dtypes=True)
                pool.affine_select(out=ident[:, :], in_=ident[:, :], compare_op=ALU.not_equal, fill=1.0, base=0,
                                   pattern=[[-1, P]], channel_multiplier=1).then_inc(consts_ready, 1)
                pool.wait_ge(consts_ready, 1)
                pool.wait_ge(ld_rank, 48)
                for n in range(3):
                    pool.tensor_scalar(Bw3[:, :, n * RL:(n + 1) * RL], BwIn[:, :, :], 0.5, None, ALU.mult).then_inc(bw_ready, 1)
                for it in range(NC):
                    pool.wait_ge(stage_free, jobno[("w2t", it, it // 4)] + 1)
                    d = A2[:, it, it * P:(it + 1) * P]
                    pool.tensor_tensor(d, d, ident[:, :], ALU.add).then_inc(a2_ready, 1)
                pool.wait_ge(ld_w1, 16 * NC)
                for it in range(NC):
                    d = E1[:, it, it * P:(it + 1) * P]
                    pool.tensor_tensor(d, d, ident[:, :], ALU.add).then_inc(e1_ready, 1)
                pool.wait_ge(ld_blang, 16 * NC)
                pool.tensor_scalar(E1[:, :, L:EW], E1[:, :, L:EW], 2.0, None, ALU.mult).then_inc(e1_ready, 1)
                pool.wait_ge(lowrank_hi, 3)
                pool.tensor_tensor(Ml[:, :, C_H:C_LOW], AT[:, :, :], Mh[:, :, C_H:C_LOW].bitcast(F32), ALU.subtract)
                pool.tensor_tensor(Ml[:, :, C_LOW:MW], LAp[:, 0:NC, :], Mh[:, :, C_LOW:MW].bitcast(F32), ALU.subtract)
                pool.tensor_tensor(BLl[:, :], LAp[:, NC, :], BLh[:, :].bitcast(F32), ALU.subtract)
                for q in range(QUARTERS):
                    for t in range(QT_TILES):
                        kt = q * QT_TILES + t
                        if q:
                            pool.wait_ge(m_lo, mno[("m", q, 0)])
                        pool.wait_ge(stage_free, jobno[("a3", q, kt // 2)] + 1)
                        d = A3[:, kt, t * P:(t + 1) * P]
                        pool.tensor_tensor(d, d, ident[:, :], ALU.add).then_inc(a3_ready, 1)
                    for mt in range(MT + 1):
                        n = mno[("m", q, mt)]
                        pool.wait_ge(m_taken, n + 1)
                        rows, hi, lo = m_parts(q, mt)
                        if lo is None:
                            pool.wait_ge(m_lo, n)
                        if lo is None:
                            rows, lo = slice(2 * RL, 3 * RL), hi[2 * RL:3 * RL, :]
                            hi = lo
                        pool.tensor_tensor(lo, m32[rows, n % 2, :], hi.bitcast(F32), ALU.subtract).then_inc(m_lo, 1)

            @block.tensor
            def _(pe):
                pe.wait_ge(consts_ready, 1)

                def several(j, count, one):
                    if jobno[j] >= 2:
                        pe.wait_ge(stage_free, jobno[j] - 1)
                    for n in range(count):
                        last = one(stage(j), n)
                    last.then_inc(stage_full, 1)

                def b3t(g):
                    if g == 0:
                        pe.wait_ge(ld_b3, 32)
                    several(("b3t", g), 4, lambda ps, n: pe.transpose(ps[0:R3, n * P:(n + 1) * P], B3n[:, 4 * g + n, :], ident[:, :]))

                def delta(q, n):
                    t, half = n // 2, n % 2
                    if q == 0 and n == 0:
                        pe.wait_ge(stage_free, jobno[("b3t", 1)] + 1)
                    o = (q * QT_TILES + t) * P
                    several(("delta", q, n), 1, lambda ps, _: pe.matmul(ps[:, :], B3T[:, o:o + P], A3l[:, half * BANK:(half + 1) * BANK],
                                                                         start=True, stop=True))

                def w2t(ot, half):
                    if half == 0:
                        pe.wait_ge(ld_w2[ot % 2], 16 * (ot // 2 + 1))
                    several(("w2t", ot, half), 4, lambda ps, n: pe.transpose(
                        ps[:, n * P:(n + 1) * P], W2s[:, ot % 2, (4 * half + n) * P:(4 * half + n + 1) * P], ident[:, :]))

                def codes_t():
                    pe.wait_ge(places_ready, 1)
                    src = (cbw[:, 3, :], tau[:, 0:K_CODES], cb[:, :])
                    several(("codesT",), 3, lambda ps, n: pe.transpose(ps[0:K_CODES, n * P:(n + 1) * P], src[n], ident[:, :]))

                def codes():
                    pe.wait_ge(sel_ready, 1)
                    several(("codes",), 2, lambda ps, n: pe.matmul(ps[:, n * K_CODES:(n + 1) * K_CODES], codesT[:, 1 + n, :], sel[:, :],
                                                                    start=True, stop=True))

                def nat4_t():
                    pe.wait_ge(nat4_ready, 1)
                    several(("nat4",), 4, lambda ps, n: pe.transpose(ps[:, n * H:(n + 1) * H], nat4[:, n, :], ident[0:H, 0:H]))

                def at(g):
                    if g == 0:
                        pe.wait_ge(ld_rank, 48)
                    several(("at", g), 4, lambda ps, n: pe.transpose(
                        ps[:, n * P:(n + 1) * P], A_nat[:, (4 * g + n) * P:(4 * g + n + 1) * P], ident[:, :]))

                def wrt():
                    several(("wrt",), NC, lambda ps, c: pe.transpose(ps[:, c * E:(c + 1) * E], Wr_nat[:, c * P:(c + 1) * P], ident[0:E, 0:E]))

                def qt(kt):
                    if kt == 0:
                        pe.wait_ge(a2_ready, NC)
                        pe.wait_ge(e1_ready, NC + 1)
                    if kt >= 2:
                        pe.wait_ge(qt_free, kt - 1)
                    s = 2 + 3 * (kt % 2)
                    for n, (a, b) in enumerate(((0, BANK), (BANK, L), (L, EW))):
                        for it in range(NC):
                            last = pe.matmul(bank[s + n][:, 0:b - a], A2[:, it, kt * P:(kt + 1) * P], E1[:, it, a:b],
                                             start=(it == 0), stop=(it == NC - 1))
                    last.then_inc(qt_full, 1)

                def lap(mt):
                    if mt == 0:
                        pe.wait_ge(ld_la, 16 * NC)
                    several(("lap", mt), NC, lambda ps, it: pe.matmul(
                        ps[:, 0:LR], E1[:, it, mt * P:(mt + 1) * P], LA[:, it, :, :].rearrange("p l r -> p (l r)"),
                        start=(it == 0), stop=(it == NC - 1)))

                def a3(q, n):
                    if n == 0:
                        pe.wait_ge(quant_done, q + 1)
                    several(("a3", q, n), 2 * QT_TILES, lambda ps, m: pe.transpose(
                        ps[:, m * P:(m + 1) * P], qq[q][:, m % QT_TILES, (2 * n + m // QT_TILES) * P:(2 * n + m // QT_TILES + 1) * P], ident[:, :]))

                def kern(g):
                    if g == 0:
                        pe.wait_ge(tab_ready, 2)
                    several(("kern", g), 16, lambda ps, n: pe.matmul(ps[0:SPAN, n * SPAN:(n + 1) * SPAN], Ut[:, 16 * g + n, :], Vt[:, 16 * g + n, :],
                                                                      start=True, stop=True))

                def m(q, mt):
                    n = mno[("m", q, mt)]
                    if mt == 0:
                        pe.wait_ge(stage_free, jobno[("a3", q, 3)] + 1)
                        pe.wait_ge(a3_ready, QT_TILES * (q + 1))
                        if q == 0:
                            pe.wait_ge(qt_free, NC)
                            pe.wait_ge(bw_ready, 3)
                    if n >= 6:
                        pe.wait_ge(m_taken, n - 5)
                    rows = 3 * RL if mt == MT else P
                    for kt in range(NC):
                        lhs = Bw3[:, kt, :] if mt == MT else QT[:, kt, mt * P:(mt + 1) * P]
                        last = pe.matmul(bank[2 + n % 6][0:rows, 0:QO], lhs, A3[:, kt, :], start=(kt == 0), stop=(kt == NC - 1))
                    last.then_inc(m_full, 1)

                do = dict(b3t=b3t, delta=delta, w2t=w2t, codesT=codes_t, codes=codes, nat4=nat4_t, at=at, wrt=wrt, qt=qt, lap=lap,
                          a3=a3, kern=kern, m=m)
                for name, *which in order:
                    do[name](*which)

            @block.scalar
            def _(act):
                n_step = [0]

                def step(ins):
                    n_step[0] += 1
                    ins.then_inc(act_step, 1)
                    act.wait_ge(act_step, n_step[0])

                def take(j, out, in_, scale=1.0):
                    act.wait_ge(stage_full, jobno[j] + 1)
                    act.activation(out, in_, ACT.Copy, scale=scale).then_inc(stage_free, 1)

                def table(k):
                    act.wait_ge(tab_rem, k + 1)
                    step(act.activation(sin_half[:, :, :], rem[:, :, :], ACT.Sin, scale=0.5))
                    step(act.activation(turns[:, :, :], rem[:, :, :], ACT.Abs))
                    step(act.activation(cos_half[:, :, :], turns[:, :, :], ACT.Sin, bias=half_pi[:, 0:1], scale=-0.5))
                    act.activation(rem[:, :, :], expo[:, :, :], ACT.Exp, scale=(1.0, float(SPAN))[k % 2]).then_inc(tab_sin, 1)

                def nat_sine():
                    act.wait_ge(nat_rem, 1)
                    act.wait_ge(consts_ready, 1)
                    step(act.activation(nat[:, 4, :], nat[:, 3, :], ACT.Sin, scale=0.5))
                    step(act.activation(nat[:, 5, :], nat[:, 3, :], ACT.Abs))
                    act.activation(nat[:, 6, :], nat[:, 5, :], ACT.Sin, bias=half_pi[0:H, 0:1], scale=-0.5).then_inc(nat_sin, 1)

                def init_quarter(q):
                    act.activation(qq[q][:, :, :].rearrange("p t k -> p (t k)"), cb[:, 0:1].to_broadcast([P, QCOLS]), ACT.Copy).then_inc(quant_init, 1)

                for j in order:
                    name, *which = j
                    if name == "b3t":
                        take(j, B3T[:, which[0] * BANK:(which[0] + 1) * BANK], stage(j)[0:R3, :], scale=0.5)
                    elif name == "delta":
                        q, n = which
                        if n == 0 and q:
                            act.wait_ge(quant_done, q)
                        take(j, dq[:, n // 2, n % 2 * BANK:(n % 2 + 1) * BANK], stage(j)[:, :])
                    elif name == "w2t":
                        ot, half = which
                        take(j, A2[:, 4 * half:4 * half + 4, ot * P:(ot + 1) * P], stage(j)[:, :].rearrange("p (t k) -> p t k", t=4))
                        if j == ("w2t", 2, 1):
                            nat_sine()
                    elif name == "codesT":
                        take(j, codesT[:, :, :], stage(j)[0:K_CODES, 0:3 * P].rearrange("p (n k) -> p n k", n=3))
                        for q in range(QUARTERS):
                            init_quarter(q)
                    elif name == "codes":
                        take(j, steps[:, :, :], stage(j)[:, 0:2 * K_CODES].rearrange("p (n k) -> p n k", n=2))
                    elif name == "nat4":
                        take(j, tabs[:, :, :], stage(j)[:, 0:4 * H].rearrange("p (q h) -> p q h", q=4))
                    elif name == "at":
                        g = which[0]
                        take(j, AT[:, 4 * g:4 * g + 4, 0:ER], stage(j)[:, :].rearrange("p (c e) -> p c e", c=4))
                    elif name == "wrt":
                        take(j, AT[:, :, ER:ER + E], stage(j)[:, 0:NC * E].rearrange("p (c e) -> p c e", c=NC))
                    elif name == "qt":
                        kt = which[0]
                        if kt == 0:
                            act.wait_ge(bw_ready, 3)
                            act.wait_ge(kpad_stored, 16)
                            act.wait_ge(early_done, 1)
                        s = 2 + 3 * (kt % 2)
                        act.wait_ge(qt_full, kt + 1)
                        act.activation(QT[:, kt, 0:BANK], bank[s][:, :], ACT.Copy)
                        act.activation(QT[:, kt, BANK:L], bank[s + 1][:, :], ACT.Copy)
                        act.activation(QT[:, kt, L:EW], bank[s + 2][:, 0:ER], ACT.Copy).then_inc(qt_free, 1)
                    elif name == "lap":
                        mt = which[0]
                        take(j, LAp[:, mt, :], stage(j)[:, 0:LR])
                        if mt == MT - 1:
                            act.wait_ge(stage_free, jobno[j] + 1)
                            act.activation(Mh[:, :, C_H:C_LOW], AT[:, :, :], ACT.Copy).then_inc(lowrank_hi, 1)
                            act.activation(Mh[:, :, C_LOW:MW], LAp[:, 0:NC, :], ACT.Copy).then_inc(lowrank_hi, 1)
                            act.activation(BLh[:, :], LAp[:, NC, :], ACT.Copy).then_inc(lowrank_hi, 1)
                    elif name == "a3":
                        q, n = which
                        take(j, A3[:, 2 * n:2 * n + 2, :], stage(j)[:, :].rearrange("p (t o) -> p t o", t=2))
                    elif name == "kern":
                        g = which[0]
                        take(j, Kf[:, 16 * g:16 * g + 16, :], stage(j)[0:SPAN, :].rearrange("a (h b) -> a h b", h=16))
                    else:
                        q, mt = which
                        n = mno[j]
                        rows, hi, _ = m_parts(q, mt)
                        act.wait_ge(m_full, n + 1)
                        act.activation(hi, bank[2 + n % 6][rows, 0:QO], ACT.Copy)
                        if n >= 2:
                            act.wait_ge(m_lo, n - 1)
                        act.activation(m32[rows, n % 2, :], bank[2 + n % 6][rows, 0:QO], ACT.Copy).then_inc(m_taken, 1)
                        if (q, mt) in TABLES_AT:
                            table(TABLES_AT.index((q, mt)))
                        if (q, mt) == (QUARTERS - 1, 1):
                            act.wait_ge(kf_ready, 1)
                            act.activation(Kh[:, :, :], Kf[:, :, :], ACT.Copy).then_inc(kh_ready, 1)

            @block.vector
            def _(dve):
                n_step = [0]

                def step(ins):
                    n_step[0] += 1
                    ins.then_inc(dve_step, 1)
                    dve.wait_ge(dve_step, n_step[0])

                def exp_to(dst, src, rows, w):
                    t = [ex[0:rows, n, 0:w] for n in range(6)]
                    bits = ex_bits[0:rows, 0:w]
                    step(dve.tensor_scalar(t[0], src, -87.0, 88.0, ALU.max, ALU.min))
                    step(dve.tensor_scalar(t[1], t[0], 1.0 / math.log(2.0), MAGIC, ALU.mult, ALU.add))
                    step(dve.tensor_scalar(t[2], t[1], MAGIC, None, ALU.subtract))
                    step(dve.scalar_tensor_tensor(t[3], t[2], -LN2_HI, t[0], ALU.mult, ALU.add))
                    step(dve.scalar_tensor_tensor(t[4], t[2], -LN2_LO, t[3], ALU.mult, ALU.add))
                    step(dve.tensor_scalar(t[5], t[4], 1.0 / math.factorial(7), None, ALU.mult))
                    for n in range(6, 0, -1):
                        step(dve.scalar_tensor_tensor(t[5], t[5], 1.0 / math.factorial(n), t[4], ALU.add, ALU.mult))
                    step(dve.tensor_scalar(t[5], t[5], 1.0, None, ALU.add))
                    step(dve.tensor_scalar(bits, t[2], 127.0, float(1 << 23), ALU.add, ALU.mult))
                    step(dve.tensor_tensor(dst, t[5], bits.bitcast(F32), ALU.mult))

                def reduce_angle(dst, ang, tmp):
                    step(dve.tensor_scalar(tmp, ang, 1.0 / (2 * math.pi), MAGIC, ALU.mult, ALU.add))
                    step(dve.tensor_scalar(tmp, tmp, MAGIC, None, ALU.subtract))
                    step(dve.scalar_tensor_tensor(dst, tmp, -TWO_PI[0], ang, ALU.mult, ALU.add))
                    step(dve.scalar_tensor_tensor(dst, tmp, -TWO_PI[1], dst, ALU.mult, ALU.add))
                    return dve.scalar_tensor_tensor(dst, tmp, -TWO_PI[2], dst, ALU.mult, ALU.add)

                dve.wait_ge(ld_codes, 32)
                w0, w1, w2, places = (cbw[:, k, :] for k in range(4))
                step(dve.scalar_tensor_tensor(w0, cb[:, :], -1.0, cb[:, :], ALU.mult, ALU.max))
                step(dve.reduce_max(cbs[:, 1:2], w0, AX_X))
                step(dve.tensor_scalar(cbs[:, 0:1], cbs[:, 1:2], 1e-8, None, ALU.max))
                step(dve.reciprocal(cbs[:, 1:2], cbs[:, 0:1]))
                step(dve.tensor_scalar(cb[:, :], cb[:, :], cbs[:, 1:2], None, ALU.mult))
                step(dve.tensor_tensor(tau[:, 1:K_CODES], cb[:, 0:K_CODES - 1], cb[:, 1:K_CODES], ALU.add))
                step(dve.tensor_scalar(tau[:, 1:K_CODES], tau[:, 1:K_CODES], 0.5, None, ALU.mult))
                step(dve.memset(tau[:, 0:1], -BIG))
                step(dve.memset(tau[:, K_CODES:K_CODES + 1], BIG))
                s = K_CODES // 2
                while s >= 1:
                    mid, below, above = (tau[:, a:a + K_CODES - 2 * s + 1:2 * s] for a in (s, 0, 2 * s))
                    step(dve.tensor_tensor(mid, mid, below, ALU.max))
                    step(dve.tensor_tensor(mid, mid, above, ALU.min))
                    s //= 2
                step(dve.tensor_tensor(w0, tau[:, 1:K_CODES + 1], tau[:, 0:K_CODES], ALU.is_gt))
                step(dve.memset(w0[:, 0:1], 0.0))
                a, b = w0, w1
                s = 1
                while s < K_CODES:
                    step(dve.tensor_copy(b[:, 0:s], a[:, 0:s]))
                    step(dve.tensor_tensor(b[:, s:], a[:, s:], a[:, 0:K_CODES - s], ALU.add))
                    a, b = b, (w2 if b is w1 else w1)
                    s *= 2
                step(dve.tensor_tensor(places, a, w0, ALU.mult))
                step(dve.tensor_copy(n_steps[:, :], a[0:1, K_CODES - 1:K_CODES]))
                dve.tensor_scalar(places, places, 1.0, None, ALU.subtract).then_inc(places_ready, 1)
                flat = scale3[:, :, :].rearrange("p t g -> p (t g)")
                exp_to(flat, flat, P, NC * NC)
                step(dve.reciprocal(inv_scale3[:, :, :], scale3[:, :, :]))

                dve.wait_ge(ld_kgen, 64)
                exp_to(exps[:, :], logs[:, :], H, 1 + N)
                dt, eA, Aim = exps[:, 0:1], exps[:, 1:1 + N], nat[:, 0, :]
                step(dve.tensor_scalar(nat[:, 1, :], eA, dt, -1.0, ALU.mult, ALU.mult))
                step(dve.tensor_scalar(nat[:, 2, :], Aim, dt, None, ALU.mult))
                dtA_re, dtA_im = nat[:, 1, :], nat[:, 2, :]
                reduce_angle(nat[:, 3, :], dtA_im, nat[:, 7, :]).then_inc(nat_rem, 1)
                exp_to(nat[:, 8, :], dtA_re, H, N)
                dve.wait_ge(stage_free, jobno[("codesT",)] + 1)
                dve.wait_ge(consts_ready, 1)
                dve.tensor_scalar(sel[:, :], iota[0:K_CODES, :], codesT[:, 0, 0:1], None, ALU.is_equal).then_inc(sel_ready, 1)
                dve.wait_ge(nat_sin, 1)
                sh, ch, mag = nat[:, 4, :], nat[:, 6, :], nat[:, 8, :]
                step(dve.scalar_tensor_tensor(nat[:, 9, :], sh, -2.0, sh, ALU.mult, ALU.mult))
                step(dve.scalar_tensor_tensor(nat[:, 9, :], nat[:, 9, :], 1.0, mag, ALU.add, ALU.mult))
                step(dve.tensor_scalar(nat[:, 9, :], nat[:, 9, :], 1.0, None, ALU.subtract))
                step(dve.scalar_tensor_tensor(nat[:, 10, :], sh, 2.0, ch, ALU.mult, ALU.mult))
                step(dve.tensor_tensor(nat[:, 10, :], nat[:, 10, :], mag, ALU.mult))
                Er, Ei, Cr, Ci = nat[:, 9, :], nat[:, 10, :], c_in[:, :, 0], c_in[:, :, 1]
                num_r, num_i, t0, t1, t2 = (nat[:, k, :] for k in (11, 12, 13, 14, 15))
                step(dve.tensor_tensor(t0, Cr, Er, ALU.mult))
                step(dve.tensor_tensor(t1, Ci, Ei, ALU.mult))
                step(dve.tensor_tensor(num_r, t0, t1, ALU.subtract))
                step(dve.tensor_tensor(t0, Cr, Ei, ALU.mult))
                step(dve.tensor_tensor(t1, Ci, Er, ALU.mult))
                step(dve.tensor_tensor(num_i, t0, t1, ALU.add))
                step(dve.tensor_tensor(t0, eA, eA, ALU.mult))
                step(dve.tensor_tensor(t1, Aim, Aim, ALU.mult))
                step(dve.tensor_tensor(t0, t0, t1, ALU.add))
                step(dve.reciprocal(t2, t0))
                step(dve.tensor_tensor(t0, num_i, Aim, ALU.mult))
                step(dve.tensor_tensor(t1, num_r, eA, ALU.mult))
                step(dve.tensor_tensor(t0, t0, t1, ALU.subtract))
                step(dve.scalar_tensor_tensor(nat4[:, 2, 0:N], t0, 2.0, t2, ALU.mult, ALU.mult))
                step(dve.scalar_tensor_tensor(nat4[:, 2, N:2 * N], t0, -2.0, t2, ALU.mult, ALU.mult))
                step(dve.tensor_tensor(t0, num_r, Aim, ALU.mult))
                step(dve.tensor_tensor(t1, num_i, eA, ALU.mult))
                step(dve.tensor_tensor(t0, t0, t1, ALU.add))
                for s in range(2):
                    cols = slice(s * N, (s + 1) * N)
                    step(dve.scalar_tensor_tensor(nat4[:, 3, cols], t0, 2.0, t2, ALU.mult, ALU.mult))
                    step(dve.tensor_copy(nat4[:, 0, cols], dtA_re))
                    last = dve.tensor_copy(nat4[:, 1, cols], dtA_im)
                    if s == 0:
                        step(last)
                last.then_inc(nat4_ready, 1)

                dve.wait_ge(ld_ids, 80)
                step(dve.tensor_copy(len_f[:, :], len_i[:, :]))
                step(dve.tensor_tensor(mask[:, :, :], lidx[:, :, :], len_f[:, :].unsqueeze(1).broadcast_to([P, NC, B]), ALU.is_lt))
                step(dve.tensor_copy(ids_f[:, :], ids_i[:, :]))
                step(dve.tensor_scalar(langbias[:, :], iota[:, 0:E], ids_f[:, 0:1], 5.0, ALU.is_equal, ALU.mult))
                dve.tensor_scalar(labsel[:, :], iota[:, 0:NL], ids_f[:, 1:2], None, ALU.is_equal).then_inc(early_done, 1)

                dve.wait_ge(stage_free, jobno[("codes",)] + 1)
                kept_tau, kept_code = steps[:, 0, :], steps[:, 1, :]
                held = step_t[:, 0:K_CODES]
                step(dve.tensor_copy(held[:, 0:1], cb[:, 0:1]))
                step(dve.tensor_copy(held[:, 1:K_CODES], kept_code[:, 0:K_CODES - 1]))
                step(dve.tensor_tensor(kept_code, kept_code, held, ALU.subtract))
                rise = kept_code

                n_kept = dve.value_load(n_steps[0:1, 0:1], min_val=0, max_val=K_CODES - 1)
                CH = step_t.shape[1]
                n_ch = QCOLS // CH
                GROUP = 7
                assert (K_CODES - 1) % GROUP == 0
                per = 2 * n_ch
                groups = QT_TILES * NC
                for q in range(QUARTERS):
                    tiles = slice(q * QT_TILES, (q + 1) * QT_TILES)
                    vf, df, qf = (t[:, :, :].rearrange("p t k -> p (t k)") for t in (vq, dq, qq[q]))
                    vg, qg = (t[:, :, :].rearrange("p t (g k) -> p (t g) k", g=NC) for t in (vq, qq[q]))
                    inv_g, scale_g = (t[:, tiles, :].rearrange("p t g -> p (t g)").unsqueeze(2).broadcast_to([P, groups, P])
                                      for t in (inv_scale3, scale3))
                    dve.wait_ge(ld_w3, 16 * (q + 1))
                    dve.wait_ge(stage_free, jobno[("delta", q, 2 * QT_TILES - 1)] + 1)
                    step(dve.tensor_tensor(vf, vf, df, ALU.add))
                    step(dve.tensor_tensor(vg, vg, inv_g, ALU.mult))
                    dve.wait_ge(quant_init, q + 1)
                    base = n_step[0]
                    with dve.Fori(0, (K_CODES - 1) // GROUP) as g:
                        with dve.If(n_kept > g * GROUP):
                            with dve.Fori(0, GROUP) as kk:
                                k = g * GROUP + kk
                                at = base + k * per
                                with dve.If(n_kept > k):
                                    for c in range(n_ch):
                                        cols = slice(c * CH, (c + 1) * CH)
                                        dve.tensor_scalar(step_t[:, :], vf[:, cols], kept_tau[:, bass.ds(k, 1)], rise[:, bass.ds(k, 1)],
                                                          ALU.is_gt, ALU.mult).then_inc(dve_step, 1)
                                        dve.wait_ge(dve_step, at + 2 * c + 1)
                                        dve.tensor_tensor(qf[:, cols], qf[:, cols], step_t[:, :], ALU.add).then_inc(dve_step, 1)
                                        dve.wait_ge(dve_step, at + 2 * c + 2)
                                    hold(dve, "dve")
                                with dve.Else():
                                    dve.sem_inc(dve_step, per)
                        with dve.Else():
                            dve.sem_inc(dve_step, per * GROUP)
                    n_step[0] = base + per * (K_CODES - 1)
                    step(dve.tensor_tensor(qf, qf, vf, ALU.subtract))
                    step(dve.tensor_tensor(qf, qf, vf, ALU.add))
                    step(dve.tensor_tensor(qg, qg, scale_g, ALU.mult))
                    dve.tensor_tensor(qf, qf, df, ALU.add).then_inc(quant_done, 1)

                dve.wait_ge(quant_done, QUARTERS)
                dve.wait_ge(stage_full, jobno[("a3", 1, 3)] + 1)
                tb = [P, HH, SPAN]
                lo, hi = slice(0, N), slice(N, 2 * N)
                for half in range(2):
                    rows = slice(half * HH, (half + 1) * HH)
                    q = [tabs[:, k, rows].unsqueeze(2).broadcast_to(tb) for k in range(4)]
                    m = mrow[:, :].unsqueeze(1).broadcast_to(tb)
                    step(dve.tensor_tensor(theta[:, :, :], q[1], m, ALU.mult))
                    step(dve.tensor_tensor(expo[:, :, :], q[0], m, ALU.mult))
                    reduce_angle(rem[:, :, :], theta[:, :, :], turns[:, :, :]).then_inc(tab_rem, 1)
                    dve.wait_ge(tab_sin, 2 * half + 1)
                    step(dve.scalar_tensor_tensor(turns[lo, :, :], sin_half[lo, :, :], -2.0, sin_half[lo, :, :], ALU.mult, ALU.mult))
                    step(dve.tensor_scalar(turns[lo, :, :], turns[lo, :, :], 1.0, None, ALU.add))
                    step(dve.scalar_tensor_tensor(turns[hi, :, :], sin_half[hi, :, :], 2.0, cos_half[hi, :, :], ALU.mult, ALU.mult))
                    step(dve.tensor_tensor(Vt[:, rows, :], turns[:, :, :], rem[:, :, :], ALU.mult))
                    step(dve.tensor_scalar(theta[:, :, :], theta[:, :, :], float(SPAN), None, ALU.mult))
                    reduce_angle(rem[:, :, :], theta[:, :, :], turns[:, :, :]).then_inc(tab_rem, 1)
                    dve.wait_ge(tab_sin, 2 * half + 2)
                    sine, cosine = cos_half, sin_half
                    step(dve.scalar_tensor_tensor(sine[:, :, :], sin_half[:, :, :], 2.0, cos_half[:, :, :], ALU.mult, ALU.mult))
                    step(dve.scalar_tensor_tensor(cosine[:, :, :], sin_half[:, :, :], -2.0, sin_half[:, :, :], ALU.mult, ALU.mult))
                    step(dve.tensor_scalar(cosine[:, :, :], cosine[:, :, :], 1.0, None, ALU.add))
                    for part, first, second in ((lo, cosine, sine), (hi, sine, cosine)):
                        step(dve.tensor_tensor(turns[part, :, :], first[part, :, :], q[2][part, :, :], ALU.mult))
                        step(dve.tensor_tensor(theta[part, :, :], second[part, :, :], q[3][part, :, :], ALU.mult))
                    step(dve.tensor_tensor(turns[:, :, :], turns[:, :, :], theta[:, :, :], ALU.add))
                    dve.tensor_tensor(Ut[:, rows, :], turns[:, :, :], rem[:, :, :], ALU.mult).then_inc(tab_ready, 1)
                    dve.wait_ge(tab_ready, half + 1)

                dve.wait_ge(stage_free, jobno[("kern", 3)] + 1)
                dve.wait_ge(ld_d, 16)
                dve.scalar_tensor_tensor(Kf[0:1, :, 0], Kf[0:1, :, 0], 1.0, Drow[:, :], ALU.add, ALU.add).then_inc(kf_ready, 1)
                dve.wait_ge(kh_ready, 1)
                dve.tensor_tensor(Kl[:, :, :], Kf[:, :, :], Kh[:, :, :].bitcast(F32), ALU.subtract).then_inc(kl_ready, 1)

        x_loaded, xr_copied, out_stored = sem("x_loaded"), sem("xr_copied"), sem("out_stored")
        toep_loaded = [sem("toep0_loaded"), sem("toep1_loaded")]
        xrev_ready, xrh_done, xrl_done = sem("xrev_ready"), sem("xrh_done"), sem("xrl_done")
        xnat_ready, xT_done = sem("xnat_ready"), sem("xT_done")
        conv_done, x0_done, x0h_done, x0l_done = sem("conv_done"), sem("x0_done"), sem("x0h_done"), sem("x0l_done")
        lr_done, gap_done, gexp_done, hg_done = sem("lr_done"), sem("gap_done"), sem("gexp_done"), sem("hg_done")
        hgT_ready, hgTh_done, hgTl_done = sem("hgT_ready"), sem("hgTh_done"), sem("hgTl_done")
        low_done, low3_done, lowT_ready, lowTh_done, lowTl_done = (
            sem("low_done"), sem("low3_done"), sem("lowT_ready"), sem("lowTh_done"), sem("lowTl_done"))
        out_full, out_taken, gate_step, gate_low = sem("out_full"), sem("out_taken"), sem("gate_step"), sem("gate_low")
        psX, psY, psO, psL, psT = bank[0:2], bank[2:4], bank[4:6], bank[6], bank[7]
        LAST = TILES - 1

        with nc.Block() as block:

            @block.sync
            def _(sp):
                def load_x(i):
                    for hh in range(HB):
                        sp.dma_start(X[hh * B:(hh + 1) * B, :],
                                     bass.AP(x.tensor, (HB * i + hh) * L, [[H * L, B], [1, L]])).then_inc(x_loaded, 16)

                def load_toep(i, hh):
                    src = bass.AP(kpad.tensor, (HB * i + hh) * 2 * KP + 1, [[1, P], [KP, 2], [1, L]])
                    sp.dma_start(toep[hh][:, :, :].bitcast(F32), src).then_inc(toep_loaded[hh], 16)

                def store(i):
                    for hh in range(HB):
                        sp.dma_start(bass.AP(out.tensor, (HB * i + hh) * L, [[H * L, B], [1, L]]),
                                     O[hh * B:(hh + 1) * B, :]).then_inc(out_stored, 16)

                def tile(i, more):
                    if more:
                        sp.wait_ge(xnat_ready, HB * i + 2 * HB)
                        load_x(i + 2)
                        for hh in range(HB):
                            sp.wait_ge(conv_done, HB * i + HB + hh + 1)
                            load_toep(i + 2, hh)
                    sp.wait_ge(out_taken, 2 * i + 3)
                    store(i)

                load_x(0)
                for hh in range(HB):
                    load_toep(0, hh)
                sp.wait_ge(xnat_ready, HB)
                load_x(1)
                for hh in range(HB):
                    sp.wait_ge(conv_done, hh + 1)
                    load_toep(1, hh)
                with sp.Fori(0, TILES - 2) as i:
                    tile(i, True)
                for i in range(TILES - 2, TILES):
                    tile(i, False)
                sp.wait_ge(out_stored, 32 * TILES)

            @block.gpsimd
            def _(pool):
                def reverse(i, first=False):
                    if not first:
                        pool.wait_ge(xrev_ready, HB * i)
                        hold(pool, "pool")
                    pool.wait_ge(x_loaded, 32 * i + 32)
                    hold(pool, "pool")
                    pool.tensor_copy(Xr[:, :, :], X[:, :].rearrange("p (c l) -> p c l", c=NC)[:, :, ::-1]).then_inc(xr_copied, 1)

                reverse(0, first=True)
                with pool.Fori(1, TILES) as i:
                    reverse(i)

            @block.tensor
            def _(pe):
                def reversed_in(i, first=False):
                    pe.wait_ge(xr_copied, i + 1)
                    if not first:
                        pe.wait_ge(xT_done, HB * i)
                    for c in range(NC):
                        last = pe.transpose(psX[c // 4][:, c % 4 * P:(c % 4 + 1) * P], Xr[:, c, :], ident[:, :])
                        if c % 4 == 3:
                            last.then_inc(xrev_ready, 1)

                def natural_in(i):
                    for g in range(2):
                        pe.wait_ge(xrl_done, 2 * i + g + 1)
                        for c in range(4 * g, 4 * g + 4):
                            last = pe.transpose(psX[g][:, c % 4 * P:(c % 4 + 1) * P], X[:, c * P:(c + 1) * P], ident[:, :])
                        last.then_inc(xnat_ready, 1)

                def conv(i, hh):
                    pe.wait_ge(toep_loaded[hh], 16 * i + 16)
                    for d in range(NC):
                        cols = slice(d * P, (d + 1) * P)
                        for n, (part, xr) in enumerate(((0, xrh), (0, xrl), (1, xrh))):
                            last = pe.matmul(psY[hh][:, d * B:NC * B].rearrange("p (c b) -> p c b", b=B), toep[hh][:, part, cols],
                                             xr[:, 0:NC - d, hh * B:(hh + 1) * B],
                                             start=(d == 0 and n == 0), stop=(d == NC - 1 and n == 2))
                    last.then_inc(conv_done, 1)

                def low_in(i):
                    pe.wait_ge(x0l_done, HB * i + HB)
                    for c in range(NC):
                        for n, (xs, ms) in enumerate(((x0h, Mh), (x0h, Ml), (x0l, Mh))):
                            last = pe.matmul(psL[:, 0:LOWC], xs[:, c, :], ms[:, c, L:MW], start=(c == 0 and n == 0), stop=False,
                                             skip_group_check=True)
                    last.then_inc(lr_done, 1)

                def main(i):
                    pe.wait_ge(out_taken, 2 * i + 1)
                    for c in range(NC):
                        for n, (xs, ms) in enumerate(((x0h, Mh), (x0h, Ml), (x0l, Mh))):
                            for nh in range(2):
                                pe.matmul(psO[nh][:, :], xs[:, c, :], ms[:, c, nh * BANK:(nh + 1) * BANK],
                                          start=(c == 0 and n == 0), stop=False)

                def gated_transpose(i):
                    pe.wait_ge(hg_done, i + 1)
                    pe.transpose(psT[:, 0:P], hg[:, :, :].rearrange("p e r -> p (e r)"), ident[:, :]).then_inc(hgT_ready, 1)

                def low_gated(i):
                    pe.wait_ge(hgTl_done, i + 1)
                    for n, (a, b) in enumerate(((hgTh, BLh), (hgTh, BLl), (hgTl, BLh))):
                        last = pe.matmul(psL[:, ER + E:LOWC], a[:, :], b[:, :], start=False, stop=(n == 2), skip_group_check=True)
                    last.then_inc(low_done, 1)

                def low_transpose(i):
                    pe.wait_ge(low3_done, i + 1)
                    pe.transpose(psT[0:3 * RL, P:2 * P], low3[:, :, :].rearrange("p n r -> p (n r)"), ident[:, :]).then_inc(lowT_ready, 1)

                def gated_out(i):
                    for a, b in ((hgTh, R1h), (hgTh, R1l), (hgTl, R1h)):
                        for nh in range(2):
                            pe.matmul(psO[nh][:, :], a[:, :], b[:, nh * BANK:(nh + 1) * BANK], start=False, stop=False)

                def low_out(i):
                    pe.wait_ge(lowTl_done, i + 1)
                    for nh in range(2):
                        last = pe.matmul(psO[nh][:, :], lowTs[:, :], R2s[:, nh * BANK:(nh + 1) * BANK], start=False, stop=True)
                    last.then_inc(out_full, 1)

                def tile(i, more):
                    if more:
                        reversed_in(i + 1)
                    low_in(i)
                    if more:
                        natural_in(i + 1)
                    main(i)
                    gated_transpose(i)
                    if more:
                        conv(i + 1, 0)
                    low_gated(i)
                    if more:
                        conv(i + 1, 1)
                    low_transpose(i)
                    gated_out(i)
                    low_out(i)

                reversed_in(0, first=True)
                natural_in(0)
                conv(0, 0)
                conv(0, 1)
                with pe.Fori(0, LAST) as i:
                    tile(i, True)
                tile(LAST, False)

            @block.scalar
            def _(act):
                def reversed_hi(i):
                    for g in range(2):
                        act.wait_ge(xrev_ready, 2 * i + g + 1)
                        act.activation(xrh[:, 4 * g:4 * g + 4, :].rearrange("p c b -> p (c b)"), psX[g][:, :], ACT.Copy).then_inc(xrh_done, 1)

                def natural(i):
                    for g in range(2):
                        act.wait_ge(xnat_ready, 2 * i + g + 1)
                        act.activation(xT[:, 4 * g:4 * g + 4, :].rearrange("p c b -> p (c b)"), psX[g][:, :], ACT.Copy).then_inc(xT_done, 1)

                def x0_hi(i, hh):
                    act.wait_ge(x0_done, HB * i + hh + 1)
                    cols = slice(hh * B, (hh + 1) * B)
                    act.activation(x0h[:, :, cols], xT[:, :, cols], ACT.Copy).then_inc(x0h_done, 1)

                def gate_exp(i):
                    act.wait_ge(gap_done, i + 1)
                    act.activation(gsm[:, 3, 0:1], gsm[:, 2, 0:1], ACT.Exp).then_inc(gexp_done, 1)

                def gated_hi(i):
                    act.wait_ge(hgT_ready, i + 1)
                    act.activation(hgTh[:, :], psT[:, 0:P], ACT.Copy).then_inc(hgTh_done, 1)

                def low_hi(i):
                    act.wait_ge(lowT_ready, i + 1)
                    act.activation(lowTs[:, :], psT[0:3 * RL, P:2 * P], ACT.Copy).then_inc(lowTh_done, 1)

                def take_out(i, first=False):
                    act.wait_ge(out_full, i + 1)
                    if not first:
                        act.wait_ge(out_stored, 32 * i)
                    for nh in range(2):
                        act.activation(O[:, nh * BANK:(nh + 1) * BANK], psO[nh][:, :], ACT.Copy).then_inc(out_taken, 1)

                def tile(i, more, first=False):
                    if more:
                        reversed_hi(i + 1)
                    gate_exp(i)
                    if more:
                        natural(i + 1)
                    gated_hi(i)
                    if more:
                        x0_hi(i + 1, 0)
                    low_hi(i)
                    if more:
                        x0_hi(i + 1, 1)
                    take_out(i, first)

                act.sem_inc(out_taken, 1)
                reversed_hi(0)
                natural(0)
                x0_hi(0, 0)
                x0_hi(0, 1)
                tile(0, True, first=True)
                with act.Fori(1, LAST) as i:
                    tile(i, True)
                tile(LAST, False)

            @block.vector
            def _(dve):
                def reversed_lo(i):
                    for g in range(2):
                        dve.wait_ge(xrh_done, 2 * i + g + 1)
                        t = [v[:, 4 * g:4 * g + 4, :].rearrange("p c b -> p (c b)") for v in (xrl, xrh)]
                        dve.tensor_tensor(t[0], psX[g][:, :], t[1].bitcast(F32), ALU.subtract).then_inc(xrl_done, 1)

                def select(i, hh):
                    dve.wait_ge(xT_done, 2 * i + 2)
                    dve.wait_ge(conv_done, HB * i + hh + 1)
                    hold(dve, "dve")
                    dve.copy_predicated(xT[:, :, hh * B:(hh + 1) * B], mask[:, :, :],
                                        psY[hh][:, :].rearrange("p (c b) -> p c b", b=B)).then_inc(x0_done, 1)

                def x0_lo(i, hh):
                    dve.wait_ge(x0h_done, HB * i + hh + 1)
                    cols = slice(hh * B, (hh + 1) * B)
                    dve.tensor_tensor(x0l[:, :, cols], xT[:, :, cols], x0h[:, :, cols].bitcast(F32), ALU.subtract).then_inc(x0l_done, 1)

                GATE_STEPS = 10

                def gate(i):
                    done = [0]

                    def step(ins):
                        done[0] += 1
                        ins.then_inc(gate_step, 1)
                        dve.wait_ge(gate_step, GATE_STEPS * i + done[0])

                    logit, top, gap, e, g0, g1, g = (gsm[:, k, :] for k in range(7))
                    w = gsm[:, 7, :]
                    dve.wait_ge(lr_done, i + 1)
                    step(dve.tensor_tensor(logit, psL[:, ER:ER + E], langbias[:, :], ALU.add))
                    hold(dve, "dve")
                    step(dve.max(top, logit))
                    dve.tensor_tensor(gap[:, 0:1], top[:, 1:2], top[:, 0:1], ALU.subtract).then_inc(gap_done, 1)
                    step(dve.max_index(gidx[:, :], top, logit))
                    step(dve.tensor_copy(top[:, 0:2], gidx[:, 0:2]))
                    dve.wait_ge(gexp_done, i + 1)
                    step(dve.tensor_scalar(w[:, 2:3], e[:, 0:1], 1.0, None, ALU.add))
                    step(dve.reciprocal(w[:, 0:1], w[:, 2:3]))
                    step(dve.tensor_tensor(w[:, 1:2], e[:, 0:1], w[:, 0:1], ALU.mult))
                    step(dve.tensor_scalar(g0, iota[:, 0:E], top[:, 0:1], w[:, 0:1], ALU.is_equal, ALU.mult))
                    step(dve.tensor_scalar(g1, iota[:, 0:E], top[:, 1:2], w[:, 1:2], ALU.is_equal, ALU.mult))
                    step(dve.tensor_tensor(g, g0, g1, ALU.add))
                    assert done[0] == GATE_STEPS
                    dve.tensor_tensor(hg[:, :, :], psL[:, 0:ER].rearrange("p (e r) -> p e r", e=E),
                                      g.unsqueeze(2).broadcast_to([P, E, R]), ALU.mult).then_inc(hg_done, 1)

                def gated_lo(i):
                    dve.wait_ge(hgTh_done, i + 1)
                    dve.tensor_tensor(hgTl[:, :], psT[:, 0:P], hgTh[:, :].bitcast(F32), ALU.subtract).then_inc(hgTl_done, 1)

                def low_select(i):
                    dve.wait_ge(low_done, i + 1)
                    dve.tensor_tensor(lowm[:, :, :], psL[:, ER + E:LOWC].rearrange("p (l r) -> p l r", l=NL),
                                      labsel[:, :].unsqueeze(2).broadcast_to([P, NL, RL]), ALU.mult).then_inc(gate_low, 1)
                    dve.wait_ge(gate_low, 2 * i + 1)
                    dve.tensor_reduce(low3[:, 0, :], lowm[:, :, :].rearrange("p l r -> p r l"), AX_X, ALU.add).then_inc(gate_low, 1)
                    dve.wait_ge(gate_low, 2 * i + 2)
                    dve.tensor_copy(low3[:, 1:3, :], low3[:, 0:1, :].broadcast_to([P, 2, RL])).then_inc(low3_done, 1)

                def low_lo(i):
                    dve.wait_ge(lowTh_done, i + 1)
                    part = lowTs[RL:2 * RL, :]
                    dve.tensor_tensor(part, psT[RL:2 * RL, P:2 * P], part.bitcast(F32), ALU.subtract).then_inc(lowTl_done, 1)

                def tile(i, more):
                    if more:
                        reversed_lo(i + 1)
                    gate(i)
                    gated_lo(i)
                    if more:
                        select(i + 1, 0)
                        x0_lo(i + 1, 0)
                    low_select(i)
                    if more:
                        select(i + 1, 1)
                    low_lo(i)
                    if more:
                        x0_lo(i + 1, 1)

                reversed_lo(0)
                for hh in range(HB):
                    select(0, hh)
                    x0_lo(0, hh)
                with dve.Fori(0, LAST) as i:
                    tile(i, True)
                tile(LAST, False)


_INS = ["x", "itok_B_8_3872", "itok_B_0_7", "itok_B_0_2", "condB_codebook", "L0_cond_log_dt", "L0_cond_C",
        "L0_cond_log_A_real", "L0_cond_A_imag", "L0_cond_D", "L1_cond_W", "L1_cond_Wr", "L1_cond_A", "L1_cond_B",
        "L2_cond_W", "L2_cond_lora_A", "L2_cond_lora_B_w", "L3_cond_weight", "L3_cond_scale_log", "L3_cond_lora_A",
        "L3_cond_lora_B"]


def kernel(**inputs):
    import numpy as np
    import concourse.bacc as bacc
    from concourse.bass_utils import run_bass_kernel_spmd

    nc = bacc.Bacc("TRN2", target_bir_lowering=False, num_devices=1, dynamic_dma_scratch_size=1024)
    arrays, args = {}, []
    for name in _INS:
        a = np.ascontiguousarray(inputs[name])
        arrays[f"in_{name}"] = a
        args.append(nc.dram_tensor(f"in_{name}", a.shape, mybir.dt.from_np(a.dtype), kind="ExternalInput").ap())
    shape = inputs["x"].shape
    args.append(nc.dram_tensor("out_x", shape, F32, kind="ExternalOutput").ap())
    resid_stack_kernel(nc, *args)
    r = run_bass_kernel_spmd(nc, [arrays], core_ids=[0])
    return r.results[0]["out_x"]
```

```python
from contextlib import ExitStack
import math

import concourse.bass as bass
from concourse import mybir

F32 = mybir.dt.float32
F32R = mybir.dt.float32r
I32 = mybir.dt.int32
U32 = mybir.dt.uint32
ALU = mybir.AluOpType
ACT = mybir.ActivationFunctionType
AX_X = mybir.AxisListType.X

P = 128
BANK = 512
MAGIC = 12582912.0
LN2_HI, LN2_LO = 0.693145751953125, 1.42860682030941723e-6
TWO_PI = (6.28125, 0.0019350051879882812, 3.0199157663446e-07)
BIG = 3.0e38


def resid_stack_kernel(nc, x, lengths, languages, labels, codebook, log_dt, C_ri, log_A_real, A_imag, D_skip,
                       W1, Wr, A_lang, B_lang, W2, A_lab, B_lab, W3, scale_log, A3_lora, B3_lora, out):
    B, H, L = x.shape
    N = A_imag.shape[1]
    NC = L // P
    E, R, _ = A_lang.shape
    ER = E * R
    NL, _, RL = A_lab.shape
    LR = NL * RL
    R3 = A3_lora.shape[0]
    K_CODES = codebook.shape[0]
    HB = 2
    TILES = H // HB
    SPAN = 32
    LOWC = ER + E + LR
    C_H, C_LOG, C_LOW = L, L + ER, L + ER + E
    MW = L + LOWC
    EW = L + ER
    KP = P + L
    assert (B, N, ER, LR, HB * B, L // SPAN) == (64, 64, 128, 160, P, SPAN)
    MT = EW // P

    kpad = nc.dram_tensor("kpad", [H, 2, KP], F32, kind="Internal").ap()

    cursor = [(nc.sbuf_base + 31) // 32 * 32]

    def place(name, shape, dt, at=None):
        off = cursor[0] if at is None else at
        size = 4 * math.prod(shape[1:])
        t = nc.alloc_sbuf_tensor_at(name, shape, dt, offset=off)
        cursor[0] = off + (size + 31) // 32 * 32
        return t

    QUARTERS = 4
    QO = L // QUARTERS
    QT_TILES = QO // P
    QCOLS = QT_TILES * L
    ident = place("ident", [P, P], F32)
    iota = place("iota", [P, K_CODES], F32)
    mask = place("mask", [P, NC, B], I32)
    langbias = place("langbias", [P, E], F32)
    labsel = place("labsel", [P, NL], F32)
    region_m = cursor[0]
    Mh = place("Mh", [P, NC, MW], F32R)
    Ml = place("Ml", [P, NC, MW], F32R)
    R1h = place("R1h", [P, L], F32R)
    R1l = place("R1l", [P, L], F32R)
    R2s = place("R2s", [3 * RL, L], F32R)
    BLh = place("BLh", [P, LR], F32R)
    BLl = place("BLl", [P, LR], F32R)
    region_carry = cursor[0]
    QT = place("QT", [P, NC, EW], F32)
    region_lowrank = cursor[0]
    LAp = place("LAp", [P, MT, LR], F32)
    AT = place("AT", [P, NC, ER + E], F32)
    after_lowrank = region_lowrank + 4 * (NC * QO + 2 * QO)
    assert cursor[0] <= after_lowrank
    cursor[0] = after_lowrank
    Bw3 = place("Bw3", [P, NC, 3 * RL], F32)
    A3 = [place("A3a", [P, NC, QO], F32)]
    region_q = cursor[0]
    vq = place("vq", [P, QT_TILES, L], F32)
    dq = [place(f"dq{n}", [P, QT_TILES, L], F32) for n in range(2)]
    step_t = place("step_t", [P, 2, 1024], F32)
    qq = [place(f"quant{q}", [P, QT_TILES, L], F32) for q in range(QUARTERS)]
    tau = place("tau", [P, K_CODES + 1], F32)
    cb = place("cb", [P, K_CODES], F32)
    steps = place("steps", [P, 2, K_CODES], F32)
    n_steps = place("n_steps", [1, 1], I32)
    tabs = place("tabs", [P, 4, H], F32)
    mrow = place("mrow", [P, SPAN], F32)
    Drow = place("Drow", [1, H], F32)
    half_pi = place("half_pi", [P, 1], F32)
    scale3 = place("scale3", [P, NC, NC], F32)
    inv_scale3 = place("inv_scale3", [P, NC, NC], F32)
    assert cursor[0] <= nc.sbuf_usable_end, cursor[0]
    E1 = place("E1", [P, NC, EW], F32, at=region_m)
    A2 = place("A2", [P, NC, L], F32)
    LA = place("LA", [P, NC, NL, RL], F32)
    W2s = place("W2s", [P, 2, L], F32)
    B3s = place("B3s", [2 * R3, L], F32R)
    A3hh = place("A3hh", [2 * R3, L], F32R)
    A3lo = place("A3lo", [R3, L], F32R)
    assert cursor[0] <= region_carry, (cursor[0], region_carry)
    A3.append(place("A3b", [P, NC, QO], F32, at=region_lowrank))
    m32 = place("m32", [P, 2, QO], F32)
    assert cursor[0] <= after_lowrank
    B3n = place("B3n", [P, NC, 2, R3], F32, at=region_q + 4 * (5 * QCOLS + 2 * 1024))
    B3raw = place("B3raw", [2 * R3, L], F32, at=region_q + 4 * (6 * QCOLS + 2 * 1024))
    A3raw = place("A3raw", [2 * R3, L], F32)
    HH = H // 2
    theta, turns, expo, mag_v, rem_v, sin_v, rem_u, sin_u = (
        place(name, [P, HH, SPAN], F32, **({"at": region_q} if name == "theta" else {}))
        for name in ("theta", "turns", "expo", "mag_v", "rem_v", "sin_v", "rem_u", "sin_u"))
    Ut = place("Ut", [P, H, SPAN], F32)
    Vt = place("Vt", [P, H, SPAN], F32)
    assert cursor[0] <= region_q + 4 * (5 * QCOLS + 2 * 1024)
    Kf = place("Kf", [SPAN, H, SPAN], F32, at=region_q)
    Kh = place("Kh", [SPAN, H, SPAN], F32R)
    Kl = place("Kl", [SPAN, H, SPAN], F32R)
    after_kernels = cursor[0]
    nat = place("nat", [H, 16, N], F32, at=region_carry + 4 * 2 * EW)
    logs = place("logs", [H, 1 + N], F32)
    exps = place("exps", [H, 1 + N], F32)
    c_in = place("c_in", [H, N, 2], F32)
    nat4 = place("nat4", [H, 4, 2 * N], F32)
    ex = place("ex", [P, 6, H + 1], F32)
    ex_bits = place("ex_bits", [P, H + 1], I32)
    A_nat = place("A_nat", [P, L], F32)
    Wr_nat = place("Wr_nat", [E, L], F32)
    BwIn = place("BwIn", [P, NC, RL], F32)
    len_i = place("len_i", [P, B], I32)
    len_f = place("len_f", [P, B], F32)
    ids_i = place("ids_i", [P, 2], I32)
    ids_f = place("ids_f", [P, 2], F32)
    lidx = place("lidx", [P, NC, B], F32)
    zpad = place("zpad", [H, 2, P], F32)
    cbw = place("cbw", [P, 4, K_CODES], F32)
    cbs = place("cbs", [P, 4], F32)
    codesT = place("codesT", [K_CODES, 3, P], F32)
    sel = place("sel", [K_CODES, K_CODES], F32)
    assert cursor[0] <= region_carry + 4 * NC * EW

    X = place("X", [P, L], F32, at=after_kernels)
    Xr = place("Xr", [P, NC, P], F32)
    toep = [place(f"toep{hh}", [P, 2, L], F32R) for hh in range(HB)]
    assert cursor[0] <= nc.sbuf_usable_end
    xT = place("xT", [P, NC, P], F32, at=region_carry)
    xrh = place("xrh", [P, NC, P], F32R)
    xrl = place("xrl", [P, NC, P], F32R)
    x0h = place("x0h", [P, NC, P], F32R)
    x0l = place("x0l", [P, NC, P], F32R)
    O = place("O", [P, L], F32)
    gsm = place("gsm", [P, 8, E], F32)
    gidx = place("gidx", [P, E], U32)
    hg = place("hg", [P, E, R], F32)
    hgTh = place("hgTh", [P, P], F32R)
    hgTl = place("hgTl", [P, P], F32R)
    lowm = place("lowm", [P, NL, RL], F32)
    low3 = place("low3", [P, 3, RL], F32)
    lowTs = place("lowTs", [3 * RL, P], F32R)
    assert cursor[0] <= after_kernels

    with ExitStack() as ctx:
        bank = [ctx.enter_context(nc.psum_tensor(f"bank{n}", [P, BANK], F32)) for n in range(8)]

        def sem(name):
            return ctx.enter_context(nc.semaphore(name))

        ld_kgen, ld_codes, ld_ids, ld_d = sem("ld_kgen"), sem("ld_codes"), sem("ld_ids"), sem("ld_d")
        ld_b3, ld_rank, ld_w1, ld_blang, ld_la = sem("ld_b3"), sem("ld_rank"), sem("ld_w1"), sem("ld_blang"), sem("ld_la")
        ld_w2, ld_w3 = [sem("ld_w2a"), sem("ld_w2b")], [sem(f"ld_w3_tile{t}") for t in range(QT_TILES)]
        kpad_stored = sem("kpad_stored")
        consts_ready, pool_step, bw_ready, e1_ready, a2_ready = (
            sem("consts_ready"), sem("pool_step"), sem("bw_ready"), sem("e1_ready"), sem("a2_ready"))
        dve_step, act_step, stage_full, stage_free = sem("dve_step"), sem("act_step"), sem("stage_full"), sem("stage_free")
        places_ready, sel_ready, early_done = sem("places_ready"), sem("sel_ready"), sem("early_done")
        nat_rem, nat_sin, nat4_ready = sem("nat_rem"), sem("nat_sin"), sem("nat4_ready")
        tab_rem, tab_sin, tab_ready = sem("tab_rem"), sem("tab_sin"), sem("tab_ready")
        kf_ready, kh_ready, kl_ready = sem("kf_ready"), sem("kh_ready"), sem("kl_ready")
        b3_hi, b3_lo = sem("b3_hi"), sem("b3_lo")
        quant_init, quant_done, v_used = sem("quant_init"), sem("quant_done"), sem("v_used")
        qt_full, qt_free, a3_ready = sem("qt_full"), sem("qt_free"), sem("a3_ready")
        m_full, m_taken, m_lo, lowrank_hi, lowrank_lo = sem("m_full"), sem("m_taken"), sem("m_lo"), sem("lowrank_hi"), sem("lowrank_lo")
        passed = {e: sem(f"waits_passed_{e}") for e in ("dve", "pool")}

        def hold(eng, name):
            eng.sem_inc(passed[name], 1)

        def deltas(q):
            return [("delta", q, n) for n in range(2 * QT_TILES)]

        TABLES_AT = [(1, 7), (2, 0), (2, 6), (2, 9)]
        KERNELS_AT = (QUARTERS - 1, 5)
        order = [("b3t", 0), ("b3t", 1), ("codesT",)] + deltas(0) + [("w2t", 0, 0), ("w2t", 0, 1)]
        between = {0: [("codes",)], 1: [("nat4",), ("at", 0), ("at", 1), ("wrt",)], 2: deltas(1), 5: deltas(2), NC - 1: deltas(3)}
        for kt in range(NC):
            if kt + 1 < NC:
                order += [("w2t", kt + 1, 0), ("w2t", kt + 1, 1)]
            order += [("qt", kt)] + between.get(kt, [])
        order += [("a3", 0, n) for n in range(4)] + [("lap", mt) for mt in range(MT)]
        for q in range(QUARTERS):
            for mt in range(MT + 1):
                if (q, mt) == KERNELS_AT:
                    order += [("kern", g) for g in range(4)]
                order += [("m", q, mt)]
                if q + 1 < QUARTERS and mt in (2, 4, 6, 8):
                    order += [("a3", q + 1, mt // 2 - 1)]
        jobs = [j for j in order if j[0] not in ("qt", "m")]
        jobno = {j: n for n, j in enumerate(jobs)}
        mno = {j: n for n, j in enumerate(j for j in order if j[0] == "m")}

        def stage(j):
            return bank[jobno[j] % 2]

        def m_parts(q, mt):
            cols = slice(q * QO, (q + 1) * QO)
            if mt == MT:
                return slice(0, 3 * RL), R2s[:, cols], None
            if mt == NC:
                return slice(0, P), R1h[:, cols], R1l[:, cols]
            return slice(0, P), Mh[:, mt, cols], Ml[:, mt, cols]

        x_loaded, xr_copied, out_stored = sem("x_loaded"), sem("xr_copied"), sem("out_stored")
        toep_loaded = [sem("toep0_loaded"), sem("toep1_loaded")]

        def load_x(i):
            for hh in range(HB):
                nc.sync.dma_start(X[hh * B:(hh + 1) * B, :],
                             bass.AP(x.tensor, (HB * i + hh) * L, [[H * L, B], [1, L]])).then_inc(x_loaded, 16)

        def load_toep(i, hh):
            src = bass.AP(kpad.tensor, (HB * i + hh) * 2 * KP + 1, [[1, P], [KP, 2], [1, L]])
            nc.sync.dma_start(toep[hh][:, :, :].bitcast(F32), src).then_inc(toep_loaded[hh], 16)

        def reverse(i):
            nc.gpsimd.wait_ge(x_loaded, 32 * i + 32)
            hold(nc.gpsimd, "pool")
            nc.gpsimd.tensor_copy(Xr[:, :, :], X[:, :].rearrange("p (c l) -> p c l", c=NC)[:, :, ::-1]).then_inc(xr_copied, 1)

        with nc.Block() as block:

            @block.sync
            def _(sp):
                for n in range(2):
                    sp.dma_start(B3n[:, :, n, :], B3_lora.rearrange("(t p) r -> p t r", p=P)).then_inc(ld_b3, 16)
                    sp.dma_start(A3raw[n * R3:(n + 1) * R3, :], A3_lora).then_inc(ld_b3, 16)
                sp.dma_start(cb[:, :], bass.AP(codebook.tensor, 0, [[0, P], [1, K_CODES]])).then_inc(ld_codes, 16)
                sp.dma_start(scale3[:, :, :], scale_log.rearrange("(t p) g a -> p t (g a)", p=P)).then_inc(ld_codes, 16)
                sp.dma_start(logs[:, 0:1], log_dt.rearrange("(h a) -> h a", a=1)).then_inc(ld_kgen, 16)
                sp.dma_start(logs[:, 1:1 + N], log_A_real).then_inc(ld_kgen, 16)
                sp.dma_start(nat[:, 0, :], A_imag).then_inc(ld_kgen, 16)
                sp.dma_start(c_in[:, :, :], C_ri).then_inc(ld_kgen, 16)
                for ot in range(NC):
                    sp.dma_start(E1[:, ot, 0:L], W1[ot * P:(ot + 1) * P, :]).then_inc(ld_w1, 16)

                def load_w2(ot):
                    sp.dma_start(W2s[:, ot % 2, :], W2[ot * P:(ot + 1) * P, :]).then_inc(ld_w2[ot % 2], 16)

                def load_w3(q, t):
                    sp.dma_start(vq[:, t, :], W3[q * QO + t * P:q * QO + (t + 1) * P, :]).then_inc(ld_w3[t], 16)

                load_w2(0)
                load_w2(1)
                for it in range(NC):
                    sp.dma_start(E1[:, it, L:EW].rearrange("p (e r) -> p e r", e=E),
                                 B_lang[:, it * P:(it + 1) * P, :].rearrange("e o r -> o e r")).then_inc(ld_blang, 16)
                for t in range(QT_TILES):
                    load_w3(0, t)
                sp.dma_start(len_i[:, :], bass.AP(lengths.tensor, 0, [[0, P], [1, B]])).then_inc(ld_ids, 16)
                for hh in range(HB):
                    rows = slice(hh * B, (hh + 1) * B)
                    sp.dma_start(ids_i[rows, 0:1], languages.rearrange("(b a) -> b a", a=1)).then_inc(ld_ids, 16)
                    sp.dma_start(ids_i[rows, 1:2], labels.rearrange("(b a) -> b a", a=1)).then_inc(ld_ids, 16)
                sp.dma_start(A_nat[:, :], A_lang.rearrange("e r d -> (e r) d")).then_inc(ld_rank, 16)
                sp.dma_start(Wr_nat[:, :], Wr).then_inc(ld_rank, 16)
                sp.dma_start(BwIn[:, :, :], B_lab.rearrange("(t p) r -> p t r", p=P)).then_inc(ld_rank, 16)
                sp.wait_ge(consts_ready, 1)
                sp.dma_start(kpad[:, :, 0:P], zpad[:, :, :]).then_inc(kpad_stored, 16)
                sp.dma_start(Drow[:, :], D_skip.rearrange("(a h) -> a h", a=1)).then_inc(ld_d, 16)
                for it in range(NC):
                    sp.dma_start(LA[:, it, :, :], A_lab[:, it * P:(it + 1) * P, :].rearrange("l i r -> i l r")).then_inc(ld_la, 16)

                def next_w3(q):
                    for t in range(QT_TILES):
                        sp.wait_ge(v_used, QT_TILES * (q - 1) + t + 1)
                        load_w3(q, t)

                for ot in range(2, NC):
                    sp.wait_ge(stage_full, jobno[("w2t", ot - 2, 1)] + 1)
                    load_w2(ot)
                    if ot == 5:
                        next_w3(1)
                for q in range(2, QUARTERS):
                    next_w3(q)
                sp.wait_ge(tab_ready, 2)
                load_x(0)
                for part, t, ready in ((0, Kh, kh_ready), (1, Kl, kl_ready)):
                    sp.wait_ge(ready, 1)
                    sp.dma_start(bass.AP(kpad.tensor, part * KP + P, [[SPAN, SPAN], [2 * KP, H], [1, SPAN]]),
                                 t[:, :, :].bitcast(F32)).then_inc(kpad_stored, 16)
                sp.wait_ge(kpad_stored, 48)
                for hh in range(HB):
                    load_toep(0, hh)

            @block.gpsimd
            def _(pool):
                n_step = [0]

                def step(ins):
                    n_step[0] += 1
                    ins.then_inc(pool_step, 1)
                    pool.wait_ge(pool_step, n_step[0])

                step(pool.memset(ident[:, :], 0.0))
                pool.memset(half_pi[:, :], math.pi / 2)
                pool.memset(zpad[:, :, :], 0.0)
                for t, pattern, multiplier in ((mrow[:, :], [[1, SPAN]], 0), (iota[:, :], [[1, K_CODES]], 0),
                                               (lidx[:, :, :], [[P, NC], [0, B]], 1)):
                    pool.iota(t, pattern=pattern, base=0, channel_multiplier=multiplier, allow_small_or_imprecise_dtypes=True)
                pool.affine_select(out=ident[:, :], in_=ident[:, :], compare_op=ALU.not_equal, fill=1.0, base=0,
                                   pattern=[[-1, P]], channel_multiplier=1).then_inc(consts_ready, 1)
                pool.wait_ge(consts_ready, 1)

                def finish_quarter(q):
                    for t in range(QT_TILES):
                        pool.wait_ge(v_used, QT_TILES * q + t + 1)
                        rounded = qq[q][:, t, :].rearrange("p (g k) -> p g k", g=NC)
                        step(pool.tensor_tensor(rounded, rounded, scale3[:, q * QT_TILES + t, :].unsqueeze(2).broadcast_to([P, NC, P]), ALU.mult))
                    pool.tensor_tensor(qq[q][:, :, :], qq[q][:, :, :], dq[q % 2][:, :, :], ALU.add).then_inc(quant_done, 1)

                pool.wait_ge(ld_w1, 16 * NC)
                for it in range(NC):
                    d = E1[:, it, it * P:(it + 1) * P]
                    pool.tensor_tensor(d, d, ident[:, :], ALU.add).then_inc(e1_ready, 1)
                for it in range(NC):
                    pool.wait_ge(stage_free, jobno[("w2t", it, it // 4)] + 1)
                    d = A2[:, it, it * P:(it + 1) * P]
                    pool.tensor_tensor(d, d, ident[:, :], ALU.add).then_inc(a2_ready, 1)
                    if it == 0:
                        pool.wait_ge(ld_blang, 16 * NC)
                        pool.tensor_scalar(E1[:, :, L:EW], E1[:, :, L:EW], 2.0, None, ALU.mult).then_inc(e1_ready, 1)
                    if it == 1:
                        pool.wait_ge(ld_rank, 48)
                        for n in range(3):
                            pool.tensor_scalar(Bw3[:, :, n * RL:(n + 1) * RL], BwIn[:, :, :], 0.5, None, ALU.mult).then_inc(bw_ready, 1)
                    if it == NC - 3:
                        finish_quarter(0)
                finish_quarter(1)
                for j in order:
                    name, *which = j
                    if j == ("lap", MT - 1):
                        pool.wait_ge(lowrank_hi, 3)
                        pool.tensor_tensor(Ml[:, :, C_H:C_LOW], AT[:, :, :], Mh[:, :, C_H:C_LOW].bitcast(F32), ALU.subtract).then_inc(lowrank_lo, 1)
                        pool.tensor_tensor(Ml[:, :, C_LOW:MW], LAp[:, 0:NC, :], Mh[:, :, C_LOW:MW].bitcast(F32), ALU.subtract).then_inc(lowrank_lo, 1)
                        pool.tensor_tensor(BLl[:, :], LAp[:, NC, :], BLh[:, :].bitcast(F32), ALU.subtract).then_inc(lowrank_lo, 1)
                    elif name == "a3" and which[0] == which[1]:
                        q = which[0]
                        pool.wait_ge(stage_free, jobno[j] + 1)
                        for t in range(QT_TILES):
                            d = A3[q % 2][:, q * QT_TILES + t, t * P:(t + 1) * P]
                            pool.tensor_tensor(d, d, ident[:, :], ALU.add).then_inc(a3_ready, 1)
                    elif name == "m":
                        q, mt = which
                        n = mno[j]
                        pool.wait_ge(m_taken, n + 1)
                        rows, hi, lo = m_parts(q, mt)
                        if mt == MT:
                            rows = slice(2 * RL, 3 * RL)
                            lo = hi = hi[2 * RL:3 * RL, :]
                            pool.wait_ge(m_lo, n)
                            pool.wait_ge(a3_ready, QT_TILES * min(q + 2, QUARTERS))
                        pool.tensor_tensor(lo, m32[rows, n % 2, :], hi.bitcast(F32), ALU.subtract).then_inc(m_lo, 1)
                        if mt == MT:
                            pool.wait_ge(m_lo, n + 1)
                        if j == ("m", 0, 4):
                            finish_quarter(2)
                        if j == ("m", QUARTERS - 1, 6):
                            reverse(0)

            @block.tensor
            def _(pe):
                pe.wait_ge(consts_ready, 1)

                def several(j, count, one):
                    if jobno[j] >= 2:
                        pe.wait_ge(stage_free, jobno[j] - 1)
                    for n in range(count):
                        last = one(stage(j), n)
                    last.then_inc(stage_full, 1)

                def b3t(g):
                    if g == 0:
                        pe.wait_ge(ld_b3, 64)
                    several(("b3t", g), 4, lambda ps, n: pe.transpose(
                        ps[0:2 * R3, n * P:(n + 1) * P], B3n[:, 4 * g + n, :, :].rearrange("p n r -> p (n r)"), ident[:, :]))

                def delta(q, n):
                    t, half = n // 2, n % 2
                    if q == 0 and n == 0:
                        pe.wait_ge(b3_lo, 2)
                    o = (q * QT_TILES + t) * P
                    cols = slice(half * BANK, (half + 1) * BANK)
                    factors = ((B3s[:, o:o + P], A3hh[:, cols]), (B3s[0:R3, o:o + P], A3lo[:, cols]))
                    several(("delta", q, n), 2, lambda ps, m: pe.matmul(ps[:, :], *factors[m], start=(m == 0), stop=(m == 1)))

                def w2t(ot, half):
                    if half == 0:
                        pe.wait_ge(ld_w2[ot % 2], 16 * (ot // 2 + 1))
                    several(("w2t", ot, half), 4, lambda ps, n: pe.transpose(
                        ps[:, n * P:(n + 1) * P], W2s[:, ot % 2, (4 * half + n) * P:(4 * half + n + 1) * P], ident[:, :]))

                def codes_t():
                    pe.wait_ge(places_ready, 1)
                    src = (cbw[:, 3, :], tau[:, 0:K_CODES], cb[:, :])
                    several(("codesT",), 3, lambda ps, n: pe.transpose(ps[0:K_CODES, n * P:(n + 1) * P], src[n], ident[:, :]))

                def codes():
                    pe.wait_ge(sel_ready, 1)
                    several(("codes",), 2, lambda ps, n: pe.matmul(ps[:, n * K_CODES:(n + 1) * K_CODES], codesT[:, 1 + n, :], sel[:, :],
                                                                    start=True, stop=True))

                def nat4_t():
                    pe.wait_ge(nat4_ready, 1)
                    several(("nat4",), 4, lambda ps, n: pe.transpose(ps[:, n * H:(n + 1) * H], nat4[:, n, :], ident[0:H, 0:H]))

                def at(g):
                    if g == 0:
                        pe.wait_ge(ld_rank, 48)
                    several(("at", g), 4, lambda ps, n: pe.transpose(
                        ps[:, n * P:(n + 1) * P], A_nat[:, (4 * g + n) * P:(4 * g + n + 1) * P], ident[:, :]))

                def wrt():
                    several(("wrt",), NC, lambda ps, c: pe.transpose(ps[:, c * E:(c + 1) * E], Wr_nat[:, c * P:(c + 1) * P], ident[0:E, 0:E]))

                def qt(kt):
                    if kt == 0:
                        pe.wait_ge(e1_ready, NC)
                    pe.wait_ge(a2_ready, kt + 1)
                    pe.wait_ge(stage_free, jobno[("w2t", kt, 1)] + 1)
                    if kt >= 2:
                        pe.wait_ge(qt_free, kt - 1)
                    s = 2 + 3 * (kt % 2)
                    for n, (a, b) in enumerate(((0, BANK), (BANK, L), (L, EW))):
                        if kt == 0 and a == L:
                            pe.wait_ge(e1_ready, NC + 1)
                        for it in range(NC):
                            last = pe.matmul(bank[s + n][:, 0:b - a], A2[:, it, kt * P:(kt + 1) * P], E1[:, it, a:b],
                                             start=(it == 0), stop=(it == NC - 1))
                    last.then_inc(qt_full, 1)

                def lap(mt):
                    if mt == 0:
                        pe.wait_ge(ld_la, 16 * NC)
                    several(("lap", mt), NC, lambda ps, it: pe.matmul(
                        ps[:, 0:LR], E1[:, it, mt * P:(mt + 1) * P], LA[:, it, :, :].rearrange("p l r -> p (l r)"),
                        start=(it == 0), stop=(it == NC - 1)))

                def a3(q, n):
                    if n == 0:
                        pe.wait_ge(quant_done, q + 1)
                    several(("a3", q, n), 2 * QT_TILES, lambda ps, m: pe.transpose(
                        ps[:, m * P:(m + 1) * P], qq[q][:, m % QT_TILES, (2 * n + m // QT_TILES) * P:(2 * n + m // QT_TILES + 1) * P], ident[:, :]))

                def kern(g):
                    if g == 0:
                        pe.wait_ge(tab_ready, 2)
                    several(("kern", g), 16, lambda ps, n: pe.matmul(ps[0:SPAN, n * SPAN:(n + 1) * SPAN], Ut[:, 16 * g + n, :], Vt[:, 16 * g + n, :],
                                                                      start=True, stop=True))

                def m(q, mt):
                    n = mno[("m", q, mt)]
                    if mt == 0:
                        pe.wait_ge(stage_free, jobno[("a3", q, 3)] + 1)
                        pe.wait_ge(a3_ready, QT_TILES * (q + 1))
                        if q == 0:
                            pe.wait_ge(qt_free, NC)
                            pe.wait_ge(bw_ready, 3)
                    if n >= 6:
                        pe.wait_ge(m_taken, n - 5)
                    rows = 3 * RL if mt == MT else P
                    for kt in range(NC):
                        lhs = Bw3[:, kt, :] if mt == MT else QT[:, kt, mt * P:(mt + 1) * P]
                        last = pe.matmul(bank[2 + n % 6][0:rows, 0:QO], lhs, A3[q % 2][:, kt, :], start=(kt == 0), stop=(kt == NC - 1))
                    last.then_inc(m_full, 1)

                do = dict(b3t=b3t, delta=delta, w2t=w2t, codesT=codes_t, codes=codes, nat4=nat4_t, at=at, wrt=wrt, qt=qt, lap=lap,
                          a3=a3, kern=kern, m=m)
                for name, *which in order:
                    do[name](*which)

            @block.scalar
            def _(act):
                n_step = [0]

                def step(ins):
                    n_step[0] += 1
                    ins.then_inc(act_step, 1)
                    act.wait_ge(act_step, n_step[0])

                def take(j, out, in_, scale=1.0):
                    act.wait_ge(stage_full, jobno[j] + 1)
                    act.activation(out, in_, ACT.Copy, scale=scale).then_inc(stage_free, 1)

                def table(k):
                    act.wait_ge(tab_rem, k + 1)
                    rem, sine = ((rem_v, sin_v), (rem_u, sin_u))[k % 2]
                    step(act.activation(sine[:, :, :], rem[:, :, :], ACT.Sin, scale=0.5))
                    step(act.activation(rem[:, :, :], rem[:, :, :], ACT.Abs))
                    act.activation(rem[:, :, :], rem[:, :, :], ACT.Sin, bias=half_pi[:, 0:1], scale=-0.5)
                    if k % 2 == 0:
                        act.activation(mag_v[:, :, :], expo[:, :, :], ACT.Exp).then_inc(tab_sin, 1)
                    else:
                        act.activation(expo[:, :, :], expo[:, :, :], ACT.Exp, scale=float(SPAN)).then_inc(tab_sin, 1)

                def nat_sine():
                    act.wait_ge(nat_rem, 1)
                    act.wait_ge(consts_ready, 1)
                    step(act.activation(nat[:, 4, :], nat[:, 3, :], ACT.Sin, scale=0.5))
                    step(act.activation(nat[:, 5, :], nat[:, 3, :], ACT.Abs))
                    act.activation(nat[:, 6, :], nat[:, 5, :], ACT.Sin, bias=half_pi[0:H, 0:1], scale=-0.5).then_inc(nat_sin, 1)

                def init_quarter(q):
                    act.activation(qq[q][:, :, :].rearrange("p t k -> p (t k)"), cb[:, 0:1].to_broadcast([P, QCOLS]), ACT.Copy).then_inc(quant_init, 1)

                for j in order:
                    name, *which = j
                    if name == "b3t":
                        take(j, B3raw[:, which[0] * BANK:(which[0] + 1) * BANK], stage(j)[0:2 * R3, :], scale=0.5)
                        if which[0] == 1:
                            act.wait_ge(stage_free, jobno[j] + 1)
                            act.activation(B3s[:, :], B3raw[:, :], ACT.Copy).then_inc(b3_hi, 1)
                            act.wait_ge(ld_b3, 64)
                            act.activation(A3hh[:, :], A3raw[:, :], ACT.Copy).then_inc(b3_hi, 1)
                    elif name == "delta":
                        q, n = which
                        if n == 0 and q >= 2:
                            act.wait_ge(quant_done, q - 1)
                        take(j, dq[q % 2][:, n // 2, n % 2 * BANK:(n % 2 + 1) * BANK], stage(j)[:, :])
                    elif name == "w2t":
                        ot, half = which
                        take(j, A2[:, 4 * half:4 * half + 4, ot * P:(ot + 1) * P], stage(j)[:, :].rearrange("p (t k) -> p t k", t=4))
                        if j == ("w2t", 1, 1):
                            nat_sine()
                    elif name == "codesT":
                        take(j, codesT[:, :, :], stage(j)[0:K_CODES, 0:3 * P].rearrange("p (n k) -> p n k", n=3))
                        init_quarter(0)
                    elif name == "codes":
                        take(j, steps[:, :, :], stage(j)[:, 0:2 * K_CODES].rearrange("p (n k) -> p n k", n=2))
                    elif name == "nat4":
                        take(j, tabs[:, :, :], stage(j)[:, 0:4 * H].rearrange("p (q h) -> p q h", q=4))
                    elif name == "at":
                        g = which[0]
                        take(j, AT[:, 4 * g:4 * g + 4, 0:ER], stage(j)[:, :].rearrange("p (c e) -> p c e", c=4))
                    elif name == "wrt":
                        take(j, AT[:, :, ER:ER + E], stage(j)[:, 0:NC * E].rearrange("p (c e) -> p c e", c=NC))
                    elif name == "qt":
                        kt = which[0]
                        if kt == 2:
                            act.wait_ge(bw_ready, 3)
                            act.wait_ge(kpad_stored, 16)
                            act.wait_ge(early_done, 1)
                        s = 2 + 3 * (kt % 2)
                        act.wait_ge(qt_full, kt + 1)
                        act.activation(QT[:, kt, 0:BANK], bank[s][:, :], ACT.Copy)
                        act.activation(QT[:, kt, BANK:L], bank[s + 1][:, :], ACT.Copy)
                        act.activation(QT[:, kt, L:EW], bank[s + 2][:, 0:ER], ACT.Copy).then_inc(qt_free, 1)
                        if 0 < kt < QUARTERS:
                            init_quarter(kt)
                    elif name == "lap":
                        mt = which[0]
                        take(j, LAp[:, mt, :], stage(j)[:, 0:LR])
                        if mt == MT - 1:
                            act.wait_ge(stage_free, jobno[j] + 1)
                            act.activation(Mh[:, :, C_H:C_LOW], AT[:, :, :], ACT.Copy).then_inc(lowrank_hi, 1)
                            act.activation(Mh[:, :, C_LOW:MW], LAp[:, 0:NC, :], ACT.Copy).then_inc(lowrank_hi, 1)
                            act.activation(BLh[:, :], LAp[:, NC, :], ACT.Copy).then_inc(lowrank_hi, 1)
                    elif name == "a3":
                        q, n = which
                        take(j, A3[q % 2][:, 2 * n:2 * n + 2, :], stage(j)[:, :].rearrange("p (t o) -> p t o", t=2))
                    elif name == "kern":
                        g = which[0]
                        take(j, Kf[:, 16 * g:16 * g + 16, :], stage(j)[0:SPAN, :].rearrange("a (h b) -> a h b", h=16))
                        if g == 3:
                            act.wait_ge(kf_ready, 1)
                            act.activation(Kh[:, :, :], Kf[:, :, :], ACT.Copy).then_inc(kh_ready, 1)
                    else:
                        q, mt = which
                        n = mno[j]
                        rows, hi, _ = m_parts(q, mt)
                        act.wait_ge(m_full, n + 1)
                        act.activation(hi, bank[2 + n % 6][rows, 0:QO], ACT.Copy)
                        if n == 0:
                            act.wait_ge(lowrank_lo, 3)
                        if n >= 2:
                            act.wait_ge(m_lo, n - 1)
                        act.activation(m32[rows, n % 2, :], bank[2 + n % 6][rows, 0:QO], ACT.Copy).then_inc(m_taken, 1)
                        if (q, mt) in TABLES_AT:
                            table(TABLES_AT.index((q, mt)))

            @block.vector
            def _(dve):
                n_step = [0]

                def step(ins):
                    n_step[0] += 1
                    ins.then_inc(dve_step, 1)
                    dve.wait_ge(dve_step, n_step[0])

                def exp_to(dst, src, rows, w):
                    t = [ex[0:rows, n, 0:w] for n in range(6)]
                    bits = ex_bits[0:rows, 0:w]
                    step(dve.tensor_scalar(t[0], src, -87.0, 88.0, ALU.max, ALU.min))
                    step(dve.tensor_scalar(t[1], t[0], 1.0 / math.log(2.0), MAGIC, ALU.mult, ALU.add))
                    step(dve.tensor_scalar(t[2], t[1], MAGIC, None, ALU.subtract))
                    step(dve.scalar_tensor_tensor(t[3], t[2], -LN2_HI, t[0], ALU.mult, ALU.add))
                    step(dve.scalar_tensor_tensor(t[4], t[2], -LN2_LO, t[3], ALU.mult, ALU.add))
                    step(dve.tensor_scalar(t[5], t[4], 1.0 / math.factorial(7), None, ALU.mult))
                    for n in range(6, 0, -1):
                        step(dve.scalar_tensor_tensor(t[5], t[5], 1.0 / math.factorial(n), t[4], ALU.add, ALU.mult))
                    step(dve.tensor_scalar(t[5], t[5], 1.0, None, ALU.add))
                    step(dve.tensor_scalar(bits, t[2], 127.0, float(1 << 23), ALU.add, ALU.mult))
                    step(dve.tensor_tensor(dst, t[5], bits.bitcast(F32), ALU.mult))

                def reduce_angle(dst, ang, tmp):
                    step(dve.tensor_scalar(tmp, ang, 1.0 / (2 * math.pi), MAGIC, ALU.mult, ALU.add))
                    step(dve.tensor_scalar(tmp, tmp, MAGIC, None, ALU.subtract))
                    step(dve.scalar_tensor_tensor(dst, tmp, -TWO_PI[0], ang, ALU.mult, ALU.add))
                    step(dve.scalar_tensor_tensor(dst, tmp, -TWO_PI[1], dst, ALU.mult, ALU.add))
                    return dve.scalar_tensor_tensor(dst, tmp, -TWO_PI[2], dst, ALU.mult, ALU.add)

                dve.wait_ge(ld_codes, 32)
                w0, w1, w2, places = (cbw[:, k, :] for k in range(4))
                step(dve.scalar_tensor_tensor(w0, cb[:, :], -1.0, cb[:, :], ALU.mult, ALU.max))
                step(dve.reduce_max(cbs[:, 1:2], w0, AX_X))
                step(dve.tensor_scalar(cbs[:, 0:1], cbs[:, 1:2], 1e-8, None, ALU.max))
                step(dve.reciprocal(cbs[:, 1:2], cbs[:, 0:1]))
                step(dve.tensor_scalar(cb[:, :], cb[:, :], cbs[:, 1:2], None, ALU.mult))
                step(dve.tensor_tensor(tau[:, 1:K_CODES], cb[:, 0:K_CODES - 1], cb[:, 1:K_CODES], ALU.add))
                step(dve.tensor_scalar(tau[:, 1:K_CODES], tau[:, 1:K_CODES], 0.5, None, ALU.mult))
                step(dve.memset(tau[:, 0:1], -BIG))
                step(dve.memset(tau[:, K_CODES:K_CODES + 1], BIG))
                s = K_CODES // 2
                while s >= 1:
                    mid, below, above = (tau[:, a:a + K_CODES - 2 * s + 1:2 * s] for a in (s, 0, 2 * s))
                    step(dve.tensor_tensor(mid, mid, below, ALU.max))
                    step(dve.tensor_tensor(mid, mid, above, ALU.min))
                    s //= 2
                step(dve.tensor_tensor(w0, tau[:, 1:K_CODES + 1], tau[:, 0:K_CODES], ALU.is_gt))
                step(dve.memset(w0[:, 0:1], 0.0))
                a, b = w0, w1
                s = 1
                while s < K_CODES:
                    step(dve.tensor_copy(b[:, 0:s], a[:, 0:s]))
                    step(dve.tensor_tensor(b[:, s:], a[:, s:], a[:, 0:K_CODES - s], ALU.add))
                    a, b = b, (w2 if b is w1 else w1)
                    s *= 2
                step(dve.tensor_tensor(places, a, w0, ALU.mult))
                step(dve.tensor_copy(n_steps[:, :], a[0:1, K_CODES - 1:K_CODES]))
                dve.tensor_scalar(places, places, 1.0, None, ALU.subtract).then_inc(places_ready, 1)
                for n, (lo_part, raw, hi_part) in enumerate(((B3s[R3:2 * R3, :], B3raw[R3:2 * R3, :], B3s[R3:2 * R3, :]),
                                                             (A3lo[:, :], A3raw[0:R3, :], A3hh[0:R3, :]))):
                    dve.wait_ge(b3_hi, n + 1)
                    dve.tensor_tensor(lo_part, raw, hi_part.bitcast(F32), ALU.subtract).then_inc(b3_lo, 1)
                flat = scale3[:, :, :].rearrange("p t g -> p (t g)")
                exp_to(flat, flat, P, NC * NC)
                step(dve.reciprocal(inv_scale3[:, :, :], scale3[:, :, :]))

                dve.wait_ge(ld_kgen, 64)
                exp_to(exps[:, :], logs[:, :], H, 1 + N)
                dt, eA, Aim = exps[:, 0:1], exps[:, 1:1 + N], nat[:, 0, :]
                step(dve.tensor_scalar(nat[:, 1, :], eA, dt, -1.0, ALU.mult, ALU.mult))
                step(dve.tensor_scalar(nat[:, 2, :], Aim, dt, None, ALU.mult))
                dtA_re, dtA_im = nat[:, 1, :], nat[:, 2, :]
                reduce_angle(nat[:, 3, :], dtA_im, nat[:, 7, :]).then_inc(nat_rem, 1)
                exp_to(nat[:, 8, :], dtA_re, H, N)
                dve.wait_ge(stage_free, jobno[("codesT",)] + 1)
                dve.wait_ge(consts_ready, 1)
                dve.tensor_scalar(sel[:, :], iota[0:K_CODES, :], codesT[:, 0, 0:1], None, ALU.is_equal).then_inc(sel_ready, 1)
                dve.wait_ge(nat_sin, 1)
                sh, ch, mag = nat[:, 4, :], nat[:, 6, :], nat[:, 8, :]
                step(dve.scalar_tensor_tensor(nat[:, 9, :], sh, -2.0, sh, ALU.mult, ALU.mult))
                step(dve.scalar_tensor_tensor(nat[:, 9, :], nat[:, 9, :], 1.0, mag, ALU.add, ALU.mult))
                step(dve.tensor_scalar(nat[:, 9, :], nat[:, 9, :], 1.0, None, ALU.subtract))
                step(dve.scalar_tensor_tensor(nat[:, 10, :], sh, 2.0, ch, ALU.mult, ALU.mult))
                step(dve.tensor_tensor(nat[:, 10, :], nat[:, 10, :], mag, ALU.mult))
                Er, Ei, Cr, Ci = nat[:, 9, :], nat[:, 10, :], c_in[:, :, 0], c_in[:, :, 1]
                num_r, num_i, t0, t1, t2 = (nat[:, k, :] for k in (11, 12, 13, 14, 15))
                step(dve.tensor_tensor(t0, Cr, Er, ALU.mult))
                step(dve.tensor_tensor(t1, Ci, Ei, ALU.mult))
                step(dve.tensor_tensor(num_r, t0, t1, ALU.subtract))
                step(dve.tensor_tensor(t0, Cr, Ei, ALU.mult))
                step(dve.tensor_tensor(t1, Ci, Er, ALU.mult))
                step(dve.tensor_tensor(num_i, t0, t1, ALU.add))
                step(dve.tensor_tensor(t0, eA, eA, ALU.mult))
                step(dve.tensor_tensor(t1, Aim, Aim, ALU.mult))
                step(dve.tensor_tensor(t0, t0, t1, ALU.add))
                step(dve.reciprocal(t2, t0))
                step(dve.tensor_tensor(t0, num_i, Aim, ALU.mult))
                step(dve.tensor_tensor(t1, num_r, eA, ALU.mult))
                step(dve.tensor_tensor(t0, t0, t1, ALU.subtract))
                step(dve.scalar_tensor_tensor(nat4[:, 2, 0:N], t0, 2.0, t2, ALU.mult, ALU.mult))
                step(dve.scalar_tensor_tensor(nat4[:, 2, N:2 * N], t0, -2.0, t2, ALU.mult, ALU.mult))
                step(dve.tensor_tensor(t0, num_r, Aim, ALU.mult))
                step(dve.tensor_tensor(t1, num_i, eA, ALU.mult))
                step(dve.tensor_tensor(t0, t0, t1, ALU.add))
                for s in range(2):
                    cols = slice(s * N, (s + 1) * N)
                    step(dve.scalar_tensor_tensor(nat4[:, 3, cols], t0, 2.0, t2, ALU.mult, ALU.mult))
                    step(dve.tensor_copy(nat4[:, 0, cols], dtA_re))
                    last = dve.tensor_copy(nat4[:, 1, cols], dtA_im)
                    if s == 0:
                        step(last)
                last.then_inc(nat4_ready, 1)

                dve.wait_ge(ld_ids, 80)
                step(dve.tensor_copy(len_f[:, :], len_i[:, :]))
                step(dve.tensor_tensor(mask[:, :, :], lidx[:, :, :], len_f[:, :].unsqueeze(1).broadcast_to([P, NC, B]), ALU.is_lt))
                step(dve.tensor_copy(ids_f[:, :], ids_i[:, :]))
                step(dve.tensor_scalar(langbias[:, :], iota[:, 0:E], ids_f[:, 0:1], 5.0, ALU.is_equal, ALU.mult))
                dve.tensor_scalar(labsel[:, :], iota[:, 0:NL], ids_f[:, 1:2], None, ALU.is_equal).then_inc(early_done, 1)

                dve.wait_ge(stage_free, jobno[("codes",)] + 1)
                kept_tau, kept_code = steps[:, 0, :], steps[:, 1, :]
                held = step_t[:, 0, 0:K_CODES]
                step(dve.tensor_copy(held[:, 0:1], cb[:, 0:1]))
                step(dve.tensor_copy(held[:, 1:K_CODES], kept_code[:, 0:K_CODES - 1]))
                step(dve.tensor_tensor(kept_code, kept_code, held, ALU.subtract))
                rise = kept_code

                n_kept = dve.value_load(n_steps[0:1, 0:1], min_val=0, max_val=K_CODES - 1)
                CH = step_t.shape[2]
                n_ch = QCOLS // CH
                BITS = K_CODES.bit_length() - 1
                assert K_CODES == 1 << BITS

                def rise_from(k, at, vf, qf, first):
                    k = nc.s_assert_within(k, 0, K_CODES - 1, skip_runtime_bounds_check_because="k is below n_kept")
                    assert n_ch == 2
                    for c in range(n_ch):
                        if not first:
                            dve.wait_ge(dve_step, at - 1 + c)
                        dve.tensor_scalar(step_t[:, c, :], vf[:, c * CH:(c + 1) * CH], kept_tau[:, bass.ds(k, 1)], rise[:, bass.ds(k, 1)],
                                          ALU.is_gt, ALU.mult).then_inc(dve_step, 1)
                    for c in range(n_ch):
                        cols = slice(c * CH, (c + 1) * CH)
                        dve.wait_ge(dve_step, at + c + 1)
                        dve.tensor_tensor(qf[:, cols], qf[:, cols], step_t[:, c, :], ALU.add).then_inc(dve_step, 1)

                per = 2 * n_ch
                groups = QT_TILES * NC
                for q in range(QUARTERS):
                    tiles = slice(q * QT_TILES, (q + 1) * QT_TILES)
                    vf, df, qf = (t[:, :, :].rearrange("p t k -> p (t k)") for t in (vq, dq[q % 2], qq[q]))
                    vg, qg = (t[:, :, :].rearrange("p t (g k) -> p (t g) k", g=NC) for t in (vq, qq[q]))
                    inv_g, scale_g = (t[:, tiles, :].rearrange("p t g -> p (t g)").unsqueeze(2).broadcast_to([P, groups, P])
                                      for t in (inv_scale3, scale3))
                    dve.wait_ge(stage_free, jobno[("delta", q, 2 * QT_TILES - 1)] + 1)
                    for t in range(QT_TILES):
                        dve.wait_ge(ld_w3[t], 16 * (q + 1))
                        step(dve.tensor_tensor(vq[:, t, :], vq[:, t, :], dq[q % 2][:, t, :], ALU.add))
                    step(dve.tensor_tensor(vg, vg, inv_g, ALU.mult))
                    dve.wait_ge(quant_init, q + 1)
                    base = n_step[0]
                    done = base
                    for bit in reversed(range(BITS)):
                        worth = 1 << bit
                        with dve.If((n_kept & worth) > 0):
                            first = (n_kept >> (bit + 1)) << (bit + 1)
                            if worth == 1:
                                rise_from(first, done, vf, qf, True)
                                dve.wait_ge(dve_step, done + per)
                            else:
                                with dve.Fori(0, worth // 2) as pair:
                                    for u in range(2):
                                        rise_from(first + 2 * pair + u, done + (2 * pair + u) * per, vf, qf, u == 0)
                                    dve.wait_ge(dve_step, done + (2 * pair + 2) * per)
                            hold(dve, "dve")
                        with dve.Else():
                            dve.sem_inc(dve_step, per * worth)
                        done += per * worth
                    n_step[0] = base + per * (K_CODES - 1)
                    for t in range(QT_TILES):
                        step(dve.tensor_tensor(qq[q][:, t, :], qq[q][:, t, :], vq[:, t, :], ALU.subtract))
                        dve.tensor_tensor(qq[q][:, t, :], qq[q][:, t, :], vq[:, t, :], ALU.add).then_inc(v_used, 1)
                    if q == QUARTERS - 1:
                        dve.wait_ge(v_used, QT_TILES * QUARTERS)
                        step(dve.tensor_tensor(qg, qg, scale_g, ALU.mult))
                        dve.wait_ge(quant_done, QUARTERS - 1)
                        dve.tensor_tensor(qf, qf, df, ALU.add).then_inc(quant_done, 1)

                dve.wait_ge(quant_done, QUARTERS)
                dve.wait_ge(stage_full, jobno[("a3", 1, 3)] + 1)
                tb = [P, HH, SPAN]
                lo, hi = slice(0, N), slice(N, 2 * N)
                for half in range(2):
                    rows = slice(half * HH, (half + 1) * HH)
                    q = [tabs[:, k, rows].unsqueeze(2).broadcast_to(tb) for k in range(4)]
                    m = mrow[:, :].unsqueeze(1).broadcast_to(tb)
                    step(dve.tensor_tensor(theta[:, :, :], q[1], m, ALU.mult))
                    step(dve.tensor_tensor(expo[:, :, :], q[0], m, ALU.mult))
                    reduce_angle(rem_v[:, :, :], theta[:, :, :], turns[:, :, :]).then_inc(tab_rem, 1)
                    dve.wait_ge(tab_rem, 2 * half + 1)
                    step(dve.tensor_scalar(theta[:, :, :], theta[:, :, :], float(SPAN), None, ALU.mult))
                    reduce_angle(rem_u[:, :, :], theta[:, :, :], turns[:, :, :]).then_inc(tab_rem, 1)
                    dve.wait_ge(tab_rem, 2 * half + 2)
                    dve.wait_ge(tab_sin, 2 * half + 1)
                    step(dve.scalar_tensor_tensor(turns[lo, :, :], sin_v[lo, :, :], -2.0, sin_v[lo, :, :], ALU.mult, ALU.mult))
                    step(dve.tensor_scalar(turns[lo, :, :], turns[lo, :, :], 1.0, None, ALU.add))
                    step(dve.scalar_tensor_tensor(turns[hi, :, :], sin_v[hi, :, :], 2.0, rem_v[hi, :, :], ALU.mult, ALU.mult))
                    step(dve.tensor_tensor(Vt[:, rows, :], turns[:, :, :], mag_v[:, :, :], ALU.mult))
                    dve.wait_ge(tab_sin, 2 * half + 2)
                    sine, cosine = rem_u, sin_u
                    step(dve.scalar_tensor_tensor(sine[:, :, :], sin_u[:, :, :], 2.0, rem_u[:, :, :], ALU.mult, ALU.mult))
                    step(dve.scalar_tensor_tensor(cosine[:, :, :], sin_u[:, :, :], -2.0, sin_u[:, :, :], ALU.mult, ALU.mult))
                    step(dve.tensor_scalar(cosine[:, :, :], cosine[:, :, :], 1.0, None, ALU.add))
                    for part, first, second in ((lo, cosine, sine), (hi, sine, cosine)):
                        step(dve.tensor_tensor(turns[part, :, :], first[part, :, :], q[2][part, :, :], ALU.mult))
                        step(dve.tensor_tensor(theta[part, :, :], second[part, :, :], q[3][part, :, :], ALU.mult))
                    step(dve.tensor_tensor(turns[:, :, :], turns[:, :, :], theta[:, :, :], ALU.add))
                    dve.tensor_tensor(Ut[:, rows, :], turns[:, :, :], expo[:, :, :], ALU.mult).then_inc(tab_ready, 1)
                    dve.wait_ge(tab_ready, half + 1)

                dve.wait_ge(stage_free, jobno[("kern", 3)] + 1)
                dve.wait_ge(ld_d, 16)
                dve.scalar_tensor_tensor(Kf[0:1, :, 0], Kf[0:1, :, 0], 1.0, Drow[:, :], ALU.add, ALU.add).then_inc(kf_ready, 1)
                dve.wait_ge(kh_ready, 1)
                dve.tensor_tensor(Kl[:, :, :], Kf[:, :, :], Kh[:, :, :].bitcast(F32), ALU.subtract).then_inc(kl_ready, 1)

        xrev_ready, xrh_done, xrl_done = sem("xrev_ready"), sem("xrh_done"), sem("xrl_done")
        xnat_ready, xT_done = sem("xnat_ready"), sem("xT_done")
        conv_done, x0_done, x0h_done, x0l_done = sem("conv_done"), sem("x0_done"), sem("x0h_done"), sem("x0l_done")
        lr_done, gap_done, gexp_done, hg_done = sem("lr_done"), sem("gap_done"), sem("gexp_done"), sem("hg_done")
        hgT_ready, hgTh_done, hgTl_done = sem("hgT_ready"), sem("hgTh_done"), sem("hgTl_done")
        low_done, low3_done, lowT_ready, lowTh_done, lowTl_done = (
            sem("low_done"), sem("low3_done"), sem("lowT_ready"), sem("lowTh_done"), sem("lowTl_done"))
        out_full, out_taken, gate_step, gate_low = sem("out_full"), sem("out_taken"), sem("gate_step"), sem("gate_low")
        psX, psY, psO, psL, psT = bank[0:2], bank[2:4], bank[4:6], bank[6], bank[7]
        LAST = TILES - 1

        with nc.Block() as block:

            @block.sync
            def _(sp):
                def store(i):
                    for hh in range(HB):
                        sp.dma_start(bass.AP(out.tensor, (HB * i + hh) * L, [[H * L, B], [1, L]]),
                                     O[hh * B:(hh + 1) * B, :]).then_inc(out_stored, 16)

                def tile(i, more):
                    if more:
                        sp.wait_ge(xnat_ready, HB * i + 2 * HB)
                        load_x(i + 2)
                        for hh in range(HB):
                            sp.wait_ge(conv_done, HB * i + HB + hh + 1)
                            load_toep(i + 2, hh)
                    sp.wait_ge(out_taken, 2 * i + 3)
                    store(i)

                sp.wait_ge(xnat_ready, HB)
                load_x(1)
                for hh in range(HB):
                    sp.wait_ge(conv_done, hh + 1)
                    load_toep(1, hh)
                with sp.Fori(0, TILES - 2) as i:
                    tile(i, True)
                for i in range(TILES - 2, TILES):
                    tile(i, False)
                sp.wait_ge(out_stored, 32 * TILES)

            @block.gpsimd
            def _(pool):
                with pool.Fori(1, TILES) as i:
                    pool.wait_ge(xrev_ready, HB * i)
                    hold(pool, "pool")
                    reverse(i)

            @block.tensor
            def _(pe):
                def reversed_in(i, first=False):
                    pe.wait_ge(xr_copied, i + 1)
                    if not first:
                        pe.wait_ge(xT_done, HB * i)
                    for c in range(NC):
                        last = pe.transpose(psX[c // 4][:, c % 4 * P:(c % 4 + 1) * P], Xr[:, c, :], ident[:, :])
                        if c % 4 == 3:
                            last.then_inc(xrev_ready, 1)

                def natural_in(i):
                    for g in range(2):
                        pe.wait_ge(xrl_done, 2 * i + g + 1)
                        for c in range(4 * g, 4 * g + 4):
                            last = pe.transpose(psX[g][:, c % 4 * P:(c % 4 + 1) * P], X[:, c * P:(c + 1) * P], ident[:, :])
                        last.then_inc(xnat_ready, 1)

                def conv(i, hh):
                    pe.wait_ge(toep_loaded[hh], 16 * i + 16)
                    for d in range(NC):
                        cols = slice(d * P, (d + 1) * P)
                        for n, (part, xr) in enumerate(((0, xrh), (0, xrl), (1, xrh))):
                            last = pe.matmul(psY[hh][:, d * B:NC * B].rearrange("p (c b) -> p c b", b=B), toep[hh][:, part, cols],
                                             xr[:, 0:NC - d, hh * B:(hh + 1) * B],
                                             start=(d == 0 and n == 0), stop=(d == NC - 1 and n == 2))
                    last.then_inc(conv_done, 1)

                def low_in(i):
                    pe.wait_ge(x0l_done, HB * i + HB)
                    for c in range(NC):
                        for n, (xs, ms) in enumerate(((x0h, Mh), (x0h, Ml), (x0l, Mh))):
                            last = pe.matmul(psL[:, 0:LOWC], xs[:, c, :], ms[:, c, L:MW], start=(c == 0 and n == 0), stop=False,
                                             skip_group_check=True)
                    last.then_inc(lr_done, 1)

                def main(i):
                    pe.wait_ge(out_taken, 2 * i + 1)
                    for c in range(NC):
                        for n, (xs, ms) in enumerate(((x0h, Mh), (x0h, Ml), (x0l, Mh))):
                            for nh in range(2):
                                pe.matmul(psO[nh][:, :], xs[:, c, :], ms[:, c, nh * BANK:(nh + 1) * BANK],
                                          start=(c == 0 and n == 0), stop=False)

                def gated_transpose(i):
                    pe.wait_ge(hg_done, i + 1)
                    pe.transpose(psT[:, 0:P], hg[:, :, :].rearrange("p e r -> p (e r)"), ident[:, :]).then_inc(hgT_ready, 1)

                def low_gated(i):
                    pe.wait_ge(hgTl_done, i + 1)
                    for n, (a, b) in enumerate(((hgTh, BLh), (hgTh, BLl), (hgTl, BLh))):
                        last = pe.matmul(psL[:, ER + E:LOWC], a[:, :], b[:, :], start=False, stop=(n == 2), skip_group_check=True)
                    last.then_inc(low_done, 1)

                def low_transpose(i):
                    pe.wait_ge(low3_done, i + 1)
                    pe.transpose(psT[0:3 * RL, P:2 * P], low3[:, :, :].rearrange("p n r -> p (n r)"), ident[:, :]).then_inc(lowT_ready, 1)

                def gated_out(i):
                    for a, b in ((hgTh, R1h), (hgTh, R1l), (hgTl, R1h)):
                        for nh in range(2):
                            pe.matmul(psO[nh][:, :], a[:, :], b[:, nh * BANK:(nh + 1) * BANK], start=False, stop=False)

                def low_out(i):
                    pe.wait_ge(lowTl_done, i + 1)
                    for nh in range(2):
                        last = pe.matmul(psO[nh][:, :], lowTs[:, :], R2s[:, nh * BANK:(nh + 1) * BANK], start=False, stop=True)
                    last.then_inc(out_full, 1)

                def tile(i, more):
                    if more:
                        reversed_in(i + 1)
                    low_in(i)
                    if more:
                        natural_in(i + 1)
                    main(i)
                    gated_transpose(i)
                    if more:
                        conv(i + 1, 0)
                    low_gated(i)
                    if more:
                        conv(i + 1, 1)
                    low_transpose(i)
                    gated_out(i)
                    low_out(i)

                reversed_in(0, first=True)
                natural_in(0)
                conv(0, 0)
                conv(0, 1)
                with pe.Fori(0, LAST) as i:
                    tile(i, True)
                tile(LAST, False)

            @block.scalar
            def _(act):
                def reversed_hi(i):
                    for g in range(2):
                        act.wait_ge(xrev_ready, 2 * i + g + 1)
                        act.activation(xrh[:, 4 * g:4 * g + 4, :].rearrange("p c b -> p (c b)"), psX[g][:, :], ACT.Copy).then_inc(xrh_done, 1)

                def natural(i):
                    for g in range(2):
                        act.wait_ge(xnat_ready, 2 * i + g + 1)
                        act.activation(xT[:, 4 * g:4 * g + 4, :].rearrange("p c b -> p (c b)"), psX[g][:, :], ACT.Copy).then_inc(xT_done, 1)

                def x0_hi(i, hh):
                    act.wait_ge(x0_done, HB * i + hh + 1)
                    cols = slice(hh * B, (hh + 1) * B)
                    act.activation(x0h[:, :, cols], xT[:, :, cols], ACT.Copy).then_inc(x0h_done, 1)

                def gate_exp(i):
                    act.wait_ge(gap_done, i + 1)
                    act.activation(gsm[:, 3, 0:1], gsm[:, 2, 0:1], ACT.Exp).then_inc(gexp_done, 1)

                def gated_hi(i):
                    act.wait_ge(hgT_ready, i + 1)
                    act.activation(hgTh[:, :], psT[:, 0:P], ACT.Copy).then_inc(hgTh_done, 1)

                def low_hi(i):
                    act.wait_ge(lowT_ready, i + 1)
                    act.activation(lowTs[:, :], psT[0:3 * RL, P:2 * P], ACT.Copy).then_inc(lowTh_done, 1)

                def take_out(i, first=False):
                    act.wait_ge(out_full, i + 1)
                    if not first:
                        act.wait_ge(out_stored, 32 * i)
                    for nh in range(2):
                        act.activation(O[:, nh * BANK:(nh + 1) * BANK], psO[nh][:, :], ACT.Copy).then_inc(out_taken, 1)

                def tile(i, more, first=False):
                    if more:
                        reversed_hi(i + 1)
                    gate_exp(i)
                    if more:
                        natural(i + 1)
                    gated_hi(i)
                    if more:
                        x0_hi(i + 1, 0)
                    low_hi(i)
                    if more:
                        x0_hi(i + 1, 1)
                    take_out(i, first)

                act.sem_inc(out_taken, 1)
                reversed_hi(0)
                natural(0)
                x0_hi(0, 0)
                x0_hi(0, 1)
                tile(0, True, first=True)
                with act.Fori(1, LAST) as i:
                    tile(i, True)
                tile(LAST, False)

            @block.vector
            def _(dve):
                def reversed_lo(i):
                    for g in range(2):
                        dve.wait_ge(xrh_done, 2 * i + g + 1)
                        t = [v[:, 4 * g:4 * g + 4, :].rearrange("p c b -> p (c b)") for v in (xrl, xrh)]
                        dve.tensor_tensor(t[0], psX[g][:, :], t[1].bitcast(F32), ALU.subtract).then_inc(xrl_done, 1)

                def select(i, hh):
                    dve.wait_ge(xT_done, 2 * i + 2)
                    dve.wait_ge(conv_done, HB * i + hh + 1)
                    hold(dve, "dve")
                    dve.copy_predicated(xT[:, :, hh * B:(hh + 1) * B], mask[:, :, :],
                                        psY[hh][:, :].rearrange("p (c b) -> p c b", b=B)).then_inc(x0_done, 1)

                def x0_lo(i, hh):
                    dve.wait_ge(x0h_done, HB * i + hh + 1)
                    cols = slice(hh * B, (hh + 1) * B)
                    dve.tensor_tensor(x0l[:, :, cols], xT[:, :, cols], x0h[:, :, cols].bitcast(F32), ALU.subtract).then_inc(x0l_done, 1)

                GATE_STEPS = 10

                def gate(i):
                    done = [0]

                    def step(ins):
                        done[0] += 1
                        ins.then_inc(gate_step, 1)
                        dve.wait_ge(gate_step, GATE_STEPS * i + done[0])

                    logit, top, gap, e, g0, g1, g = (gsm[:, k, :] for k in range(7))
                    w = gsm[:, 7, :]
                    dve.wait_ge(lr_done, i + 1)
                    step(dve.tensor_tensor(logit, psL[:, ER:ER + E], langbias[:, :], ALU.add))
                    hold(dve, "dve")
                    step(dve.max(top, logit))
                    dve.tensor_tensor(gap[:, 0:1], top[:, 1:2], top[:, 0:1], ALU.subtract).then_inc(gap_done, 1)
                    step(dve.max_index(gidx[:, :], top, logit))
                    step(dve.tensor_copy(top[:, 0:2], gidx[:, 0:2]))
                    dve.wait_ge(gexp_done, i + 1)
                    step(dve.tensor_scalar(w[:, 2:3], e[:, 0:1], 1.0, None, ALU.add))
                    step(dve.reciprocal(w[:, 0:1], w[:, 2:3]))
                    step(dve.tensor_tensor(w[:, 1:2], e[:, 0:1], w[:, 0:1], ALU.mult))
                    step(dve.tensor_scalar(g0, iota[:, 0:E], top[:, 0:1], w[:, 0:1], ALU.is_equal, ALU.mult))
                    step(dve.tensor_scalar(g1, iota[:, 0:E], top[:, 1:2], w[:, 1:2], ALU.is_equal, ALU.mult))
                    step(dve.tensor_tensor(g, g0, g1, ALU.add))
                    assert done[0] == GATE_STEPS
                    dve.tensor_tensor(hg[:, :, :], psL[:, 0:ER].rearrange("p (e r) -> p e r", e=E),
                                      g.unsqueeze(2).broadcast_to([P, E, R]), ALU.mult).then_inc(hg_done, 1)

                def gated_lo(i):
                    dve.wait_ge(hgTh_done, i + 1)
                    dve.tensor_tensor(hgTl[:, :], psT[:, 0:P], hgTh[:, :].bitcast(F32), ALU.subtract).then_inc(hgTl_done, 1)

                def low_select(i):
                    dve.wait_ge(low_done, i + 1)
                    dve.tensor_tensor(lowm[:, :, :], psL[:, ER + E:LOWC].rearrange("p (l r) -> p l r", l=NL),
                                      labsel[:, :].unsqueeze(2).broadcast_to([P, NL, RL]), ALU.mult).then_inc(gate_low, 1)
                    dve.wait_ge(gate_low, 2 * i + 1)
                    dve.tensor_reduce(low3[:, 0, :], lowm[:, :, :].rearrange("p l r -> p r l"), AX_X, ALU.add).then_inc(gate_low, 1)
                    dve.wait_ge(gate_low, 2 * i + 2)
                    dve.tensor_copy(low3[:, 1:3, :], low3[:, 0:1, :].broadcast_to([P, 2, RL])).then_inc(low3_done, 1)

                def low_lo(i):
                    dve.wait_ge(lowTh_done, i + 1)
                    part = lowTs[RL:2 * RL, :]
                    dve.tensor_tensor(part, psT[RL:2 * RL, P:2 * P], part.bitcast(F32), ALU.subtract).then_inc(lowTl_done, 1)

                def tile(i, more):
                    if more:
                        reversed_lo(i + 1)
                    gate(i)
                    gated_lo(i)
                    if more:
                        select(i + 1, 0)
                        x0_lo(i + 1, 0)
                    low_select(i)
                    if more:
                        select(i + 1, 1)
                    low_lo(i)
                    if more:
                        x0_lo(i + 1, 1)

                reversed_lo(0)
                for hh in range(HB):
                    select(0, hh)
                    x0_lo(0, hh)
                with dve.Fori(0, LAST) as i:
                    tile(i, True)
                tile(LAST, False)


_INS = ["x", "itok_B_8_3872", "itok_B_0_7", "itok_B_0_2", "condB_codebook", "L0_cond_log_dt", "L0_cond_C",
        "L0_cond_log_A_real", "L0_cond_A_imag", "L0_cond_D", "L1_cond_W", "L1_cond_Wr", "L1_cond_A", "L1_cond_B",
        "L2_cond_W", "L2_cond_lora_A", "L2_cond_lora_B_w", "L3_cond_weight", "L3_cond_scale_log", "L3_cond_lora_A",
        "L3_cond_lora_B"]


def kernel(**inputs):
    import numpy as np
    import concourse.bacc as bacc
    from concourse.bass_utils import run_bass_kernel_spmd

    nc = bacc.Bacc("TRN2", target_bir_lowering=False, num_devices=1, dynamic_dma_scratch_size=1024)
    arrays, args = {}, []
    for name in _INS:
        a = np.ascontiguousarray(inputs[name])
        arrays[f"in_{name}"] = a
        args.append(nc.dram_tensor(f"in_{name}", a.shape, mybir.dt.from_np(a.dtype), kind="ExternalInput").ap())
    shape = inputs["x"].shape
    args.append(nc.dram_tensor("out_x", shape, F32, kind="ExternalOutput").ap())
    resid_stack_kernel(nc, *args)
    r = run_bass_kernel_spmd(nc, [arrays], core_ids=[0])
    return r.results[0]["out_x"]
```
